# Optimizing a Trainium2 kernel written in Bass

```python
import numpy as np
import jax
import jax.numpy as jnp

def _softmax(x, axis=-1):
    return jax.nn.softmax(x, axis=axis)

def _gelu(x):
    return jax.nn.gelu(x, approximate=True)

def _silu(x):
    return jax.nn.silu(x)

def _sigmoid(x):
    return jax.nn.sigmoid(x)

def _layernorm(x, axis=-1, eps=1e-05):
    m = jnp.mean(x, axis=axis, keepdims=True)
    v = jnp.var(x, axis=axis, keepdims=True)
    return (x - m) / jnp.sqrt(v + eps)

def _scatter_add(tgt, idx, src, axis=0):
    return tgt.at[idx].add(src)

def _segment_sum(src, seg, n):
    return jax.ops.segment_sum(src, seg, n)
kernel_name = 'mk_prb_d2_jaxref_r8_79d5a0'

def setup_inputs(seed: int=0):
    np.random.seed(seed)
    _w = jnp.asarray

    def _L0_attn_setup():
        import jax, jax.numpy as jnp
        import numpy as np
        HIDDEN = 512
        NUM_HEADS = 32
        HEAD_DIM = HIDDEN // NUM_HEADS
        B, S = (2, 128)

        def _alibi_slopes(n):
            start = 2.0 ** (-2.0 ** (-(np.log2(n) - 3)))
            return np.array([start ** (i + 1) for i in range(n)], dtype=np.float32)
        key = jax.random.key(seed)
        k1, k2, k3, k4 = jax.random.split(key, 4)
        hidden_states = jax.random.normal(k1, (B, S, HIDDEN), jnp.float32)
        Wq = jax.random.normal(k2, (HIDDEN, HIDDEN), jnp.float32) * 0.02
        Wkv = jax.random.normal(k3, (HIDDEN, 2 * HEAD_DIM), jnp.float32) * 0.02
        Wo = jax.random.normal(k4, (HIDDEN, HIDDEN), jnp.float32) * 0.02
        return {'hidden_states': hidden_states, 'Wq': Wq, 'Wkv': Wkv, 'Wo': Wo}
    _L0_attn_in = _L0_attn_setup()

    def _L0_ffn_setup():
        import jax, jax.numpy as jnp
        import numpy as np
        B_L, B_H = (4, 8)
        LIN_SLOPE, LIN_INTER, EST_T = (1.0, 0.0, 64.0)
        BATCH, SEQ, IN_F, OUT_F = (4, 256, 512, 512)
        MAX_BITS = 8

        def dequant_kbit(qweight, lut, bit):
            O, I32 = (qweight.shape[1], qweight.shape[2])
            shifts = jnp.arange(32, dtype=jnp.int32)
            idx = jnp.zeros((O, I32 * 32), dtype=jnp.int32)
            for p in range(bit):
                bits = (qweight[p][:, :, None] >> shifts & 1).reshape(O, I32 * 32)
                idx = idx | bits << p
            return jnp.take_along_axis(lut, idx, axis=1)
        key = jax.random.key(seed)
        k = jax.random.split(key, 5)
        x = jax.random.normal(k[0], (BATCH, SEQ, IN_F), dtype=jnp.float32)
        qweight = jax.random.randint(k[1], (MAX_BITS, OUT_F, IN_F // 32), 0, 2147483647, dtype=jnp.int32)
        lut4 = jax.random.normal(k[2], (OUT_F, 2 ** B_L), dtype=jnp.float32) * 0.02
        lut8 = jax.random.normal(k[3], (OUT_F, 2 ** B_H), dtype=jnp.float32) * 0.02
        bias = jax.random.normal(k[4], (OUT_F,), dtype=jnp.float32) * 0.01
        return {'x': x, 'qweight': qweight, 'lut4': lut4, 'lut8': lut8, 'bias': bias}
    _L0_ffn_in = _L0_ffn_setup()

    def _L1_attn_setup():
        import jax, jax.numpy as jnp
        import numpy as np
        import math
        B, S, D = (1, 256, 512)
        H, KV, HD = (32, 8, 128)
        GROUPS = H // KV
        SYS_LEN, IMG_LEN = (35, 72)
        ENH, SUP = (1.5, 0.5)
        ROPE_BASE = 10000.0

        def _rope_cos_sin(seq_len, dtype):
            inv_freq = 1.0 / ROPE_BASE ** (jnp.arange(0, HD, 2, dtype=jnp.float32) / HD)
            pos = jnp.arange(seq_len, dtype=jnp.float32)
            freqs = pos[:, None] * inv_freq[None, :]
            emb = jnp.concatenate([freqs, freqs], axis=-1)
            return (jnp.cos(emb).astype(dtype), jnp.sin(emb).astype(dtype))

        def _rotate_half(x):
            x1, x2 = (x[..., :HD // 2], x[..., HD // 2:])
            return jnp.concatenate([-x2, x1], axis=-1)
        key = jax.random.key(seed)
        ks = jax.random.split(key, 5)
        scale = 0.02
        return {'hidden_states': jax.random.normal(ks[0], (B, S, D), dtype=jnp.float32), 'wq': jax.random.normal(ks[1], (H * HD, D), dtype=jnp.float32) * scale, 'wk': jax.random.normal(ks[2], (KV * HD, D), dtype=jnp.float32) * scale, 'wv': jax.random.normal(ks[3], (KV * HD, D), dtype=jnp.float32) * scale, 'wo': jax.random.normal(ks[4], (D, H * HD), dtype=jnp.float32) * scale}
    _L1_attn_in = _L1_attn_setup()

    def _L1_ffn_setup():
        import jax, jax.numpy as jnp
        import numpy as np
        D_MODEL = 512
        D_HIDDEN = 1376
        RANK = 16
        BATCH, SEQ = (2, 256)

        def _matmul_lora(x, w, a, b, scale=1.0):
            out = jnp.einsum('bsd,hd->bsh', x, w)
            out = out + jnp.einsum('bsr,hr->bsh', jnp.einsum('bsd,rd->bsr', x, a), b) * scale
            return out
        key = jax.random.key(seed)
        ks = jax.random.split(key, 10)
        s = 0.02
        return {'x': jax.random.normal(ks[0], (BATCH, SEQ, D_MODEL), jnp.float32), 'gate_w': jax.random.normal(ks[1], (D_HIDDEN, D_MODEL), jnp.float32) * s, 'up_w': jax.random.normal(ks[2], (D_HIDDEN, D_MODEL), jnp.float32) * s, 'down_w': jax.random.normal(ks[3], (D_MODEL, D_HIDDEN), jnp.float32) * s, 'gate_a': jax.random.normal(ks[4], (RANK, D_MODEL), jnp.float32) * s, 'gate_b': jax.random.normal(ks[5], (D_HIDDEN, RANK), jnp.float32) * s, 'up_a': jax.random.normal(ks[6], (RANK, D_MODEL), jnp.float32) * s, 'up_b': jax.random.normal(ks[7], (D_HIDDEN, RANK), jnp.float32) * s, 'down_a': jax.random.normal(ks[8], (RANK, D_HIDDEN), jnp.float32) * s, 'down_b': jax.random.normal(ks[9], (D_MODEL, RANK), jnp.float32) * s}
    _L1_ffn_in = _L1_ffn_setup()
    _d = {'L0_attn_hidden_states': _L0_attn_in['hidden_states'], 'L0_attn_Wq': _L0_attn_in['Wq'], 'L0_attn_Wkv': _L0_attn_in['Wkv'], 'L0_attn_Wo': _L0_attn_in['Wo'], 'L0_ffn_qweight': _L0_ffn_in['qweight'], 'L0_ffn_lut4': _L0_ffn_in['lut4'], 'L0_ffn_lut8': _L0_ffn_in['lut8'], 'L0_ffn_bias': _L0_ffn_in['bias'], 'L1_attn_wq': _L1_attn_in['wq'], 'L1_attn_wk': _L1_attn_in['wk'], 'L1_attn_wv': _L1_attn_in['wv'], 'L1_attn_wo': _L1_attn_in['wo'], 'L1_ffn_gate_w': _L1_ffn_in['gate_w'], 'L1_ffn_up_w': _L1_ffn_in['up_w'], 'L1_ffn_down_w': _L1_ffn_in['down_w'], 'L1_ffn_gate_a': _L1_ffn_in['gate_a'], 'L1_ffn_gate_b': _L1_ffn_in['gate_b'], 'L1_ffn_up_a': _L1_ffn_in['up_a'], 'L1_ffn_up_b': _L1_ffn_in['up_b'], 'L1_ffn_down_a': _L1_ffn_in['down_a'], 'L1_ffn_down_b': _L1_ffn_in['down_b']}
    _x0 = _d['L0_attn_hidden_states']
    _d['L0_attn_hidden_states'] = jax.random.normal(jax.random.fold_in(jax.random.key(seed), 1), (1, 1024, 512), dtype=_x0.dtype)
    del _x0
    return _d

def reference(L0_attn_hidden_states, L0_attn_Wq, L0_attn_Wkv, L0_attn_Wo, L0_ffn_qweight, L0_ffn_lut4, L0_ffn_lut8, L0_ffn_bias, L1_attn_wq, L1_attn_wk, L1_attn_wv, L1_attn_wo, L1_ffn_gate_w, L1_ffn_up_w, L1_ffn_down_w, L1_ffn_gate_a, L1_ffn_gate_b, L1_ffn_up_a, L1_ffn_up_b, L1_ffn_down_a, L1_ffn_down_b):

    def _L0_attn_ref(hidden_states, Wq, Wkv, Wo):
        import jax, jax.numpy as jnp
        import numpy as np
        HIDDEN = 512
        NUM_HEADS = 32
        HEAD_DIM = HIDDEN // NUM_HEADS
        B, S = (2, 128)

        def _alibi_slopes(n):
            start = 2.0 ** (-2.0 ** (-(np.log2(n) - 3)))
            return np.array([start ** (i + 1) for i in range(n)], dtype=np.float32)
        b, s, h = hidden_states.shape
        scale = HEAD_DIM ** (-0.5)
        q = (hidden_states @ Wq).reshape(b, s, NUM_HEADS, HEAD_DIM)
        kv = hidden_states @ Wkv
        k, v = (kv[..., :HEAD_DIM], kv[..., HEAD_DIM:])
        scores = jnp.einsum('bqhd,bkd->bhqk', q, k) * scale
        pos = jnp.arange(s)
        slopes = jnp.asarray(_alibi_slopes(NUM_HEADS))
        bias = slopes[:, None, None] * (pos[None, None, :] - pos[None, :, None]).astype(jnp.float32)
        causal = pos[None, :] <= pos[:, None]
        scores = jnp.where(causal[None, None], scores + bias[None], -jnp.inf)
        attn = jax.nn.softmax(scores, axis=-1)
        out = jnp.einsum('bhqk,bkd->bqhd', attn, v).reshape(b, s, h)
        return out @ Wo

    def _L0_ffn_ref(x, qweight, lut4, lut8, bias):
        import jax, jax.numpy as jnp
        import numpy as np
        B_L, B_H = (4, 8)
        LIN_SLOPE, LIN_INTER, EST_T = (1.0, 0.0, 64.0)
        BATCH, SEQ, IN_F, OUT_F = (4, 256, 512, 512)
        MAX_BITS = 8

        def dequant_kbit(qweight, lut, bit):
            O, I32 = (qweight.shape[1], qweight.shape[2])
            shifts = jnp.arange(32, dtype=jnp.int32)
            idx = jnp.zeros((O, I32 * 32), dtype=jnp.int32)
            for p in range(bit):
                bits = (qweight[p][:, :, None] >> shifts & 1).reshape(O, I32 * 32)
                idx = idx | bits << p
            return jnp.take_along_axis(lut, idx, axis=1)
        e = jnp.linalg.norm(x, axis=-1) * LIN_SLOPE + LIN_INTER
        mask = e > EST_T
        w_l = dequant_kbit(qweight, lut4, B_L)
        w_h = dequant_kbit(qweight, lut8, B_H)
        y_l = jnp.einsum('bsi,oi->bso', x, w_l)
        y_h = jnp.einsum('bsi,oi->bso', x, w_h)
        y = jnp.where(mask[..., None], y_h, y_l) + bias
        return y

    def _L1_attn_ref(hidden_states, wq, wk, wv, wo):
        import jax, jax.numpy as jnp
        import numpy as np
        import math
        B, S, D = (1, 256, 512)
        H, KV, HD = (32, 8, 128)
        GROUPS = H // KV
        SYS_LEN, IMG_LEN = (35, 72)
        ENH, SUP = (1.5, 0.5)
        ROPE_BASE = 10000.0

        def _rope_cos_sin(seq_len, dtype):
            inv_freq = 1.0 / ROPE_BASE ** (jnp.arange(0, HD, 2, dtype=jnp.float32) / HD)
            pos = jnp.arange(seq_len, dtype=jnp.float32)
            freqs = pos[:, None] * inv_freq[None, :]
            emb = jnp.concatenate([freqs, freqs], axis=-1)
            return (jnp.cos(emb).astype(dtype), jnp.sin(emb).astype(dtype))

        def _rotate_half(x):
            x1, x2 = (x[..., :HD // 2], x[..., HD // 2:])
            return jnp.concatenate([-x2, x1], axis=-1)
        bsz, q_len, _ = hidden_states.shape
        dt = hidden_states.dtype
        q = (hidden_states @ wq.T).reshape(bsz, q_len, H, HD).transpose(0, 2, 1, 3)
        k = (hidden_states @ wk.T).reshape(bsz, q_len, KV, HD).transpose(0, 2, 1, 3)
        v = (hidden_states @ wv.T).reshape(bsz, q_len, KV, HD).transpose(0, 2, 1, 3)
        cos, sin = _rope_cos_sin(q_len, dt)
        q = q * cos + _rotate_half(q) * sin
        k = k * cos + _rotate_half(k) * sin
        k = jnp.repeat(k, GROUPS, axis=1)
        v = jnp.repeat(v, GROUPS, axis=1)
        scores = jnp.einsum('bhqd,bhkd->bhqk', q, k) / math.sqrt(HD)
        kpos = jnp.arange(q_len)
        key_scale = jnp.where(kpos < SYS_LEN, SUP, jnp.where(kpos < SYS_LEN + IMG_LEN, ENH, 1.0)).astype(dt)
        qpos = jnp.arange(q_len)
        row_sel = (qpos >= SYS_LEN + IMG_LEN)[:, None]
        scale = jnp.where(row_sel, key_scale[None, :], jnp.ones((), dt))
        scores = scores * scale
        causal = jnp.where(qpos[:, None] >= kpos[None, :], 0.0, jnp.finfo(jnp.float32).min)
        scores = scores + causal.astype(dt)
        probs = jax.nn.softmax(scores.astype(jnp.float32), axis=-1).astype(dt)
        attn = jnp.einsum('bhqk,bhkd->bhqd', probs, v)
        attn = attn.transpose(0, 2, 1, 3).reshape(bsz, q_len, H * HD)
        return attn @ wo.T

    def _L1_ffn_ref(x, gate_w, up_w, down_w, gate_a, gate_b, up_a, up_b, down_a, down_b):
        import jax, jax.numpy as jnp
        import numpy as np
        D_MODEL = 512
        D_HIDDEN = 1376
        RANK = 16
        BATCH, SEQ = (2, 256)

        def _matmul_lora(x, w, a, b, scale=1.0):
            out = jnp.einsum('bsd,hd->bsh', x, w)
            out = out + jnp.einsum('bsr,hr->bsh', jnp.einsum('bsd,rd->bsr', x, a), b) * scale
            return out
        gate = _matmul_lora(x, gate_w, gate_a, gate_b)
        up = _matmul_lora(x, up_w, up_a, up_b)
        hidden = jax.nn.silu(gate) * up
        out = _matmul_lora(hidden, down_w, down_a, down_b)
        return out
    x = L0_attn_hidden_states
    xn = _layernorm(x, axis=-1)
    x = x + _L0_attn_ref(xn, L0_attn_Wq, L0_attn_Wkv, L0_attn_Wo) + _L0_ffn_ref(xn, L0_ffn_qweight, L0_ffn_lut4, L0_ffn_lut8, L0_ffn_bias)
    xn = _layernorm(x, axis=-1)
    x = x + _L1_attn_ref(xn, L1_attn_wq, L1_attn_wk, L1_attn_wv, L1_attn_wo) + _L1_ffn_ref(xn, L1_ffn_gate_w, L1_ffn_up_w, L1_ffn_down_w, L1_ffn_gate_a, L1_ffn_gate_b, L1_ffn_up_a, L1_ffn_up_b, L1_ffn_down_a, L1_ffn_down_b)
    return x

_drawn_inputs = setup_inputs


def setup_inputs(seed=0):
    import zlib

    import numpy as np

    out = dict(_drawn_inputs(seed))
    spreads = {}
    factors = {'L0_attn_Wq': 6.211,
     'L0_ffn_bias': 5.631,
     'L1_attn_wq': 5.818,
     'L1_attn_wk': 5.689,
     'L1_ffn_gate_a': 8.0,
     'L1_ffn_gate_b': 8.0,
     'L1_ffn_up_a': 6.479,
     'L1_ffn_up_b': 6.576,
     'L1_ffn_down_a': 6.708,
     'L1_ffn_down_b': 6.779}
    for name, (base, spread) in spreads.items():
        noise = np.random.default_rng([zlib.crc32(name.encode()), seed]).standard_normal(out[name].shape)
        drawn = base * np.exp(spread * noise) if base else spread * noise
        out[name] = jnp.asarray(drawn.astype(out[name].dtype))
    for name, factor in factors.items():
        out[name] = (out[name] * factor).astype(out[name].dtype)
    return out
```

```python
from contextlib import ExitStack

import concourse.bass as bass
from concourse import mybir

ALU = mybir.AluOpType
ACT = mybir.ActivationFunctionType
AX = mybir.AxisListType
F32 = mybir.dt.float32
F32R = mybir.dt.float32r
BF16 = mybir.dt.bfloat16
I32 = mybir.dt.int32

P = 128
S, D = 1024, 512
ST, DT, BLK = S // P, D // P, 512
NB = S // BLK
EPS = 1e-5

H0, HD0 = 32, 16
HG0 = H0 // 4
K_ROWS, T_ROWS, AUX = 121, 124, 112
QPARTS = (0, 1, 0, 1, 0, 1, 2)
KPARTS = (0, 0, 1, 1, 2, 2, 0)
PT0 = 3
NPLANE, WORDS, CODES_L, CODES_H = 8, 16, 16, 256
EST_T = 64.0

H1, KV1, HD1 = 32, 8, 128
G1 = H1 // KV1
FH, RANK = 1376, 16


class Count:

    def __init__(self, sem):
        self.sem, self.n = sem, 0

    def inc(self, ins, by=1):
        ins.then_inc(self.sem, by)
        self.n += by
        return self.n


def products(pe, out, left, right, first, last):
    (lh, ll), (rh, rl) = left, right
    pe.matmul(out, lh, rh, start=first, stop=False)
    pe.matmul(out, lh, rl, start=False, stop=False)
    return pe.matmul(out, ll, rh, start=False, stop=last)


def build(nc, a):
    ctx = ExitStack()
    with ctx:
        def sb(name, shape, dt):
            return ctx.enter_context(nc.sbuf_tensor(name, shape, dt))

        keep = {
            "resid": sb("resid", [P, ST, D], F32),
            "xth": sb("xth", [P, DT, S], F32R),
            "xtl": sb("xtl", [P, DT, S], F32R),
            "identf": sb("identf", [P, P], F32),
            "identb": sb("identb", [P, P], BF16),
            "masku": sb("masku", [P, P], BF16),
        }
        layer0(nc, a, keep)
        layer1(nc, a, keep)
        gated(nc, a, keep)



class Norm:

    def __init__(self, nc, ctx, keep, name, xn, bank):
        def sb(n, shape, dt=F32):
            return ctx.enter_context(nc.sbuf_tensor(name + n, shape, dt))

        def sem(n):
            return ctx.enter_context(nc.semaphore(name + n))

        self.x, self.xn, self.bank = keep["resid"], xn, bank
        self.xth, self.xtl, self.identf = keep["xth"], keep["xtl"], keep["identf"]
        self.stats, self.mv = sb("stats", [P, ST, 6]), sb("mv", [P, ST, 2])
        self.veps, self.sd, self.r = sb("veps", [P, ST]), sb("sd", [P, ST]), sb("r", [P, ST])
        self.t, self.rstd = sb("t", [P, ST]), self.r
        self.step = sem("norm_step")
        self.veps_ready, self.sd_ready = sem("veps_ready"), sem("sd_ready")
        self.xn_ready, self.turned = sem("xn_ready"), sem("turned")
        self.high_ready, self.low_ready = sem("high_ready"), sem("low_ready")

    def vector(self, nc, dve, arrived):
        step = Count(self.step)
        for st in range(ST):
            arrived(dve, st)
            n = step.inc(nc.vector.bn_stats(self.stats[:, st, :], self.x[:, st, :]))
        for st in range(ST):
            dve.wait_ge(self.step, st + 1)
            n = step.inc(nc.vector.bn_aggr(self.mv[:, st, :], self.stats[:, st, :]))
        dve.wait_ge(self.step, n)
        nc.vector.tensor_scalar(self.veps[:], self.mv[:, :, 1], EPS, None, ALU.add).then_inc(self.veps_ready, 1)
        dve.wait_ge(self.sd_ready, 1)
        n = step.inc(nc.vector.reciprocal(self.r[:], self.sd[:]))
        dve.wait_ge(self.step, n)
        n = step.inc(nc.vector.tensor_tensor(self.t[:], self.r[:], self.r[:], ALU.mult))
        dve.wait_ge(self.step, n)
        n = step.inc(nc.vector.tensor_tensor(self.t[:], self.t[:], self.veps[:], ALU.mult))
        dve.wait_ge(self.step, n)
        n = step.inc(nc.vector.tensor_scalar(self.t[:], self.t[:], -0.5, 1.5, ALU.mult, ALU.add))
        dve.wait_ge(self.step, n)
        n = step.inc(nc.vector.tensor_tensor(self.rstd[:], self.r[:], self.t[:], ALU.mult))
        dve.wait_ge(self.step, n)

        def low(st):
            dve.wait_ge(self.turned, st + 1)
            dve.wait_ge(self.high_ready, st + 1)
            nc.vector.tensor_tensor(self.xtl[:, :, st * P:(st + 1) * P], self.bank(st).rearrange("p (c s) -> p c s", c=DT),
                                    self.xth[:, :, st * P:(st + 1) * P].bitcast(F32), ALU.subtract).then_inc(self.low_ready, 1)

        for st in range(ST):
            nc.vector.tensor_scalar(self.xn[:, st, :], self.x[:, st, :], self.mv[:, st, 0:1], self.rstd[:, st:st + 1],
                                    ALU.subtract, ALU.mult).then_inc(self.xn_ready, 1)
            if st >= 2:
                low(st - 2)
        low(ST - 2)
        low(ST - 1)

    def tensor(self, nc, pe):
        for st in range(ST):
            pe.wait_ge(self.xn_ready, st + 1)
            for c in range(DT):
                last = nc.tensor.transpose(self.bank(st)[:, c * P:(c + 1) * P], self.xn[:, st, c * P:(c + 1) * P], self.identf[:])
            last.then_inc(self.turned, 1)

    def scalar_sqrt(self, nc, act):
        act.wait_ge(self.veps_ready, 1)
        nc.scalar.activation(self.sd[:], self.veps[:], ACT.Sqrt).then_inc(self.sd_ready, 1)

    def scalar_high(self, nc, act):
        for st in range(ST):
            act.wait_ge(self.turned, st + 1)
            nc.scalar.activation(self.xth[:, :, st * P:(st + 1) * P], self.bank(st).rearrange("p (c s) -> p c s", c=DT),
                                 ACT.Copy).then_inc(self.high_ready, 1)



def tri(t):
    return P * t * (t + 1) // 2


def interleave(main, side):
    out, at = [], 0
    for i, step in enumerate(main):
        out.append(step)
        want = (i + 1) * len(side) // len(main)
        out += side[at:want]
        at = want
    return out


def layer0(nc, a, keep):
    ctx = ExitStack()
    with ctx:
        def sb(name, shape, dt=F32):
            return ctx.enter_context(nc.sbuf_tensor(name, shape, dt))

        def sem(name):
            return ctx.enter_context(nc.semaphore(name))

        resid, xth, xtl = keep["resid"], keep["xth"], keep["xtl"]
        identf, identb, masku = keep["identf"], keep["identb"], keep["masku"]
        ps = ctx.enter_context(nc.psum_tensor("ps0", [P, 8, 512], F32))

        def bank(b):
            return ps[:, b % 8, :]

        xn = sb("xn0", [P, ST, D])
        norm = Norm(nc, ctx, keep, "l0_", xn, bank)
        esq, enorm, maskf, masks = sb("esq", [P, ST]), sb("enorm", [P, ST]), sb("maskf", [P, 1]), sb("masks", [P, ST], I32)
        flag = sb("flag", [1, 1], I32)
        credit = sb("credit", [1, 1])
        qstack = sb("qstack", [P, H0, S], BF16)
        kstack = sb("kstack", [P, tri(ST)], BF16)
        wqh, wql = sb("wqh", [P, DT, D], F32R), sb("wql", [P, DT, D], F32R)
        wlh, wll = wqh, wql
        wl = sb("wl", [P, DT, D])
        vaug = sb("vaug", [P, ST, 32])
        negm = sb("negm", [P, 2, H0])
        mrows, mrest = sb("mrows", [H0, 3, P], BF16), sb("mrest", [H0, P])
        acc_sb, rden = sb("acc_sb", [P, P]), sb("rden", [P, 4])
        biasb = sb("biasb", [P, D])
        qw = sb("qw", [P, NPLANE, DT, WORDS], I32)
        lutl = sb("lutl", [P, DT, CODES_L])
        with ExitStack() as early:
            def sbe(name, shape, dt=F32):
                return early.enter_context(nc.sbuf_tensor(name, shape, dt))
            idx, onehot = sbe("idx", [P, DT * D], BF16), sbe("onehot", [P, 2, D])
            bits = sbe("bits", [P, DT * D], I32)
            wkv = sbe("wkv", [P, DT, 2 * HD0])
            wvh, wvl = sbe("wvh", [P, DT, HD0], F32R), sbe("wvl", [P, DT, HD0], F32R)
            wkh, wkl = sbe("wkh", [P, DT, P], F32R), sbe("wkl", [P, DT, P], F32R)
            rest = sbe("rest", [P, 2, BLK])
            parts_sb = [sbe(f"part{i}", [P, 2, S], BF16) for i in range(3)]
        with ExitStack() as late:
            def sbl(name, shape, dt=F32):
                return late.enter_context(nc.sbuf_tensor(name, shape, dt))
            woraw = sbl("woraw", [P, DT, D])
            woh, wol = sbl("woh", [P, DT, D], F32R), sbl("wol", [P, DT, D], F32R)
            atth, attl = sbl("atth", [P, 2, DT, P], F32R), sbl("attl", [P, 2, DT, P], F32R)
            pt = sbl("pt0", [P, PT0, BLK])
        luth = woraw[:, :, 0:CODES_H]
        with ExitStack() as rare:
            rare.enter_context(nc.sbuf_tensor("below_rare", [P, DT, D], F32))
            ridx = rare.enter_context(nc.sbuf_tensor("ridx", [P, DT * D], F32))
            rbits = rare.enter_context(nc.sbuf_tensor("rbits", [P, DT * D], I32))
            rhot = rare.enter_context(nc.sbuf_tensor("rhot", [P, D], F32))
            rsum = rare.enter_context(nc.sbuf_tensor("rsum", [P, D], F32))

        x_in = [sem(f"x_in{i}") for i in range(4)]
        const_in, wkv_in, wq_in, wo_in = sem("const_in"), sem("wkv_in"), sem("wq_in"), sem("wo_in")
        aux_in, qw_in, lut_in, bias_in = sem("aux_in"), sem("qw_in"), sem("lut_in"), sem("bias_in")
        esq_ready, mask_ready = sem("esq_ready"), sem("mask_ready")
        wk_high, wk_low, wq_high, wq_low, wo_high, wo_low = (sem(n) for n in ("wk_high", "wk_low", "wq_high", "wq_low", "wo_high", "wo_low"))
        k_ps, v_ps, q_ps = sem("k_ps"), sem("v_ps"), sem("q_ps")
        kq_part = [sem(f"kq_part{i}") for i in range(3)]
        kq_rest = sem("kq_rest")
        v_ready, v_init = sem("v_ready"), sem("v_init")
        k_stacked = sem("k_stacked")
        q_stacked = [sem(f"q_stacked{i}") for i in range(4)]
        m_filled, m_free = sem("m_filled"), sem("m_free")
        m_turned, m_split, m_rows = sem("m_turned"), sem("m_split"), sem("m_rows")
        t_filled, exp_done, av_done = sem("t_filled"), sem("exp_done"), sem("av_done")
        acc_ready, acc_copied, acc_turned, norm_step, head_done = (
            sem(n) for n in ("acc_ready", "acc_copied", "acc_turned", "norm_step", "head_done"))
        bit_step, idx_step, hot_made, wl_step = (sem(n) for n in ("bit_step", "idx_step", "hot_made", "wl_step"))
        wl_turned, wl_high, wl_low = sem("wl_turned"), sem("wl_high"), sem("wl_low")
        att_turned, att_high, att_low = sem("att_turned"), sem("att_high"), sem("att_low")
        o_ps, y_ps, xb_ready, t_ready, x1_ready = (sem(n) for n in ("o_ps", "y_ps", "xb_ready", "t_ready", "x1_ready"))
        any_turned, any_step, flag_ready = sem("any_turned"), sem("any_step"), sem("flag_ready")
        rare_step, rare_w, rare_turned, rare_split, rare_y, rare_used = (
            sem(n) for n in ("rare_step", "rare_w", "rare_turned", "rare_split", "rare_y", "rare_used"))
        luth_in = sem("luth_in")

        block = ctx.enter_context(nc.Block())

        SCATTER = 16 * 8 * len(QPARTS)
        TB = (4, 5)
        ACCB, TURNB = 6, 7

        def parts_free(eng, n):
            if n // NB == 1:
                eng.wait_ge(k_stacked, 16 * 4 * ST)
            elif n // NB >= 2:
                eng.wait_ge(q_stacked[n // NB - 2], SCATTER)

        def t_base(t):
            return HG0 * t * (t + 1) // 2

        @block.sync
        def _(sp):
            for i in range(4):
                sp.dma_start(resid[:, 2 * i:2 * i + 2, :], a["x"].rearrange("(t p) d -> p t d", p=P)[:, 2 * i:2 * i + 2, :]).then_inc(x_in[i], 16)
            sp.dma_start(identf[:], a["identf"]).then_inc(const_in, 16)
            sp.dma_start(identb[:], a["identb"]).then_inc(const_in, 16)
            sp.dma_start(masku[:], a["masku"]).then_inc(const_in, 16)
            sp.dma_start(wkv[:], a["wkv0"].rearrange("(c p) n -> p c n", p=P)).then_inc(wkv_in, 16)
            sp.dma_start(wl[:], a["wq0"].rearrange("(c p) n -> p c n", p=P)).then_inc(wq_in, 16)
            sp.dma_start(qw[:], a["qw"].rearrange("l (c p) w -> p l c w", p=P)).then_inc(qw_in, 16)
            sp.dma_start(lutl[:], a["lut4"].rearrange("(c p) k -> p c k", p=P)).then_inc(lut_in, 16)
            sp.dma_start(qstack[AUX:K_ROWS, :, :], a["qaux"]).then_inc(aux_in, 16)
            sp.dma_start(kstack[AUX:T_ROWS, :], a["kaux"]).then_inc(aux_in, 16)
            sp.dma_start(biasb[:], a["bias"].partition_broadcast(P)).then_inc(bias_in, 16)
            for i in range(3):
                sp.wait_ge(kq_part[i], NB)
            for part, lo, hi in ((0, 0, 32), (1, 32, 64), (2, 64, 96), (0, 96, 112)):
                for t in range(ST):
                    sp.dma_start(kstack[lo:hi, tri(t):tri(t + 1)], parts_sb[part][lo:hi, 0, 0:(t + 1) * P]).then_inc(k_stacked, 16)
            for qt in range(4):
                for i in range(3):
                    sp.wait_ge(kq_part[i], NB + NB * (qt + 1))
                for r, part in enumerate(QPARTS):
                    for h in range(8):
                        sp.dma_start(qstack[16 * r:16 * r + 16, 8 * qt + h, :],
                                     parts_sb[part][16 * h:16 * h + 16, (qt + 1) % 2, :]).then_inc(q_stacked[qt], 16)
            for t in range(ST):
                if t == 2:
                    for qt in range(4):
                        sp.wait_ge(q_stacked[qt], SCATTER)
                    sp.wait_ge(wl_step, 1 + CODES_L * DT)
                    sp.dma_start(woraw[:], a["wo0"].rearrange("(c p) n -> p c n", p=P)).then_inc(wo_in, 16)
                sp.wait_ge(m_split, 3 * t + 3)
                if t:
                    sp.wait_ge(m_rows, 48 * t)
                for i in range(3):
                    sp.dma_start(qstack[K_ROWS + i:K_ROWS + i + 1, :, t * P:(t + 1) * P], mrows[:, i, :]).then_inc(m_rows, 16)
            sp.wait_ge(wo_low, DT)
            sp.dma_start(luth, a["lut8"].rearrange("(c p) k -> p c k", p=P)).then_inc(luth_in, 16)

        @block.tensor
        def _(pe):
            pe.wait_ge(const_in, 48)
            norm.tensor(nc, pe)

            pe.wait_ge(wk_low, 2)
            for b in range(NB):
                pe.wait_ge(norm.low_ready, ST // NB * (b + 1))
                for c in range(DT):
                    last = products(pe, bank(b), (wkh[:, c, :], wkl[:, c, :]),
                                    (xth[:, c, b * BLK:(b + 1) * BLK], xtl[:, c, b * BLK:(b + 1) * BLK]), c == 0, c == DT - 1)
                last.then_inc(k_ps, 1)
            for st in range(ST):
                for c in range(DT):
                    last = products(pe, ps[:, 2, st * HD0:(st + 1) * HD0],
                                    (xth[:, c, st * P:(st + 1) * P], xtl[:, c, st * P:(st + 1) * P]),
                                    (wvh[:, c, :], wvl[:, c, :]), c == 0, c == DT - 1)
            last.then_inc(v_ps, 1)
            pe.wait_ge(wq_low, DT)
            for n in range(4 * NB):
                qt, b = n // NB, n % NB
                if n == 5:
                    pe.wait_ge(kq_part[0], NB)
                    pe.wait_ge(kq_rest, NB)
                if n == 7:
                    pe.wait_ge(v_ready, 1)
                for c in range(DT):
                    last = products(pe, bank(3 + n), (wqh[:, c, qt * P:(qt + 1) * P], wql[:, c, qt * P:(qt + 1) * P]),
                                    (xth[:, c, b * BLK:(b + 1) * BLK], xtl[:, c, b * BLK:(b + 1) * BLK]), c == 0, c == DT - 1)
                last.then_inc(q_ps, 1)

            pe.wait_ge(mask_ready, 1)
            pe.wait_ge(kq_rest, NB + 4 * NB)
            nc.tensor.transpose(ps[0:1, 4, 0:P], maskf[:], identf[:]).then_inc(any_turned, 1)

            def m_scores(t, h, slot):
                pe.wait_ge(m_free, t * H0 + h + 1)
                width = (t + 1) * P
                for c0 in range(0, width, 512):
                    w = min(512, width - c0)
                    diag = c0 + w == width
                    pe.matmul(ps[:, 2 * slot + c0 // 512, 0:w], qstack[0:K_ROWS, h, t * P:(t + 1) * P],
                              kstack[0:K_ROWS, tri(t) + c0:tri(t) + c0 + w], start=True, stop=not diag)
                d = t * P
                last = pe.matmul(ps[:, 2 * slot + d // 512, d % 512:d % 512 + P], identb[:], masku[:], start=False, stop=True)
                last.then_inc(m_filled, 1)

            def m_turn(t):
                pe.wait_ge(m_free, H0 * (t + 1) + 2)
                if t:
                    pe.wait_ge(m_split, 3 * t)
                if t >= 2:
                    pe.wait_ge(head_done, HG0 * (t - 1))
                nc.tensor.transpose(ps[0:H0, TURNB, 0:P], negm[:, t % 2, :], identf[:]).then_inc(m_turned, 1)

            def t_scores(t, hg, kt):
                if kt < 2:
                    if not (t == 0 and isinstance(hg, int)):
                        pe.wait_ge(exp_done, hg * (t + 1) + t_base(t))
                else:
                    pe.wait_ge(exp_done, hg * (t + 1) + t_base(t) + kt - 1)
                out = ps[:, TB[kt % 2], :].rearrange("p (h q) -> p h q", h=4)
                q = qstack[0:T_ROWS, bass.ds(hg * 4, 4), t * P:(t + 1) * P]
                last = pe.matmul(out, kstack[0:T_ROWS, tri(t) + kt * P:tri(t) + (kt + 1) * P], q, start=True, stop=kt != t)
                if kt == t:
                    last = pe.matmul(out, masku[:],
                                     identb[:].unsqueeze(1).to_broadcast([P, 4, P]), start=False, stop=True)
                last.then_inc(t_filled, 1)

            def values(t, hg, kt):
                if kt == 0 and not (t == 0 and isinstance(hg, int)):
                    pe.wait_ge(acc_copied, hg + HG0 * t)
                pe.wait_ge(exp_done, hg * (t + 1) + t_base(t) + kt + 1)
                for j in range(4):
                    last = pe.matmul(ps[32 * j:32 * j + 32, ACCB, 0:P], vaug[:, kt, :], pt[:, kt % PT0, j * P:(j + 1) * P],
                                     start=kt == 0, stop=kt == t)
                last.then_inc(av_done, 1)

            def unit_group(t, hg):
                first = t == 0 and isinstance(hg, int)
                main = [lambda k=k: t_scores(t, hg, k) for k in range(min(2, t + 1))]
                for k in range(t + 1):
                    main.append(lambda k=k: values(t, hg, k))
                    if k + 2 <= t:
                        main.append(lambda k=k: t_scores(t, hg, k + 2))
                side = [lambda j=j: m_scores(t + 2, hg * 4 + j, j % 2) for j in range(4)] if t + 2 < ST else []
                steps = interleave(main, side)
                if not first:
                    steps.insert(min(3, len(steps) - 1), lambda: turn(t, hg))
                for step in steps:
                    step()

            def turn(t, hg):
                u = hg + (HG0 * t - 1)
                pe.wait_ge(acc_copied, u + 1)
                if not (isinstance(u, int) and u == 0):
                    pe.wait_ge(head_done, u + 1)
                pe.wait_ge(m_split, 3 * min(t + 2, ST))
                nc.tensor.transpose(ps[:, TURNB, 0:P], acc_sb[:], identf[:]).then_inc(acc_turned, 1)

            pe.wait_ge(aux_in, 32)
            pe.wait_ge(k_stacked, 16 * 4 * ST)
            for qt in range(4):
                pe.wait_ge(q_stacked[qt], SCATTER)
            for t in range(2):
                with pe.Fori(0, HG0) as hg:
                    for j in range(4):
                        m_scores(t, hg * 4 + j, j % 2)
                m_turn(t)
            pe.wait_ge(v_ready, 1)
            pe.wait_ge(flag_ready, 1)
            for t in range(ST):
                pe.wait_ge(m_rows, 48 * (t + 1))
                unit_group(t, 0)
                with pe.Fori(1, HG0) as hg:
                    unit_group(t, hg)
                if t + 2 < ST:
                    m_turn(t + 2)
            turn(ST, 0)

            pe.wait_ge(wl_step, 1 + CODES_L * DT)
            for ot in range(DT):
                for c in range(DT):
                    last = nc.tensor.transpose(ps[:, c, ot * P:(ot + 1) * P], wl[:, ot, c * P:(c + 1) * P], identf[:])
            last.then_inc(wl_turned, 1)

            pe.wait_ge(wo_low, DT)
            pe.wait_ge(wl_low, DT)

            def turn_att(t):
                pe.wait_ge(head_done, HG0 * ST + 1)
                if t >= 2:
                    pe.wait_ge(att_low, t - 1)
                for c in range(DT):
                    last = nc.tensor.transpose(ps[:, t % 2, c * P:(c + 1) * P], xn[:, t, c * P:(c + 1) * P], identf[:])
                last.then_inc(att_turned, 1)

            turn_att(0)
            for t in range(ST):
                if t >= 2:
                    pe.wait_ge(x1_ready, t - 1)
                for c in range(DT):
                    last = products(pe, ps[:, 2 + t % 2, :], (xth[:, c, t * P:(t + 1) * P], xtl[:, c, t * P:(t + 1) * P]),
                                    (wlh[:, c, :], wll[:, c, :]), c == 0, c == DT - 1)
                last.then_inc(y_ps, 1)
                if t + 1 < ST:
                    turn_att(t + 1)
                pe.wait_ge(att_low, t + 1)
                for c in range(DT):
                    last = products(pe, ps[:, 4 + t % 2, :], (atth[:, t % 2, c, :], attl[:, t % 2, c, :]),
                                    (woh[:, c, :], wol[:, c, :]), c == 0, c == DT - 1)
                last.then_inc(o_ps, 1)

            some = pe.value_load(flag[0:1, 0:1], min_val=0, max_val=1)
            with pe.If(some > 0):
                pe.wait_ge(rare_w, 1)
                for ot in range(DT):
                    for c in range(DT):
                        last = nc.tensor.transpose(ps[:, c, ot * P:(ot + 1) * P], wl[:, ot, c * P:(c + 1) * P], identf[:])
                last.then_inc(rare_turned, 1)
                pe.wait_ge(rare_split, 2 * DT)
                for t in range(ST):
                    if t >= 2:
                        pe.wait_ge(rare_used, 2 * t - 2)
                    for c in range(DT):
                        last = products(pe, ps[:, 6 + t % 2, :], (xth[:, c, t * P:(t + 1) * P], xtl[:, c, t * P:(t + 1) * P]),
                                        (wlh[:, c, :], wll[:, c, :]), c == 0, c == DT - 1)
                    last.then_inc(rare_y, 1)

        @block.scalar
        def _(act):
            norm.scalar_sqrt(nc, act)
            act.wait_ge(wkv_in, 16)
            nc.scalar.activation(wkh[:].rearrange("p c (r d) -> p c r d", r=8),
                                 wkv[:, :, 0:HD0].unsqueeze(2).to_broadcast([P, DT, 8, HD0]), ACT.Copy).then_inc(wk_high, 1)
            nc.scalar.activation(wvh[:], wkv[:, :, HD0:2 * HD0], ACT.Copy).then_inc(wk_high, 1)
            act.wait_ge(wq_in, 16)
            for c in range(DT):
                nc.scalar.activation(wqh[:, c, :], wl[:, c, :], ACT.Copy).then_inc(wq_high, 1)
            norm.scalar_high(nc, act)

            for st in range(ST):
                act.wait_ge(norm.xn_ready, st + 1)
                if st:
                    act.wait_ge(esq_ready, st)
                nc.scalar.activation(rest[:, 0, :], xn[:, st, :], ACT.Square, accum_out=esq[:, st:st + 1]).then_inc(esq_ready, 1)
            act.wait_ge(esq_ready, ST)
            nc.scalar.activation(enorm[:], esq[:], ACT.Sqrt).then_inc(esq_ready, 1)

            def two_parts(src, scale, n, out0, out1):
                nc.scalar.activation(out0, src, ACT.Copy, scale=scale).then_inc(kq_part[0], 1)
                act.wait_ge(kq_rest, n + 1)
                nc.scalar.activation(out1, rest[:, n % 2, :], ACT.Copy).then_inc(kq_part[1], 1)

            for b in range(NB):
                act.wait_ge(k_ps, b + 1)
                cols = slice(b * BLK, (b + 1) * BLK)
                two_parts(bank(b), 1.0, b, parts_sb[0][:, 0, cols], parts_sb[1][:, 0, cols])
            act.wait_ge(v_ps, 1)
            act.wait_ge(v_init, 2)
            nc.scalar.activation(vaug[:, :, 0:HD0], ps[:, 2, 0:ST * HD0].rearrange("p (t d) -> p t d", t=ST),
                                 ACT.Copy).then_inc(v_ready, 1)
            for n in range(4 * NB):
                act.wait_ge(q_ps, n + 1)
                qt, cols = n // NB, slice(n % NB * BLK, (n % NB + 1) * BLK)
                parts_free(act, n)
                two_parts(bank(3 + n), HD0 ** -0.5, NB + n, parts_sb[0][:, (qt + 1) % 2, cols], parts_sb[1][:, (qt + 1) % 2, cols])

            def unit_group(t, hg):
                first = t == 0 and isinstance(hg, int)
                for kt in range(t + 1):
                    act.wait_ge(t_filled, hg * (t + 1) + t_base(t) + kt + 1)
                    if kt < PT0:
                        if not first:
                            act.wait_ge(av_done, hg * (t + 1) + t_base(t))
                    else:
                        act.wait_ge(av_done, hg * (t + 1) + t_base(t) + kt - PT0 + 1)
                    nc.scalar.activation(pt[:, kt % PT0, :], ps[:, TB[kt % 2], :], ACT.Exp).then_inc(exp_done, 1)
                act.wait_ge(av_done, hg * (t + 1) + t_base(t) + t + 1)
                if not first:
                    act.wait_ge(acc_turned, hg + HG0 * t)
                nc.scalar.activation(acc_sb[:], ps[:, ACCB, 0:P], ACT.Copy).then_inc(acc_copied, 1)

            for qt in range(4):
                act.wait_ge(q_stacked[qt], SCATTER)
            for t in range(ST):
                unit_group(t, 0)
                with act.Fori(1, HG0) as hg:
                    unit_group(t, hg)
                if t == 3:
                    act.wait_ge(wo_in, 16)
                    for c in range(DT):
                        nc.scalar.activation(woh[:, c, :], woraw[:, c, :], ACT.Copy).then_inc(wo_high, 1)
            act.wait_ge(wl_turned, 1)
            for c in range(DT):
                nc.scalar.activation(wlh[:, c, :], bank(c), ACT.Copy).then_inc(wl_high, 1)
            for t in range(ST):
                act.wait_ge(att_turned, t + 1)
                if t >= 2:
                    act.wait_ge(o_ps, t - 1)
                nc.scalar.activation(atth[:, t % 2, :, :], bank(t % 2).rearrange("p (c s) -> p c s", c=DT), ACT.Copy).then_inc(att_high, 1)

        @block.vector
        def _(dve):
            dve.sem_inc(head_done, 1)
            nc.vector.memset(vaug[:], 0.0).then_inc(v_init, 1)
            dve.wait_ge(v_init, 1)
            nc.vector.memset(vaug[:, :, HD0:HD0 + 1], 1.0).then_inc(v_init, 1)
            nc.vector.memset(credit[:, 0:1], 0.0).then_inc(m_free, 2)
            norm.vector(nc, dve, lambda e, st: e.wait_ge(x_in[st // 2], 16))
            dve.wait_ge(wk_high, 2)
            nc.vector.tensor_tensor(wkl[:].rearrange("p c (r d) -> p c r d", r=8),
                                    wkv[:, :, 0:HD0].unsqueeze(2).to_broadcast([P, DT, 8, HD0]),
                                    wkh[:].bitcast(F32).rearrange("p c (r d) -> p c r d", r=8), ALU.subtract).then_inc(wk_low, 1)
            nc.vector.tensor_tensor(wvl[:], wkv[:, :, HD0:2 * HD0], wvh[:].bitcast(F32), ALU.subtract).then_inc(wk_low, 1)

            def parts(src, scale, n, part0, part1, part2):
                dve.wait_ge(kq_part[0], n + 1)
                if n >= 2:
                    dve.wait_ge(kq_part[2], n - 1)
                nc.vector.scalar_tensor_tensor(out=rest[:, n % 2, :], in0=src, scalar=scale, in1=part0,
                                               op0=ALU.mult, op1=ALU.subtract).then_inc(kq_rest, 1)
                dve.wait_ge(kq_rest, n + 1)
                dve.wait_ge(kq_part[1], n + 1)
                nc.vector.tensor_tensor(part2, rest[:, n % 2, :], part1, ALU.subtract).then_inc(kq_part[2], 1)

            dve.wait_ge(esq_ready, ST)
            for b in range(NB):
                dve.wait_ge(k_ps, b + 1)
                cols = slice(b * BLK, (b + 1) * BLK)
                parts(bank(b), 1.0, b, *(part[:, 0, cols] for part in parts_sb))
            for n in range(4 * NB):
                dve.wait_ge(q_ps, n + 1)
                qt, cols = n // NB, slice(n % NB * BLK, (n % NB + 1) * BLK)
                parts_free(dve, n)
                parts(bank(3 + n), HD0 ** -0.5, NB + n, *(part[:, (qt + 1) % 2, cols] for part in parts_sb))

            dve.wait_ge(qw_in, 16)
            for level in range(4):
                if level:
                    dve.wait_ge(idx_step, level)
                for j in range(32):
                    nc.vector.tensor_scalar(bits[:, j:DT * D:32], qw[:, level, :, :].rearrange("p c w -> p (c w)"),
                                            j, 1, ALU.logical_shift_right, ALU.bitwise_and).then_inc(bit_step, 1)
                dve.wait_ge(bit_step, 32 * (level + 1))
                if level == 0:
                    nc.vector.tensor_copy(idx[:], bits[:]).then_inc(idx_step, 1)
                else:
                    nc.vector.scalar_tensor_tensor(out=idx[:], in0=bits[:], scalar=float(1 << level),
                                                   in1=idx[:], op0=ALU.mult, op1=ALU.add).then_inc(idx_step, 1)
            dve.wait_ge(idx_step, 4)
            dve.wait_ge(lut_in, 16)
            for k in range(CODES_L * DT):
                c, ot = k // DT, k % DT
                if k >= 2:
                    dve.wait_ge(wl_step, k)
                nc.vector.tensor_scalar(onehot[:, k % 2, :], idx[:, ot * D:(ot + 1) * D], float(c), lutl[:, ot, c:c + 1],
                                        ALU.is_equal, ALU.mult).then_inc(hot_made, 1)

            dve.wait_ge(esq_ready, ST + 1)
            astep = Count(any_step)
            astep.inc(nc.vector.tensor_scalar(masks[:], enorm[:], EST_T, None, ALU.is_gt))
            dve.wait_ge(any_step, 1)
            nc.vector.tensor_reduce(maskf[:], masks[:], AX.X, ALU.max).then_inc(mask_ready, 1)
            dve.wait_ge(any_turned, 1)
            nc.vector.tensor_reduce(flag[:], ps[0:1, 4, 0:P], AX.X, ALU.max).then_inc(flag_ready, 1)

            def head_max(t, h, slot):
                n = h + t * H0
                dve.wait_ge(m_filled, n + 1)
                width = (t + 1) * P
                nc.vector.tensor_reduce(negm[:, t % 2, bass.ds(h, 1)], ps[:, 2 * slot:2 * slot + 2, :].rearrange("p b c -> p (b c)")[:, 0:width],
                                        AX.X, ALU.max, negate=True).then_inc(m_free, 1)

            def maxima(t, hg):
                for j in range(4):
                    head_max(t, hg * 4 + j, j % 2)

            def split_max(t):
                dve.wait_ge(m_turned, t + 1)
                if t:
                    dve.wait_ge(m_rows, 48 * t)
                src = ps[0:H0, TURNB, 0:P]
                nc.vector.tensor_copy(mrows[:, 0, :], src).then_inc(m_split, 1)
                dve.wait_ge(m_split, 3 * t + 1)
                nc.vector.tensor_tensor(mrest[:], src, mrows[:, 0, :], ALU.subtract).then_inc(any_step, 1)
                dve.wait_ge(any_step, 2 + t)
                nc.vector.tensor_copy(mrows[:, 1, :], mrest[:]).then_inc(m_split, 1)
                dve.wait_ge(m_split, 3 * t + 2)
                nc.vector.tensor_tensor(mrows[:, 2, :], mrest[:], mrows[:, 1, :], ALU.subtract).then_inc(m_split, 1)

            def normalise(t, hg):
                u = hg + (HG0 * t - 1)
                dve.wait_ge(acc_turned, u + 1)
                src = ps[:, TURNB, 0:P].rearrange("p (h d) -> p h d", h=4)
                nc.vector.reciprocal(rden[:], src[:, :, HD0]).then_inc(norm_step, 1)
                dve.wait_ge(norm_step, u + 1)
                if isinstance(hg, int) and hg == 0:
                    dst = xn[:, t - 1, (H0 - 4) * HD0:H0 * HD0]
                else:
                    dst = xn[:, t, bass.ds(hg * 64 - 64, 64)]
                nc.vector.tensor_tensor(dst.rearrange("p (h d) -> p h d", h=4), src[:, :, 0:HD0],
                                        rden[:].unsqueeze(2).to_broadcast([P, 4, HD0]), ALU.mult).then_inc(head_done, 1)

            for t in range(2):
                with dve.Fori(0, HG0) as hg:
                    maxima(t, hg)
                split_max(t)
            for t in range(ST):
                if t + 2 < ST:
                    maxima(t + 2, 0)
                if t:
                    normalise(t, 0)
                with dve.Fori(1, HG0) as hg:
                    if t + 2 < ST:
                        maxima(t + 2, hg)
                    normalise(t, hg)
                if t + 2 < ST:
                    split_max(t + 2)
            normalise(ST, 0)

            dve.wait_ge(wl_turned, 1)
            for c in range(DT):
                dve.wait_ge(wl_high, c + 1)
                nc.vector.tensor_tensor(wll[:, c, :], bank(c), wlh[:, c, :].bitcast(F32), ALU.subtract).then_inc(wl_low, 1)

            dve.wait_ge(xb_ready, ST)
            for t in range(ST):
                dve.wait_ge(att_turned, t + 1)
                dve.wait_ge(att_high, t + 1)
                if t >= 2:
                    dve.wait_ge(o_ps, t - 1)
                nc.vector.tensor_tensor(attl[:, t % 2, :, :], bank(t % 2).rearrange("p (c s) -> p c s", c=DT),
                                        atth[:, t % 2, :, :].bitcast(F32), ALU.subtract).then_inc(att_low, 1)
                dve.wait_ge(o_ps, t + 1)
                nc.vector.tensor_tensor(xn[:, t, :], ps[:, 4 + t % 2, :], resid[:, t, :], ALU.add).then_inc(t_ready, 1)
                dve.wait_ge(t_ready, t + 1)
                dve.wait_ge(y_ps, t + 1)
                nc.vector.tensor_tensor(resid[:, t, :], ps[:, 2 + t % 2, :], xn[:, t, :], ALU.add).then_inc(x1_ready, 1)

            some = dve.value_load(flag[0:1, 0:1], min_val=0, max_val=1)
            with dve.If(some > 0):
                step = Count(rare_step)
                dve.wait_ge(luth_in, 16)
                dve.wait_ge(x1_ready, ST)

                def chained(ins):
                    dve.wait_ge(rare_step, step.inc(ins))

                for level in range(NPLANE):
                    for j in range(32):
                        n = step.inc(nc.vector.tensor_scalar(rbits[:, j:DT * D:32], qw[:, level, :, :].rearrange("p c w -> p (c w)"),
                                                             j, 1, ALU.logical_shift_right, ALU.bitwise_and))
                    dve.wait_ge(rare_step, n)
                    if level == 0:
                        chained(nc.vector.tensor_copy(ridx[:], rbits[:]))
                    else:
                        chained(nc.vector.scalar_tensor_tensor(out=ridx[:], in0=rbits[:], scalar=float(1 << level),
                                                               in1=ridx[:], op0=ALU.mult, op1=ALU.add))
                chained(nc.vector.memset(wl[:], 0.0))
                base, per = step.n, 2 * DT + 1
                with dve.Fori(0, CODES_H) as c:
                    for ot in range(DT):
                        nc.vector.tensor_scalar(rhot[:], ridx[:, ot * D:(ot + 1) * D], 0.0, luth[:, ot, bass.ds(c, 1)],
                                                ALU.is_equal, ALU.mult).then_inc(rare_step, 1)
                        dve.wait_ge(rare_step, c * per + (base + 2 * ot + 1))
                        nc.vector.tensor_tensor(wl[:, ot, :], wl[:, ot, :], rhot[:], ALU.add).then_inc(rare_step, 1)
                        dve.wait_ge(rare_step, c * per + (base + 2 * ot + 2))
                    nc.vector.tensor_scalar(ridx[:], ridx[:], -1.0, None, ALU.add).then_inc(rare_step, 1)
                    dve.wait_ge(rare_step, c * per + (base + per))
                nc.vector.memset(credit[:], 0.0).then_inc(rare_w, 1)
                dve.wait_ge(rare_turned, 1)
                for c in range(DT):
                    nc.vector.tensor_copy(wlh[:, c, :], bank(c)).then_inc(rare_split, 1)
                    dve.wait_ge(rare_split, 2 * c + 1)
                    nc.vector.tensor_tensor(wll[:, c, :], bank(c), wlh[:, c, :].bitcast(F32), ALU.subtract).then_inc(rare_split, 1)
                for t in range(ST):
                    dve.wait_ge(rare_y, t + 1)
                    if t:
                        dve.wait_ge(rare_used, 2 * t)
                    nc.vector.tensor_tensor(rsum[:], ps[:, 6 + t % 2, :], xn[:, t, :], ALU.add).then_inc(rare_used, 1)
                    dve.wait_ge(rare_used, 2 * t + 1)
                    dve.wait_ge(x1_ready, ST)
                    nc.vector.copy_predicated(resid[:, t, :], masks[:, t:t + 1].to_broadcast([P, D]), rsum[:]).then_inc(rare_used, 1)
                dve.wait_ge(rare_used, 2 * ST)

        @block.gpsimd
        def _(pool):
            for c in range(DT):
                pool.wait_ge(wq_high, c + 1)
                nc.gpsimd.tensor_tensor(wql[:, c, :], wl[:, c, :], wqh[:, c, :].bitcast(F32), ALU.subtract).then_inc(wq_low, 1)
            pool.wait_ge(wq_low, DT)
            nc.gpsimd.memset(wl[:], 0.0).then_inc(wl_step, 1)
            for k in range(CODES_L * DT):
                c, ot = k // DT, k % DT
                pool.wait_ge(hot_made, k + 1)
                pool.wait_ge(wl_step, max(1, k - 2))
                nc.gpsimd.tensor_tensor(wl[:, ot, :], wl[:, ot, :], onehot[:, k % 2, :], ALU.add).then_inc(wl_step, 1)
            pool.wait_ge(bias_in, 16)
            for st in range(ST):
                pool.wait_ge(norm.xn_ready, st + 1)
                nc.gpsimd.tensor_tensor(resid[:, st, :], resid[:, st, :], biasb[:], ALU.add).then_inc(xb_ready, 1)
            for c in range(DT):
                pool.wait_ge(wo_high, c + 1)
                nc.gpsimd.tensor_tensor(wol[:, c, :], woraw[:, c, :], woh[:, c, :].bitcast(F32), ALU.subtract).then_inc(wo_low, 1)



QUADS = ((7, 0), (6, 1), (5, 2), (4, 3))
PAIRS = [(t, p) for a, b in QUADS for t, p in ((a, 0), (b, 0), (a, 1), (b, 1))]
UNITS = [(j, k) for j, (t, _) in enumerate(PAIRS) for k in range(0, t + 1, 2)]
PT_RING, W_RING, RAW_RING = 4, 3, 2
AHEAD = 3
NPAIR, NUNIT, NHEADS = len(PAIRS), len(UNITS), 2 * len(PAIRS)
NCHUNK, NFILL = 2 + G1, NB * (2 + G1)
ROT_STEPS = 5 + 2 * 9
NTOK = len(PAIRS) // 2


def group_steps(more):
    turns = [("turn", u) for u in range(NUNIT)]
    main = [[] for _ in PAIRS]
    for u, (j, k) in enumerate(UNITS):
        main[j].append(("av", u))
        if u + 2 < NUNIT:
            main[j].append(turns[u + 2])
    out = [("wo", i) for i in range(G1)] + turns[:2]
    for j in range(NPAIR):
        side = []
        if j + AHEAD < NPAIR:
            side += [("qk", 2 * (j + AHEAD)), ("qk", 2 * (j + AHEAD) + 1)]
        q, r = divmod(j, 4)
        if r == 0 and q:
            side.insert(0, ("out", 2 * q - 2))
            side.insert(2, ("out", 2 * q - 1))
        if more and 4 <= j < 4 + W_RING:
            side.append(("w", j - 4))
        if more and j >= NPAIR - 2:
            half = NFILL // 2
            for f in range((j - NPAIR + 2) * half, (j - NPAIR + 3) * half):
                side.append(("proj", f))
                if f % NB == NB - 1 and f // NB + W_RING < NCHUNK:
                    side.append(("w", f // NB + W_RING))
        out += interleave(main[j], side)
    out.append(("out", NTOK - 2))
    if more:
        out += [("vturn", 0), ("vturn", 1)] + [("qknext", n) for n in range(2 * AHEAD)]
    out.append(("out", NTOK - 1))
    return out


def first_steps():
    out = [("w", c) for c in range(W_RING)]
    for f in range(NFILL):
        out.append(("proj", f))
        if f % NB == NB - 1 and f // NB + W_RING < NCHUNK:
            out.append(("w", f // NB + W_RING))
    return out + [("vturn", 0), ("vturn", 1)] + [("qknext", n) for n in range(2 * AHEAD)]


BANK_KINDS = ("turn", "vturn", "out")
SPLIT_FIRST = 2
SPLIT_GROUP = NUNIT + 2


FIRST_TILE = [n for n in range(NHEADS) if PAIRS[n // 2][0] == 0]


class Place:

    def __init__(self, steps):
        self.fill, self.split = {}, {}
        fills = [s for s in steps if s[0] in BANK_KINDS]
        self.fills = fills
        n = 0
        for i, s in enumerate(fills):
            self.fill[s] = i
            if s[0] != "out":
                self.split[s] = n
                n += 1


def layer1(nc, a, keep):
    ctx = ExitStack()
    with ctx:
        def sb(name, shape, dt=F32):
            return ctx.enter_context(nc.sbuf_tensor(name, shape, dt))

        def sem(name):
            return ctx.enter_context(nc.semaphore(name))

        resid, xth, xtl = keep["resid"], keep["xth"], keep["xtl"]
        identf, identb, masku = keep["identf"], keep["identb"], keep["masku"]
        ps = ctx.enter_context(nc.psum_tensor("ps1", [P, 8, 512], F32))

        def bank(b):
            return ps[:, b % 8, :]

        qth, qtl = sb("qth", [P, G1, S], F32R), sb("qtl", [P, G1, S], F32R)
        kth, ktl = sb("kth", [P, S], F32R), sb("ktl", [P, S], F32R)
        k0h, k0l = sb("k0h", [P, 2 * P], F32R), sb("k0l", [P, 2 * P], F32R)
        vh, vl = sb("vh", [P, ST, P], F32R), sb("vl", [P, ST, P], F32R)
        wh, wl = sb("wh", [P, W_RING, BLK], F32R), sb("wl1", [P, W_RING, BLK], F32R)
        woh, wol = sb("woh1", [P, G1, D], F32R), sb("wol1", [P, G1, D], F32R)
        raw = sb("raw", [P, RAW_RING, BLK])
        cos, sin = sb("cos", [P, S]), sb("sin", [P, S])
        kscale, tscale = sb("kscale", [P, P]), sb("tscale", [P, P])
        negm, rowsum, rinv = sb("negm1", [P, NHEADS]), sb("rowsum", [P, NHEADS]), sb("rinv", [P, NHEADS])
        norm = Norm(nc, ctx, keep, "l1_", None, bank)
        with ExitStack() as early:
            norm.xn = early.enter_context(nc.sbuf_tensor("xn1", [P, ST, D], F32))
        with ExitStack() as late:
            def sbl(name, shape, dt=F32):
                return late.enter_context(nc.sbuf_tensor(name, shape, dt))
            plong, pshort = sbl("plong", [P, 2, 2, S]), sbl("pshort", [P, 2, 2, BLK])
            ptnh, ptnl = sbl("ptnh", [P, PT_RING, BLK], F32R), sbl("ptnl", [P, PT_RING, BLK], F32R)
            oth, otl = sbl("oth", [P, 2, G1, P], F32R), sbl("otl", [P, 2, G1, P], F32R)
            rota, rotb = sbl("rota", [P, 2, BLK]), sbl("rotb", [P, 2, BLK])
            vt = sbl("vt", [P, NB, BLK])

        const_in = sem("c1_in")
        raw_in = [sem(f"raw_in{i}") for i in range(RAW_RING)]
        w_split, w_high = sem("w_split"), sem("w_high")
        proj_filled, rope_read, vt_ready = sem("proj_filled"), sem("rope_read"), sem("vt_ready")
        rot_step, kq_ready = sem("rot_step"), sem("kq_ready")
        qk_filled, max_step, max_ready, exp_ready, rinv_ready, p_ready = (
            sem(n) for n in ("qk_filled", "max_step", "max_ready", "exp_ready", "rinv_ready", "p_ready"))
        bank_filled, high_ready, low_ready, av_unit = sem("bank_filled"), sem("bk_high"), sem("bk_low"), sem("av_unit")
        o_high, o_low, y_added = sem("o_high"), sem("o_low"), sem("y_added")
        k0_init, waited = sem("k0_init"), sem("waited")

        block = ctx.enter_context(nc.Block())

        first, more, final = first_steps(), group_steps(True), group_steps(False)
        place_first, place_more, place_final = Place(first), Place(more), Place(final)
        GFILL = len(place_more.fills)
        CHUNKS = NCHUNK + G1

        def length(j):
            return PAIRS[j][0] + 1

        def pbuf(n):
            j, i = divmod(n, 2)
            t = PAIRS[j][0]
            if t >= 4:
                return plong[:, j // 2 % 2, i, 0:(t + 1) * P]
            return pshort[:, j // 2 % 2, i, 0:(t + 1) * P]

        def qk_banks(n):
            return ps[:, 2 * (n % 2):2 * (n % 2) + 2, :].rearrange("p b c -> p (b c)")

        def place_of(g):
            return (place_first if g < 0 else place_final) if isinstance(g, int) else place_more

        def bank_of(s, g):
            return 4 + place_of(g).fill[s] % 2

        def walk(eng, step, lag=0, late_step=None):
            def go(steps, g):
                for i, s in enumerate(steps):
                    step(s, g)
                    if late_step and i >= lag:
                        late_step(steps[i - lag], g)
                if late_step:
                    for s in steps[max(0, len(steps) - lag):]:
                        late_step(s, g)
            go(first, -1)
            with eng.Fori(0, KV1 - 1) as g:
                go(more, g)
            go(final, KV1 - 1)

        def fill_count(s, g):
            if isinstance(g, int) and g < 0:
                return place_first.fill[s]
            return g * GFILL + (SPLIT_FIRST + place_of(g).fill[s])

        def split_count(s, g):
            if isinstance(g, int) and g < 0:
                return place_first.split[s]
            return g * SPLIT_GROUP + (SPLIT_FIRST + place_of(g).split[s])

        def free_probabilities(eng, n, g):
            j = n // 2
            if j >= 4:
                u = max(i for i, (jj, _) in enumerate(UNITS) if jj == j - 4)
                eng.wait_ge(bank_filled, fill_count(("turn", u), g) + 1)

        @block.sync
        def _(sp):
            sp.dma_start(cos[:], a["cos"]).then_inc(const_in, 16)
            sp.dma_start(sin[:], a["sin"]).then_inc(const_in, 16)
            sp.dma_start(kscale[:], a["kscale"]).then_inc(const_in, 16)
            sp.dma_start(tscale[:], a["tscale"]).then_inc(const_in, 16)

            def load(c, g, k):
                r = k % RAW_RING
                src = a["w1"][g, c] if c < NCHUNK else a["wo1"][g, c - NCHUNK]
                sp.dma_start(raw[:, r, :], src).then_inc(raw_in[r], 16)

            for c in range(NCHUNK):
                if c >= RAW_RING:
                    sp.wait_ge(w_split, c - RAW_RING + 1)
                load(c, 0, c)
            def group(g, chunks):
                for k in range(chunks):
                    sp.wait_ge(w_split, g * CHUNKS + (NCHUNK + k - RAW_RING + 1))
                    if k < G1:
                        load(NCHUNK + k, g, k)
                    else:
                        load(k - G1, g + 1, k)

            with sp.Fori(0, KV1 - 1) as g:
                group(g, CHUNKS)
            group(KV1 - 1, G1)

        @block.tensor
        def _(pe):
            norm.tensor(nc, pe)

            def proj(f, g):
                c, b = divmod(f, NB)
                if f < 4:
                    if isinstance(g, int) and g == 0:
                        if f == 0:
                            pe.wait_ge(norm.low_ready, ST)
                    else:
                        pe.wait_ge(exp_ready, g * NHEADS)
                elif f < 6:
                    pe.wait_ge(rope_read, g * 10 + (f - 3))
                elif f < 8:
                    pe.wait_ge(vt_ready, g * 2 + (f - 5))
                else:
                    pe.wait_ge(rope_read, g * 10 + (f - 5))
                if b == 0:
                    pe.wait_ge(w_split, g * CHUNKS + (c + 1))
                for d in range(DT):
                    w = (wh[:, c % W_RING, d * P:(d + 1) * P], wl[:, c % W_RING, d * P:(d + 1) * P])
                    last = products(pe, bank(f % 4), w, (xth[:, d, b * BLK:(b + 1) * BLK], xtl[:, d, b * BLK:(b + 1) * BLK]),
                                    d == 0, d == DT - 1)
                last.then_inc(proj_filled, 1)

            def qk(n, g):
                j, i = divmod(n, 2)
                t, p = PAIRS[j]
                h = 2 * p + i
                if n >= 2:
                    pe.wait_ge(exp_ready, g * NHEADS + (n - 1))
                else:
                    pe.wait_ge(rope_read, g * 10 + 10)
                    pe.wait_ge(vt_ready, g * 2 + 2)
                pe.wait_ge(kq_ready, g * 10 + (2 * h + 4))
                q = (qth[:, h, t * P:(t + 1) * P], qtl[:, h, t * P:(t + 1) * P])
                out = qk_banks(n)
                width = (t + 1) * P
                for c0 in range(0, width, BLK):
                    w = max(2 * P, min(BLK, width - c0))
                    k = (k0h[:, 0:w], k0l[:, 0:w]) if t == 0 else (kth[:, c0:c0 + w], ktl[:, c0:c0 + w])
                    products(pe, out[:, c0:c0 + w], q, k, True, c0 + BLK < width)
                pe.matmul(out[:, t * P:(t + 1) * P], identb[:], masku[:], start=False, stop=True).then_inc(qk_filled, 1)

            def bank_free(s, g):
                if isinstance(g, int) and g < 0:
                    return
                place = place_of(g)
                i = place.fill[s]
                past = place.fills[i - 2] if i >= 2 else place_more.fills[i - 2]
                if past[0] == "out":
                    pe.wait_ge(y_added, g * NTOK + (past[1] + 2 - (0 if i >= 2 else NTOK)))
                else:
                    pe.wait_ge(low_ready, g * SPLIT_GROUP + (SPLIT_FIRST + place_more.split[past] + 1 - (0 if i >= 2 else SPLIT_GROUP)))

            def turn(u, g):
                j, k = UNITS[u]
                t = PAIRS[j][0]
                bank_free(("turn", u), g)
                pe.wait_ge(p_ready, g * NPAIR + (j + 1))
                b = bank_of(("turn", u), g)
                for kk in range(k, min(k + 2, t + 1)):
                    for i in range(2):
                        last = nc.tensor.transpose(ps[:, b, (2 * (kk - k) + i) * P:(2 * (kk - k) + i + 1) * P],
                                                   pbuf(2 * j + i)[:, kk * P:(kk + 1) * P], identf[:])
                last.then_inc(bank_filled, 1)

            def av(u, g):
                j, k = UNITS[u]
                t = PAIRS[j][0]
                if k == 0:
                    pe.wait_ge(o_low, g * NPAIR + max(1, j))
                pe.wait_ge(low_ready, split_count(("turn", u), g) + 1)
                for kk in range(k, min(k + 2, t + 1)):
                    c = 2 * P * (kk - k)
                    last = products(pe, ps[:, 6 + j % 2, 0:2 * P], (vh[:, kk, :], vl[:, kk, :]),
                                    (ptnh[:, u % PT_RING, c:c + 2 * P], ptnl[:, u % PT_RING, c:c + 2 * P]), kk == 0, kk == t)
                last.then_inc(av_unit, 1)

            def out(o, g):
                q, ab = divmod(o, 2)
                bank_free(("out", o), g)
                pe.wait_ge(o_low, g * NPAIR + (4 * q + 4 + ab))
                pe.wait_ge(w_split, g * CHUNKS + CHUNKS)
                b = bank_of(("out", o), g)
                for h in range(G1):
                    last = products(pe, bank(b), (oth[:, ab, h, :], otl[:, ab, h, :]), (woh[:, h, :], wol[:, h, :]), h == 0, h == G1 - 1)
                last.then_inc(bank_filled, 1)

            def vturn(v, g):
                bank_free(("vturn", v), g)
                pe.wait_ge(vt_ready, (g + 1) * 2 + (v + 1))
                b = bank_of(("vturn", v), g)
                for i in range(4):
                    last = nc.tensor.transpose(ps[:, b, i * P:(i + 1) * P], vt[:, v, i * P:(i + 1) * P], identf[:])
                last.then_inc(bank_filled, 1)

            def step(s, g):
                kind, i = s
                if kind == "proj":
                    proj(i, g + 1)
                elif kind == "qk":
                    qk(i, g)
                elif kind == "qknext":
                    qk(i, g + 1)
                elif kind == "turn":
                    turn(i, g)
                elif kind == "av":
                    av(i, g)
                elif kind == "out":
                    out(i, g)
                elif kind == "vturn":
                    vturn(i, g)

            pe.wait_ge(k0_init, 2)
            walk(pe, step)

        @block.scalar
        def _(act):
            norm.scalar_sqrt(nc, act)
            norm.scalar_high(nc, act)

            def step(s, g):
                kind, i = s
                if kind == "proj" and i in (2, 3):
                    gg = g + 1
                    act.wait_ge(proj_filled, gg * NFILL + (i + 1))
                    nc.scalar.activation(vt[:, i - 2, :], bank(i), ACT.Copy).then_inc(vt_ready, 1)
                elif kind in ("turn", "vturn"):
                    act.wait_ge(bank_filled, fill_count(s, g) + 1)
                    if kind == "turn":
                        j, k = UNITS[i]
                        w = 2 * P * min(2, PAIRS[j][0] + 1 - k)
                        if i >= PT_RING:
                            act.wait_ge(av_unit, g * NUNIT + (i - PT_RING + 1))
                        b = bank_of(s, g)
                        nc.scalar.activation(ptnh[:, i % PT_RING, 0:w], ps[:, b, 0:w], ACT.Copy).then_inc(high_ready, 1)
                    else:
                        gg = g + 1
                        b = bank_of(s, g)
                        act.wait_ge(av_unit, gg * NUNIT)
                        nc.scalar.activation(vh[:, 4 * i:4 * i + 4, :], bank(b).rearrange("p (t d) -> p t d", t=4),
                                             ACT.Copy).then_inc(high_ready, 1)
                elif kind == "av":
                    j, k = UNITS[i]
                    t, p = PAIRS[j]
                    if k + 2 > t:
                        act.wait_ge(av_unit, g * NUNIT + (i + 1))
                        ab = j % 2
                        act.wait_ge(y_added, g * NTOK + max(1, 2 * (j // 4) + ab))
                        nc.scalar.activation(oth[:, ab, 2 * p:2 * p + 2, :], ps[:, 6 + j % 2, 0:2 * P].rearrange("p (h q) -> p h q", h=2),
                                             ACT.Copy).then_inc(o_high, 1)

            def late_step(s, g):
                kind, n = s
                if kind in ("qk", "qknext"):
                    gg = g + 1 if kind == "qknext" else g
                    j, i = divmod(n, 2)
                    t = PAIRS[j][0]
                    act.wait_ge(max_ready, gg * NHEADS + (n + 1))
                    src = qk_banks(n)[:, 0:(t + 1) * P] if t else pbuf(n)
                    if t:
                        free_probabilities(act, n, gg)
                    nc.scalar.activation(pbuf(n), src, ACT.Exp, bias=negm[:, n:n + 1], accum_out=rowsum[:, n:n + 1]).then_inc(exp_ready, 1)

            walk(act, step, 1, late_step)

        @block.vector
        def _(dve):
            dve.sem_inc(y_added, 1)
            dve.sem_inc(o_low, 1)
            nc.vector.memset(k0h[:].bitcast(F32), 0.0).then_inc(k0_init, 1)
            nc.vector.memset(k0l[:].bitcast(F32), 0.0).then_inc(k0_init, 1)
            norm.vector(nc, dve, lambda e, st: None)
            dve.wait_ge(norm.xn_ready, ST)
            dve.wait_ge(const_in, 64)

            def rope(f, g):
                gg = g + 1
                r = f if f < 2 else f - 2
                c = HD1 ** -0.5 if f >= 4 else 1.0
                dve.wait_ge(proj_filled, gg * NFILL + (f + 1))
                if r >= 2 or not isinstance(gg, int):
                    dve.wait_ge(kq_ready, gg * 10 + (r - 1))
                cols = slice(f % NB * BLK, (f % NB + 1) * BLK)
                src = bank(f % 4)
                nc.vector.scalar_tensor_tensor(out=rota[:, r % 2, :], in0=src, scalar=c, in1=cos[:, cols], op0=ALU.mult, op1=ALU.mult)
                nc.vector.scalar_tensor_tensor(out=rotb[0:64, r % 2, :], in0=src[64:128, :], scalar=c, in1=sin[64:128, cols],
                                               op0=ALU.mult, op1=ALU.mult)
                nc.vector.scalar_tensor_tensor(out=rotb[64:128, r % 2, :], in0=src[0:64, :], scalar=c, in1=sin[0:64, cols],
                                               op0=ALU.mult, op1=ALU.mult).then_inc(rope_read, 1)

            def step(s, g):
                kind, i = s
                if kind == "proj" and i not in (2, 3):
                    rope(i, g)
                elif kind in ("qk", "qknext"):
                    gg = g + 1 if kind == "qknext" else g
                    t = PAIRS[i // 2][0]
                    dve.wait_ge(qk_filled, gg * NHEADS + (i + 1))
                    if t:
                        nc.vector.tensor_reduce(negm[:, i:i + 1], qk_banks(i)[:, 0:(t + 1) * P], AX.X, ALU.max, negate=True).then_inc(max_ready, 1)
                    else:
                        free_probabilities(dve, i, gg)
                        nc.vector.tensor_tensor(pbuf(i), qk_banks(i)[:, 0:P], tscale[:], ALU.mult).then_inc(max_step, 1)
                        dve.wait_ge(max_step, gg * 4 + FIRST_TILE.index(i) + 1)
                        nc.vector.tensor_reduce(negm[:, i:i + 1], pbuf(i), AX.X, ALU.max, negate=True).then_inc(max_ready, 1)
                elif kind in ("turn", "vturn"):
                    dve.wait_ge(high_ready, split_count(s, g) + 1)
                    if kind == "turn":
                        j, k = UNITS[i]
                        w = 2 * P * min(2, PAIRS[j][0] + 1 - k)
                        b = bank_of(s, g)
                        nc.vector.tensor_tensor(ptnl[:, i % PT_RING, 0:w], ps[:, b, 0:w], ptnh[:, i % PT_RING, 0:w].bitcast(F32),
                                                ALU.subtract).then_inc(low_ready, 1)
                    else:
                        b = bank_of(s, g)
                        nc.vector.tensor_tensor(vl[:, 4 * i:4 * i + 4, :], bank(b).rearrange("p (t d) -> p t d", t=4),
                                                vh[:, 4 * i:4 * i + 4, :].bitcast(F32), ALU.subtract).then_inc(low_ready, 1)
                elif kind == "av":
                    j, k = UNITS[i]
                    t, p = PAIRS[j]
                    if k + 2 > t:
                        dve.wait_ge(o_high, g * NPAIR + (j + 1))
                        ab = j % 2
                        nc.vector.tensor_tensor(otl[:, ab, 2 * p:2 * p + 2, :], ps[:, 6 + j % 2, 0:2 * P].rearrange("p (h q) -> p h q", h=2),
                                                oth[:, ab, 2 * p:2 * p + 2, :].bitcast(F32), ALU.subtract).then_inc(o_low, 1)
                elif kind == "out":
                    t = QUADS[i // 2][i % 2]
                    dve.wait_ge(bank_filled, fill_count(s, g) + 1)
                    dve.wait_ge(y_added, g * NTOK + 1)
                    nc.vector.tensor_tensor(resid[:, t, :], ps[:, bank_of(s, g), :], resid[:, t, :], ALU.add).then_inc(y_added, 1)

            def late_step(s, g):
                kind, n = s
                if kind in ("qk", "qknext") and n % 2 == 1:
                    gg = g + 1 if kind == "qknext" else g
                    dve.wait_ge(exp_ready, gg * NHEADS + (n + 1))
                    nc.vector.reciprocal(rinv[:, n - 1:n + 1], rowsum[:, n - 1:n + 1]).then_inc(rinv_ready, 1)

            walk(dve, step, 2, late_step)

        @block.gpsimd
        def _(pool):
            def split(src, high, low, n):
                pool.sem_inc(waited, 1)
                nc.gpsimd.tensor_scalar(high, src, 1.0, 1.0, ALU.mult, ALU.mult).then_inc(w_high, 1)
                pool.wait_ge(w_high, n)
                nc.gpsimd.tensor_tensor(low, src, high.bitcast(F32), ALU.subtract).then_inc(w_split, 1)

            def rotated(f, gg):
                r = f if f < 2 else f - 2
                base = 0 if r == 0 else 5 + 2 * (r - 1)
                pool.wait_ge(rope_read, gg * 10 + (r + 1))
                pool.wait_ge(qk_filled, gg * NHEADS)
                sums, other = rota[:, r % 2, :], rotb[:, r % 2, :]

                def chained(ins, n):
                    ins.then_inc(rot_step, 1)
                    pool.wait_ge(rot_step, gg * ROT_STEPS + (base + n))

                chained(nc.gpsimd.tensor_tensor(sums, sums, other, ALU.add), 1)
                cols = slice(f % NB * BLK, (f % NB + 1) * BLK)
                if r == 0:
                    pool.sem_inc(waited, 1)
                    chained(nc.gpsimd.tensor_scalar(k0h[:, 0:P], sums[:, 0:P], 1.0, 1.0, ALU.mult, ALU.mult), 2)
                    chained(nc.gpsimd.tensor_tensor(k0l[:, 0:P], sums[:, 0:P], k0h[:, 0:P].bitcast(F32), ALU.subtract), 3)
                    chained(nc.gpsimd.tensor_tensor(sums[:, 0:P], sums[:, 0:P], kscale[:], ALU.mult), 4)
                high, low = (kth[:, cols], ktl[:, cols]) if r < 2 else (qth[:, (r - 2) // NB, cols], qtl[:, (r - 2) // NB, cols])
                pool.sem_inc(waited, 1)
                chained(nc.gpsimd.tensor_scalar(high, sums, 1.0, 1.0, ALU.mult, ALU.mult), 5 if r == 0 else 2)
                nc.gpsimd.tensor_tensor(low, sums, high.bitcast(F32), ALU.subtract).then_inc(kq_ready, 1)

            def step(s, g):
                kind, i = s
                gg = g + 1
                if kind == "w":
                    pool.wait_ge(raw_in[i % RAW_RING], gg * (8 * CHUNKS) + 16 * (i // RAW_RING + 1))
                    if i >= W_RING:
                        pool.wait_ge(proj_filled, gg * NFILL + NB * (i - W_RING + 1))
                    else:
                        pool.wait_ge(proj_filled, gg * NFILL)
                    split(raw[:, i % RAW_RING, :], wh[:, i % W_RING, :], wl[:, i % W_RING, :], gg * CHUNKS + (i + 1))
                elif kind == "wo":
                    k = NCHUNK + i
                    pool.wait_ge(raw_in[k % RAW_RING], g * (8 * CHUNKS) + 16 * (k // RAW_RING + 1))
                    pool.wait_ge(y_added, g * NTOK + 1)
                    split(raw[:, k % RAW_RING, :], woh[:, i, :], wol[:, i, :], g * CHUNKS + (k + 1))
                elif kind == "proj" and i not in (2, 3):
                    rotated(i, gg)

            def late_step(s, g):
                kind, n = s
                if kind in ("qk", "qknext") and n % 2 == 1:
                    gg = g + 1 if kind == "qknext" else g
                    pool.wait_ge(rinv_ready, gg * NPAIR + (n // 2 + 1))
                    pool.sem_inc(waited, 1)
                    nc.gpsimd.tensor_scalar(pbuf(n - 1), pbuf(n - 1), rinv[:, n - 1:n], 1.0, ALU.mult, ALU.mult)
                    nc.gpsimd.tensor_scalar(pbuf(n), pbuf(n), rinv[:, n:n + 1], 1.0, ALU.mult, ALU.mult).then_inc(p_ready, 1)

            pool.wait_ge(const_in, 64)
            pool.wait_ge(k0_init, 2)
            walk(pool, step, 2, late_step)



FT = -(-FH // P)
FLAST = FH - (FT - 1) * P
RS, RROWS = 32, 96


def gated(nc, a, keep):
    ctx = ExitStack()
    with ctx:
        def sb(name, shape, dt=F32):
            return ctx.enter_context(nc.sbuf_tensor(name, shape, dt))

        def sem(name):
            return ctx.enter_context(nc.semaphore(name))

        resid, xth, xtl = keep["resid"], keep["xth"], keep["xtl"]
        ps = ctx.enter_context(nc.psum_tensor("ps2", [P, 8, 512], F32))
        raw = sb("raw2", [P, 6, BLK])
        wh, wl = sb("wh2", [P, 6, BLK], F32R), sb("wl2", [P, 6, BLK], F32R)
        sg, hid = sb("sg", [P, NB, BLK]), sb("hid", [P, NB, BLK])
        hidh, hidl = sb("hidh", [P, 2, S], F32R), sb("hidl", [P, 2, S], F32R)
        araw = sb("araw", [P, 2 * DT + FT, RANK])
        asplit = sb("asplit", [P, 2, 2 * DT + FT, RROWS], F32R)
        ah, al = asplit[:, 0, :, :], asplit[:, 1, :, :]
        bnow, anow = sb("bnow", [RROWS, 2, 2, P], F32R), sb("anow", [P, 2, 2, RROWS], F32R)
        BW = 2 * FH + D
        braw, bs = sb("braw", [RROWS, BW]), sb("bs", [RROWS, BW], F32R)
        xa = sb("xa", [RROWS, 2, S], F32R)
        zero = sb("zero", [P, P], BF16)
        ha = sb("ha", [RROWS, S], F32R)

        raw_in = [sem(f"raw2_in{i}") for i in range(6)]
        zero_ready, now_ready, waited = sem("zero_ready"), sem("now_ready"), sem("waited2")
        a_in, b_in, b_zero, a_zero = sem("a_in"), sem("b_in"), sem("b_zero"), sem("a_zero")
        a_high, a_low, b_high, b_ready = sem("a_high"), sem("a_low"), sem("b_high"), sem("b_ready")
        xa_filled, xa_high, xa_ready = sem("xa_filled"), sem("xa_high"), sem("xa_ready")
        w_high, w_split = sem("w2_high"), sem("w2_split")
        gu_filled, silu_done, hid_made, hid_high, hid_low = (sem(n) for n in ("gu_filled", "silu_done", "hid_made", "hid_high", "hid_low"))
        ha_filled, ha_high, ha_ready = sem("ha_filled"), sem("ha_high"), sem("ha_ready")
        down_filled, added, out_done = sem("down_filled"), sem("added"), sem("out2_done")
        block = ctx.enter_context(nc.Block())

        def rows(j):
            return FLAST if isinstance(j, int) and j == FT - 1 else P

        def walk(eng, start, body):
            start()
            loops = (FT - 2) // 2
            with eng.Fori(0, loops) as jj:
                body(jj * 2, 0)
                body(jj * 2 + 1, 1)
            for j in range(2 * loops, FT):
                body(j, j % 2)

        @block.sync
        def _(sp):
            def load(j, par, which):
                if not (isinstance(j, int) and j < 2):
                    sp.wait_ge(w_split, 3 * j + (which - 5))
                k, n = 3 * par + which, rows(j)
                if which < 2:
                    name = "gate" if which == 0 else "up"
                    src = a[name + "_last"] if n < P else a[name + "_main"][j]
                    sp.dma_start(raw[:, k, 0:DT * n], src).then_inc(raw_in[k], 16)
                else:
                    src = a["down_main"][j] if n == P else a["down_last"]
                    sp.dma_start(raw[0:n, k, :], src).then_inc(raw_in[k], 16)

            sp.dma_start(araw[:, 0:DT, :], a["gate_a"].rearrange("(c p) r -> p c r", p=P)).then_inc(a_in, 16)
            sp.dma_start(araw[:, DT:2 * DT, :], a["up_a"].rearrange("(c p) r -> p c r", p=P)).then_inc(a_in, 16)
            for which in (0, 1):
                load(0, 0, which)
            sp.wait_ge(a_zero, 1)
            sp.dma_start(araw[:, 2 * DT:2 * DT + FT - 1, :], a["down_a"][0:(FT - 1) * P, :].rearrange("(c p) r -> p c r", p=P)).then_inc(a_in, 16)
            sp.dma_start(araw[0:FLAST, 2 * DT + FT - 1, :], a["down_a"][(FT - 1) * P:FH, :]).then_inc(a_in, 16)
            sp.wait_ge(b_zero, 1)
            for r in range(3):
                for name, c0, n in (("gate_b", 0, FH), ("up_b", FH, FH), ("down_b", 2 * FH, D)):
                    sp.dma_start(braw[RS * r:RS * r + RANK, c0:c0 + n], a[name]).then_inc(b_in, 16)
            load(0, 0, 2)
            for which in (0, 1, 2):
                load(1, 1, which)

            def body(j, par):
                if not (isinstance(j, int) and j + 2 >= FT):
                    for which in (0, 1, 2):
                        load(j + 2, par, which)
            walk(sp, lambda: None, body)
            for t in range(ST):
                sp.wait_ge(added, ST * (FT - 1) + t + 2)
                sp.dma_start(a["out"].rearrange("(t p) d -> p t d", p=P)[:, t, :], resid[:, t, :]).then_inc(out_done, 16)
            sp.wait_ge(out_done, 16 * ST)

        @block.tensor
        def _(pe):
            pe.sem_inc(down_filled, 1)
            pe.wait_ge(a_low, 1)
            for g in range(2):
                for b in range(NB):
                    for d in range(DT):
                        last = products(pe, ps[0:RROWS, 2 * g + b, :], (ah[:, g * DT + d, :], al[:, g * DT + d, :]),
                                        (xth[:, d, b * BLK:(b + 1) * BLK], xtl[:, d, b * BLK:(b + 1) * BLK]), d == 0, d == DT - 1)
                    last.then_inc(xa_filled, 1)

            def gate_up(j, par):
                n = rows(j)
                for b in range(NB):
                    if isinstance(j, int) and j == 0:
                        pe.wait_ge(xa_ready, 4)
                    else:
                        pe.wait_ge(hid_made, j * 2 + (b - 1))
                    for which in range(2):
                        if b == 0:
                            pe.wait_ge(w_split, 3 * j + which + 1)
                        k = 3 * par + which
                        w3h = wh[:, k, 0:DT * n].rearrange("p (d n) -> p d n", d=DT)
                        w3l = wl[:, k, 0:DT * n].rearrange("p (d n) -> p d n", d=DT)
                        out = ps[0:n, 2 * b + which, :]
                        for d in range(DT):
                            products(pe, out, (w3h[:, d, :], w3l[:, d, :]),
                                     (xth[:, d, b * BLK:(b + 1) * BLK], xtl[:, d, b * BLK:(b + 1) * BLK]), d == 0, False)
                        pe.wait_ge(now_ready, 2 * j + 2)
                        last = pe.matmul(out, bnow[:, par, which, 0:n], xa[:, which, b * BLK:(b + 1) * BLK], start=False, stop=True)
                    last.then_inc(gu_filled, 1)

            def hidden_a(j, par):
                n = rows(j)
                pe.wait_ge(hid_low, 2 * j + 2)
                for b in range(NB):
                    cols = slice(b * BLK, (b + 1) * BLK)
                    l = (anow[0:n, par, 0, :], anow[0:n, par, 1, :])
                    r = (hidh[0:n, par, cols], hidl[0:n, par, cols])
                    start = isinstance(j, int) and j == 0
                    lastj = isinstance(j, int) and j == FT - 1
                    last = products(pe, ps[0:RROWS, 6 + b, :], l, r, start, lastj)
                    if lastj:
                        last.then_inc(ha_filled, 1)

            def down(j, par):
                n = rows(j)
                pe.wait_ge(w_split, 3 * j + 3)
                lastj = isinstance(j, int) and j == FT - 1
                if lastj:
                    pe.wait_ge(ha_ready, NB)
                for t in range(ST):
                    if not (isinstance(j, int) and j == 0 and t < 2):
                        pe.wait_ge(added, ST * j + max(1, t))
                    out = ps[:, 4 + t % 2, :]
                    last = products(pe, out, (hidh[0:n, par, t * P:(t + 1) * P], hidl[0:n, par, t * P:(t + 1) * P]),
                                    (wh[0:n, 3 * par + 2, :], wl[0:n, 3 * par + 2, :]), True, not lastj)
                    if lastj:
                        last = pe.matmul(out, ha[:, t * P:(t + 1) * P], bs[:, 2 * FH:2 * FH + D], start=False, stop=True)
                    last.then_inc(down_filled, 1)

            def start():
                pe.wait_ge(b_ready, 1)
                gate_up(0, 0)
                pe.wait_ge(zero_ready, 1)
                for b in range(NB):
                    pe.matmul(ps[0:RROWS, 6 + b, :], zero[:, 0:RROWS], zero[:, 0:1].to_broadcast([P, BLK]), start=True, stop=False)

            def body(j, par):
                if not (isinstance(j, int) and j == FT - 1):
                    gate_up(j + 1, 1 - par)
                hidden_a(j, par)
                down(j, par)
            walk(pe, start, body)

        @block.scalar
        def _(act):
            for g in range(2):
                for b in range(NB):
                    act.wait_ge(xa_filled, 2 * g + b + 1)
                    nc.scalar.activation(xa[:, g, b * BLK:(b + 1) * BLK], ps[0:RROWS, 2 * g + b, :], ACT.Copy).then_inc(xa_high, 1)

            def low_rank(j, par):
                n = rows(j)
                if not (isinstance(j, int) and j < 2):
                    act.wait_ge(down_filled, ST * j - (ST - 1))
                cols = slice(j * P, j * P + n) if isinstance(j, int) else bass.ds(j * P, n)
                nc.scalar.activation(bnow[:, par, :, 0:n], bs[:, 0:2 * FH].bitcast(F32).rearrange("p (w n) -> p w n", w=2)[:, :, cols],
                                     ACT.Copy).then_inc(now_ready, 1)
                tile = slice(2 * DT + j, 2 * DT + j + 1) if isinstance(j, int) else bass.ds(2 * DT + j, 1)
                nc.scalar.activation(anow[:, par, :, :].unsqueeze(2), asplit[:, :, tile, :].bitcast(F32), ACT.Copy).then_inc(now_ready, 1)

            def hidden(j, par):
                n = rows(j)
                for b in range(NB):
                    act.wait_ge(gu_filled, 2 * j + (b + 1))
                    nc.scalar.activation(sg[0:n, b, :], ps[0:n, 2 * b, :], ACT.Silu).then_inc(silu_done, 1)
                for b in range(NB):
                    act.wait_ge(hid_made, 2 * j + (b + 1))
                    if not (isinstance(j, int) and j < 2):
                        act.wait_ge(down_filled, ST * j - (ST - 1))
                    nc.scalar.activation(hidh[0:n, par, b * BLK:(b + 1) * BLK], hid[0:n, b, :], ACT.Copy).then_inc(hid_high, 1)

            def body(j, par):
                if not (isinstance(j, int) and j == FT - 1):
                    low_rank(j + 1, 1 - par)
                    hidden(j + 1, 1 - par)

            def start():
                act.wait_ge(b_ready, 1)
                low_rank(0, 0)
                hidden(0, 0)
            walk(act, start, body)
            for b in range(NB):
                act.wait_ge(ha_filled, b + 1)
                nc.scalar.activation(ha[:, b * BLK:(b + 1) * BLK], ps[0:RROWS, 6 + b, :], ACT.Copy).then_inc(ha_high, 1)

        @block.vector
        def _(dve):
            dve.sem_inc(added, 1)
            nc.vector.memset(araw[:, 2 * DT + FT - 1, :], 0.0).then_inc(a_zero, 1)
            nc.vector.memset(braw[:], 0.0).then_inc(b_zero, 1)
            nc.vector.memset(zero[:], 0.0).then_inc(zero_ready, 1)
            dve.wait_ge(a_in, 64)
            rep = araw[:].unsqueeze(2).to_broadcast([P, 2 * DT + FT, RROWS // RANK, RANK])
            nc.vector.tensor_copy(ah.rearrange("p c (k r) -> p c k r", r=RANK), rep).then_inc(a_high, 1)
            dve.wait_ge(a_high, 1)
            nc.vector.tensor_tensor(al.rearrange("p c (k r) -> p c k r", r=RANK), rep,
                                    ah.bitcast(F32).rearrange("p c (k r) -> p c k r", r=RANK), ALU.subtract).then_inc(a_low, 1)
            dve.wait_ge(b_in, 16 * 9)
            nc.vector.tensor_copy(bs[:], braw[:]).then_inc(b_high, 1)
            dve.wait_ge(b_high, 1)
            nc.vector.tensor_tensor(bs[RS:2 * RS, :], braw[RS:2 * RS, :], bs[RS:2 * RS, :].bitcast(F32), ALU.subtract).then_inc(b_ready, 1)
            for g in range(2):
                for b in range(NB):
                    dve.wait_ge(xa_high, 2 * g + b + 1)
                    part = xa[2 * RS:RROWS, g, b * BLK:(b + 1) * BLK]
                    nc.vector.tensor_tensor(part, ps[2 * RS:RROWS, 2 * g + b, :], part.bitcast(F32), ALU.subtract).then_inc(xa_ready, 1)

            def hidden(j):
                n = rows(j)
                for b in range(NB):
                    dve.wait_ge(silu_done, 2 * j + (b + 1))
                    if not (isinstance(j, int) and j == 0):
                        dve.wait_ge(hid_low, 2 * j + (b - 1))
                    nc.vector.tensor_tensor(hid[0:n, b, :], ps[0:n, 2 * b + 1, :], sg[0:n, b, :], ALU.mult).then_inc(hid_made, 1)

            def body(j, par):
                if not (isinstance(j, int) and j == FT - 1):
                    hidden(j + 1)
                else:
                    for b in range(NB):
                        dve.wait_ge(ha_high, b + 1)
                        part = ha[2 * RS:RROWS, b * BLK:(b + 1) * BLK]
                        nc.vector.tensor_tensor(part, ps[2 * RS:RROWS, 6 + b, :], part.bitcast(F32), ALU.subtract).then_inc(ha_ready, 1)
                dve.wait_ge(added, ST * j + 1)
                for t in range(ST):
                    dve.wait_ge(down_filled, ST * j + (t + 2))
                    nc.vector.tensor_tensor(resid[:, t, :], ps[:, 4 + t % 2, :], resid[:, t, :], ALU.add).then_inc(added, 1)
            walk(dve, lambda: hidden(0), body)

        @block.gpsimd
        def _(pool):
            def split(j, par, which):
                k, n = 3 * par + which, rows(j)
                pool.wait_ge(raw_in[k], 8 * (j - par) + 16)
                if not (isinstance(j, int) and j < 2):
                    if which < 2:
                        pool.wait_ge(gu_filled, 2 * j - 2)
                    else:
                        pool.wait_ge(down_filled, ST * j - (ST - 1))
                if which < 2:
                    src, high, low = raw[:, k, 0:DT * n], wh[:, k, 0:DT * n], wl[:, k, 0:DT * n]
                else:
                    src, high, low = raw[0:n, k, :], wh[0:n, k, :], wl[0:n, k, :]
                pool.sem_inc(waited, 1)
                nc.gpsimd.tensor_scalar(high, src, 1.0, 1.0, ALU.mult, ALU.mult).then_inc(w_high, 1)
                pool.wait_ge(w_high, 3 * j + which + 1)
                nc.gpsimd.tensor_tensor(low, src, high.bitcast(F32), ALU.subtract).then_inc(w_split, 1)

            def hidden(j, par):
                n = rows(j)
                for b in range(NB):
                    pool.wait_ge(hid_high, 2 * j + (b + 1))
                    cols = slice(b * BLK, (b + 1) * BLK)
                    nc.gpsimd.tensor_tensor(hidl[0:n, par, cols], hid[0:n, b, :], hidh[0:n, par, cols].bitcast(F32), ALU.subtract).then_inc(hid_low, 1)

            def start():
                for which in range(3):
                    split(0, 0, which)
                for which in range(3):
                    split(1, 1, which)
                hidden(0, 0)

            def body(j, par):
                if not (isinstance(j, int) and j == FT - 1):
                    hidden(j + 1, 1 - par)
                if not (isinstance(j, int) and j + 2 >= FT):
                    for which in range(3):
                        split(j + 2, par, which)
            walk(pool, start, body)


def _constants():
    import numpy as np
    bf = mybir.dt.np(BF16)

    def parts(v):
        v = np.asarray(v, np.float32)
        p0 = v.astype(bf)
        p1 = (v - p0.astype(np.float32)).astype(bf)
        return [p0, p1, (v - p0.astype(np.float32) - p1.astype(np.float32)).astype(bf)]

    ident = np.eye(P, dtype=np.float32)
    masku = np.where(np.arange(P)[None, :] > np.arange(P)[:, None], -1e30, 0.0).astype(np.float32)
    start = 2.0 ** (-2.0 ** (-(np.log2(H0) - 3)))
    slopes = np.array([start ** (i + 1) for i in range(H0)], dtype=np.float32)
    inner = (np.arange(S) % P).astype(np.float32)
    qaux = np.zeros((K_ROWS - AUX, H0, S), bf)
    for i, p in enumerate(parts(slopes)):
        qaux[i] = p[:, None]
        qaux[3 + i] = p[:, None]
    for i, p in enumerate(parts(-slopes[:, None] * inner[None, :])):
        qaux[6 + i] = p
    kaux = np.zeros((T_ROWS - AUX, tri(ST)), bf)
    for t in range(ST):
        k = np.arange((t + 1) * P)
        kaux[0:3, tri(t):tri(t + 1)] = (P * (k // P - t)).astype(bf)
        kaux[3:6, tri(t):tri(t + 1)] = (k % P).astype(bf)
        kaux[6:, tri(t):tri(t + 1)] = 1.0
    inv_freq = (1.0 / 10000.0 ** (np.arange(0, HD1, 2, dtype=np.float32) / np.float32(HD1))).astype(np.float32)
    angle = np.arange(S, dtype=np.float32)[None, :] * np.concatenate([inv_freq, inv_freq])[:, None]
    cos, sin = np.cos(angle).astype(np.float32), np.sin(angle).astype(np.float32)
    sin[HD1 // 2:] *= -1.0
    pos = np.arange(P)
    key_scale = np.where(pos < 35, 0.5, np.where(pos < 35 + 72, 1.5, 1.0)).astype(np.float32)
    kscale = np.tile(key_scale[None, :], (P, 1))
    tscale = np.where(pos[:, None] >= 35 + 72, key_scale[None, :], 1.0).astype(np.float32)
    return {"cos": cos, "sin": sin, "kscale": kscale, "tscale": tscale, "identf": ident, "identb": ident.astype(bf), "masku": masku.astype(bf), "qaux": qaux, "kaux": kaux}


def kernel(**inputs):
    import numpy as np
    import concourse.bacc as _bacc
    from concourse.bass_utils import run_bass_kernel_spmd as _run

    nc = _bacc.Bacc("TRN2", target_bir_lowering=False, num_devices=1)
    host = {k: np.asarray(v) for k, v in inputs.items()}
    laid = {
        "x": host["L0_attn_hidden_states"].reshape(S, D),
        "wq0": host["L0_attn_Wq"], "wkv0": host["L0_attn_Wkv"], "wo0": host["L0_attn_Wo"],
        "qw": host["L0_ffn_qweight"], "lut4": host["L0_ffn_lut4"], "lut8": host["L0_ffn_lut8"], "bias": host["L0_ffn_bias"],
    }
    wq, wk, wv = (host[f"L1_attn_w{n}"] for n in "qkv")
    def chunks(w, heads):
        return w.reshape(KV1, heads, HD1, DT, P).transpose(0, 1, 4, 3, 2).reshape(KV1, heads, P, BLK)

    laid["w1"] = np.concatenate([chunks(wk, 1), chunks(wv, 1), chunks(wq, G1)], axis=1)
    laid["wo1"] = host["L1_attn_wo"].T.reshape(KV1, G1, HD1, D)
    cut = (FT - 1) * P
    for name in ("gate", "up"):
        w = host[f"L1_ffn_{name}_w"]
        laid[name + "_main"] = w[:cut].reshape(FT - 1, P, DT, P).transpose(0, 3, 2, 1).reshape(FT - 1, P, BLK)
        laid[name + "_last"] = w[cut:].reshape(FLAST, DT, P).transpose(2, 1, 0).reshape(P, DT * FLAST)
    down = host["L1_ffn_down_w"].T
    laid["down_main"], laid["down_last"] = down[:cut].reshape(FT - 1, P, D), down[cut:]
    for name in ("gate", "up", "down"):
        laid[name + "_a"], laid[name + "_b"] = host[f"L1_ffn_{name}_a"].T, host[f"L1_ffn_{name}_b"].T
    laid.update(_constants())
    arrays, aps = {}, {}
    for name, v in laid.items():
        v = np.ascontiguousarray(v)
        arrays[f"in_{name}"] = v
        aps[name] = nc.dram_tensor(f"in_{name}", v.shape, mybir.dt.from_np(v.dtype), kind="ExternalInput").ap()
    aps["out"] = nc.dram_tensor("out_0", (S, D), F32, kind="ExternalOutput").ap()
    build(nc, aps)
    r = _run(nc, [arrays], core_ids=[0])
    return r.results[0]["out_0"].reshape(1, S, D)
```

```python
from contextlib import ExitStack

import concourse.bass as bass
from concourse import mybir

ALU = mybir.AluOpType
ACT = mybir.ActivationFunctionType
AX = mybir.AxisListType
F32 = mybir.dt.float32
F32R = mybir.dt.float32r
BF16 = mybir.dt.bfloat16
I32 = mybir.dt.int32

P = 128
S, D = 1024, 512
ST, DT, BLK = S // P, D // P, 512
NB = S // BLK
EPS = 1e-5

H0, HD0 = 32, 16
HG0 = H0 // 4
K_ROWS, T_ROWS, AUX = 121, 124, 112
QPARTS = (0, 1, 0, 1, 0, 1, 2)
KPARTS = (0, 0, 1, 1, 2, 2, 0)
PT0 = 2
CODES_AT = (0, 0, 1, 1, 2, 2, 5, 5)
NPLANE, WORDS, CODES_L, CODES_H = 8, 16, 16, 256
CUT = D * (D // P) // HG0
EST_T = 64.0

H1, KV1, HD1 = 32, 8, 128
G1 = H1 // KV1
FH, RANK = 1376, 16


class Count:

    def __init__(self, sem):
        self.sem, self.n = sem, 0

    def inc(self, ins, by=1):
        ins.then_inc(self.sem, by)
        self.n += by
        return self.n


def products(pe, out, left, right, first, last):
    (lh, ll), (rh, rl) = left, right
    pe.matmul(out, lh, rh, start=first, stop=False)
    pe.matmul(out, lh, rl, start=False, stop=False)
    return pe.matmul(out, ll, rh, start=False, stop=last)


def build(nc, a):
    ctx = ExitStack()
    with ctx:
        def sb(name, shape, dt):
            return ctx.enter_context(nc.sbuf_tensor(name, shape, dt))

        keep = {
            "resid": sb("resid", [P, ST, D], F32),
            "xth": sb("xth", [P, DT, S], F32R),
            "xtl": sb("xtl", [P, DT, S], F32R),
            "identf": sb("identf", [P, P], F32),
            "identb": sb("identb", [P, P], BF16),
            "masku": sb("masku", [P, P], BF16),
        }
        layer0(nc, a, keep)
        layer1(nc, a, keep)
        gated(nc, a, keep)



class Norm:

    def __init__(self, nc, ctx, keep, name, xn, bank):
        def sb(n, shape, dt=F32):
            return ctx.enter_context(nc.sbuf_tensor(name + n, shape, dt))

        def sem(n):
            return ctx.enter_context(nc.semaphore(name + n))

        self.x, self.xn, self.bank = keep["resid"], xn, bank
        self.xth, self.xtl, self.identf = keep["xth"], keep["xtl"], keep["identf"]
        self.stats, self.mv = sb("stats", [P, ST, 6]), sb("mv", [P, ST, 2])
        self.veps, self.sd, self.r = sb("veps", [P, ST]), sb("sd", [P, ST]), sb("r", [P, ST])
        self.t, self.rstd = sb("t", [P, ST]), self.r
        self.step = sem("norm_step")
        self.veps_ready, self.sd_ready = sem("veps_ready"), sem("sd_ready")
        self.xn_ready, self.turned = sem("xn_ready"), sem("turned")
        self.high_ready, self.low_ready = sem("high_ready"), sem("low_ready")

    def vector(self, nc, dve, arrived):
        step = Count(self.step)
        for st in range(ST):
            arrived(dve, st)
            n = step.inc(nc.vector.bn_stats(self.stats[:, st, :], self.x[:, st, :]))
        for st in range(ST):
            dve.wait_ge(self.step, st + 1)
            n = step.inc(nc.vector.bn_aggr(self.mv[:, st, :], self.stats[:, st, :]))
        dve.wait_ge(self.step, n)
        nc.vector.tensor_scalar(self.veps[:], self.mv[:, :, 1], EPS, None, ALU.add).then_inc(self.veps_ready, 1)
        dve.wait_ge(self.sd_ready, 1)
        n = step.inc(nc.vector.reciprocal(self.r[:], self.sd[:]))
        dve.wait_ge(self.step, n)
        n = step.inc(nc.vector.tensor_tensor(self.t[:], self.r[:], self.r[:], ALU.mult))
        dve.wait_ge(self.step, n)
        n = step.inc(nc.vector.tensor_tensor(self.t[:], self.t[:], self.veps[:], ALU.mult))
        dve.wait_ge(self.step, n)
        n = step.inc(nc.vector.tensor_scalar(self.t[:], self.t[:], -0.5, 1.5, ALU.mult, ALU.add))
        dve.wait_ge(self.step, n)
        n = step.inc(nc.vector.tensor_tensor(self.rstd[:], self.r[:], self.t[:], ALU.mult))
        dve.wait_ge(self.step, n)

        def low(st):
            dve.wait_ge(self.turned, st + 1)
            dve.wait_ge(self.high_ready, st + 1)
            nc.vector.tensor_tensor(self.xtl[:, :, st * P:(st + 1) * P], self.bank(st).rearrange("p (c s) -> p c s", c=DT),
                                    self.xth[:, :, st * P:(st + 1) * P].bitcast(F32), ALU.subtract).then_inc(self.low_ready, 1)

        for st in range(ST):
            nc.vector.tensor_scalar(self.xn[:, st, :], self.x[:, st, :], self.mv[:, st, 0:1], self.rstd[:, st:st + 1],
                                    ALU.subtract, ALU.mult).then_inc(self.xn_ready, 1)
            if st >= 2:
                low(st - 2)
        low(ST - 2)
        low(ST - 1)

    def tensor(self, nc, pe):
        for st in range(ST):
            pe.wait_ge(self.xn_ready, st + 1)
            for c in range(DT):
                last = nc.tensor.transpose(self.bank(st)[:, c * P:(c + 1) * P], self.xn[:, st, c * P:(c + 1) * P], self.identf[:])
            last.then_inc(self.turned, 1)

    def scalar_sqrt(self, nc, act):
        act.wait_ge(self.veps_ready, 1)
        nc.scalar.activation(self.sd[:], self.veps[:], ACT.Sqrt).then_inc(self.sd_ready, 1)

    def scalar_high(self, nc, act):
        for st in range(ST):
            act.wait_ge(self.turned, st + 1)
            nc.scalar.activation(self.xth[:, :, st * P:(st + 1) * P], self.bank(st).rearrange("p (c s) -> p c s", c=DT),
                                 ACT.Copy).then_inc(self.high_ready, 1)



def tri(t):
    return P * t * (t + 1) // 2


def interleave(main, side):
    out, at = [], 0
    for i, step in enumerate(main):
        out.append(step)
        want = (i + 1) * len(side) // len(main)
        out += side[at:want]
        at = want
    return out


def layer0(nc, a, keep):
    ctx = ExitStack()
    with ctx:
        def sb(name, shape, dt=F32):
            return ctx.enter_context(nc.sbuf_tensor(name, shape, dt))

        def sem(name):
            return ctx.enter_context(nc.semaphore(name))

        resid, xth, xtl = keep["resid"], keep["xth"], keep["xtl"]
        identf, identb, masku = keep["identf"], keep["identb"], keep["masku"]
        ps = ctx.enter_context(nc.psum_tensor("ps0", [P, 8, 512], F32))

        def bank(b):
            return ps[:, b % 8, :]

        xn = sb("xn0", [P, ST, D])
        bits = xn[:, 0:DT, :].rearrange("p c n -> p (c n)").bitcast(I32)
        woraw = xn[:, DT:2 * DT, :]
        norm = Norm(nc, ctx, keep, "l0_", xn, bank)
        esq, enorm, maskf, masks = sb("esq", [P, ST]), sb("enorm", [P, ST]), sb("maskf", [P, 1]), sb("masks", [P, ST], I32)
        flag = sb("flag", [1, 1], I32)
        credit = sb("credit", [1, 1])
        qstack = sb("qstack", [P, H0, S], BF16)
        kstack = sb("kstack", [P, tri(ST)], BF16)
        wqh, wql = sb("wqh", [P, DT, D], F32R), sb("wql", [P, DT, D], F32R)
        wlh, wll = wqh, wql
        wl = sb("wl", [P, DT, D])
        vaug = sb("vaug", [P, ST, 32])
        negm = sb("negm", [P, 2, H0])
        mrows, mrest = sb("mrows", [H0, 3, P], BF16), sb("mrest", [H0, P])
        acc_sb, rden = sb("acc_sb", [P, P]), sb("rden", [P, 4])
        biasb = sb("biasb", [P, D])
        qw = sb("qw", [P, NPLANE, DT, WORDS], I32)
        lutl = sb("lutl", [P, DT, CODES_L])
        idx = sb("idx", [P, DT * D], BF16)
        onehot = sb("onehot", [P, 2, CUT])
        lut2 = sb("lut2", [P, CODES_L, HG0])
        with ExitStack() as early:
            def sbe(name, shape, dt=F32):
                return early.enter_context(nc.sbuf_tensor(name, shape, dt))
            wkv = sbe("wkv", [P, DT, 2 * HD0])
            wvh, wvl = sbe("wvh", [P, DT, HD0], F32R), sbe("wvl", [P, DT, HD0], F32R)
            wkh, wkl = sbe("wkh", [P, DT, P], F32R), sbe("wkl", [P, DT, P], F32R)
            rest = sbe("rest", [P, 2, BLK])
            parts_sb = [sbe(f"part{i}", [P, 2, S], BF16) for i in range(3)]
            sel = sbe("sel", [P, 8, 3, AUX], BF16)
        with ExitStack() as late:
            def sbl(name, shape, dt=F32):
                return late.enter_context(nc.sbuf_tensor(name, shape, dt))
            woh, wol = sbl("woh", [P, DT, D], F32R), sbl("wol", [P, DT, D], F32R)
            atth, attl = sbl("atth", [P, 2, DT, P], F32R), sbl("attl", [P, 2, DT, P], F32R)
            pt = sbl("pt0", [P, PT0, BLK])
        luth = qstack[:, 0:2, :].rearrange("p h s -> p (h s)").bitcast(F32).rearrange("p (c k) -> p c k", c=DT)
        with ExitStack() as rare:
            ridx = rare.enter_context(nc.sbuf_tensor("ridx", [P, DT * D], F32))
            rbits = rare.enter_context(nc.sbuf_tensor("rbits", [P, DT * D], I32))
            rhot = rare.enter_context(nc.sbuf_tensor("rhot", [P, D], F32))
            rsum = rare.enter_context(nc.sbuf_tensor("rsum", [P, D], F32))

        x_in = [sem(f"x_in{i}") for i in range(4)]
        const_in, wkv_in, wq_in, wo_in = sem("const_in"), sem("wkv_in"), sem("wq_in"), sem("wo_in")
        aux_in, qw_in, lut_in, bias_in = sem("aux_in"), sem("qw_in"), sem("lut_in"), sem("bias_in")
        esq_ready, mask_ready = sem("esq_ready"), sem("mask_ready")
        wk_high, wk_low, wq_high, wq_low, wo_high, wo_low = (sem(n) for n in ("wk_high", "wk_low", "wq_high", "wq_low", "wo_high", "wo_low"))
        k_ps, v_ps, q_ps = sem("k_ps"), sem("v_ps"), sem("q_ps")
        kq_part = [sem(f"kq_part{i}") for i in range(3)]
        kq_rest = sem("kq_rest")
        v_ready, v_init = sem("v_ready"), sem("v_init")
        sel_in, lut2_made, k_placed = sem("sel_in"), sem("lut2_made"), sem("k_placed")
        place_filled, placed = sem("place_filled"), [sem("placed_act"), sem("placed_dve")]
        m_filled, m_free = sem("m_filled"), sem("m_free")
        m_turned, m_split, m_rows = sem("m_turned"), sem("m_split"), sem("m_rows")
        t_filled, exp_done, av_done = sem("t_filled"), sem("exp_done"), sem("av_done")
        acc_ready, acc_copied, acc_turned, norm_step, head_done = (
            sem(n) for n in ("acc_ready", "acc_copied", "acc_turned", "norm_step", "head_done"))
        bit_step, idx_step, hot_made, wl_step, waited = (sem(n) for n in ("bit_step", "idx_step", "hot_made", "wl_step", "waited0"))
        wl_turned, wl_high, wl_low = sem("wl_turned"), sem("wl_high"), sem("wl_low")
        att_turned, att_high, att_low = sem("att_turned"), sem("att_high"), sem("att_low")
        o_ps, y_ps, xb_ready, t_ready, x1_ready = (sem(n) for n in ("o_ps", "y_ps", "xb_ready", "t_ready", "x1_ready"))
        any_turned, any_step, flag_ready = sem("any_turned"), sem("any_step"), sem("flag_ready")
        rare_step, rare_w, rare_turned, rare_split, rare_y, rare_used = (
            sem(n) for n in ("rare_step", "rare_w", "rare_turned", "rare_split", "rare_y", "rare_used"))
        luth_in = sem("luth_in")

        block = ctx.enter_context(nc.Block())

        K_PLACES = 4 + ST - 1
        QT_PLACES = 8 * NB
        TB = (4, 5)
        ACCB, TURNB = 6, 7

        def parts_free(eng, n):
            if n // NB == 1:
                eng.wait_ge(k_placed, K_PLACES)
            elif n // NB >= 2:
                eng.wait_ge(place_filled, QT_PLACES * (n // NB - 1))

        def q_bank(n):
            return ps[:, 3 + n % 4, :]

        def place_bank(i):
            return ps[0:AUX, (7, 0, 1, 2)[i % 4], :]

        def all_placed(eng):
            for sem_placed in placed:
                eng.wait_ge(sem_placed, QT_PLACES * 4 // 2)

        def unit(t, hg, kt):
            return hg * (t + 1) + (HG0 * t * (t + 1) // 2 + kt)

        def parity(t, hg, kt, odd):
            return (odd * (t + 1) + kt) % 2

        def groups(eng, t, step):
            step(t, 0, 0, (t, 1, 1))
            with eng.Fori(0, HG0 // 2 - 1) as pair:
                hg = pair * 2 + 1
                step(t, hg, 1, (t, pair * 2 + 2, 0))
                step(t, pair * 2 + 2, 0, (t, pair * 2 + 3, 1))
            step(t, HG0 - 1, 1, (t + 1, 0, 0) if t + 1 < ST else None)

        @block.sync
        def _(sp):
            for i in range(4):
                sp.dma_start(resid[:, 2 * i:2 * i + 2, :], a["x"].rearrange("(t p) d -> p t d", p=P)[:, 2 * i:2 * i + 2, :]).then_inc(x_in[i], 16)
            sp.dma_start(identf[:], a["identf"]).then_inc(const_in, 16)
            sp.dma_start(identb[:], a["identb"]).then_inc(const_in, 16)
            sp.dma_start(masku[:], a["masku"]).then_inc(const_in, 16)
            sp.dma_start(wkv[:], a["wkv0"].rearrange("(c p) n -> p c n", p=P)).then_inc(wkv_in, 16)
            sp.dma_start(wl[:], a["wq0"].rearrange("(c p) n -> p c n", p=P)).then_inc(wq_in, 16)
            sp.dma_start(qw[:], a["qw"].rearrange("l (c p) w -> p l c w", p=P)).then_inc(qw_in, 16)
            sp.dma_start(lutl[:], a["lut4"].rearrange("(c p) k -> p c k", p=P)).then_inc(lut_in, 16)
            sp.dma_start(sel[:], a["sel"]).then_inc(sel_in, 16)
            sp.dma_start(qstack[AUX:K_ROWS, :, :], a["qaux"]).then_inc(aux_in, 16)
            sp.dma_start(kstack[AUX:T_ROWS, :], a["kaux"]).then_inc(aux_in, 16)
            sp.dma_start(biasb[:], a["bias"].partition_broadcast(P)).then_inc(bias_in, 16)
            sp.wait_ge(norm.turned, ST)
            sp.wait_ge(esq_ready, ST)
            sp.dma_start(woraw, a["wo0"].rearrange("(c p) n -> p c n", p=P)).then_inc(wo_in, 16)
            for t in range(ST):
                sp.wait_ge(m_split, 3 * t + 3)
                if t:
                    sp.wait_ge(m_rows, 48 * t)
                for i in range(3):
                    sp.dma_start(qstack[K_ROWS + i:K_ROWS + i + 1, :, t * P:(t + 1) * P], mrows[:, i, :]).then_inc(m_rows, 16)
            sp.wait_ge(head_done, HG0 * ST + 1)
            sp.dma_start(luth, a["lut8"].rearrange("(c p) k -> p c k", p=P)).then_inc(luth_in, 16)
            sp.wait_ge(luth_in, 16)

        @block.tensor
        def _(pe):
            pe.wait_ge(const_in, 48)
            norm.tensor(nc, pe)

            pe.wait_ge(wk_low, 2)
            for b in range(NB):
                pe.wait_ge(norm.low_ready, ST // NB * (b + 1))
                for c in range(DT):
                    last = products(pe, bank(b), (wkh[:, c, :], wkl[:, c, :]),
                                    (xth[:, c, b * BLK:(b + 1) * BLK], xtl[:, c, b * BLK:(b + 1) * BLK]), c == 0, c == DT - 1)
                last.then_inc(k_ps, 1)
            for st in range(ST):
                for c in range(DT):
                    last = products(pe, ps[:, 2, st * HD0:(st + 1) * HD0],
                                    (xth[:, c, st * P:(st + 1) * P], xtl[:, c, st * P:(st + 1) * P]),
                                    (wvh[:, c, :], wvl[:, c, :]), c == 0, c == DT - 1)
            last.then_inc(v_ps, 1)
            pe.wait_ge(wq_low, DT)
            def project_q(qt):
                for n in (NB * qt, NB * qt + 1):
                    b = n % NB
                    if n >= 4:
                        pe.wait_ge(kq_rest, NB + n - 3)
                    for c in range(DT):
                        last = products(pe, q_bank(n), (wqh[:, c, qt * P:(qt + 1) * P], wql[:, c, qt * P:(qt + 1) * P]),
                                        (xth[:, c, b * BLK:(b + 1) * BLK], xtl[:, c, b * BLK:(b + 1) * BLK]), c == 0, c == DT - 1)
                    last.then_inc(q_ps, 1)

            def place_q(qt):
                for i in range(3):
                    pe.wait_ge(kq_part[i], NB + NB * (qt + 1))
                for h in range(8):
                    for b in range(NB):
                        i = QT_PLACES * qt + NB * h + b
                        if i == 1:
                            pe.wait_ge(kq_rest, NB)
                        if i == 3:
                            pe.wait_ge(v_ready, 1)
                        if i >= 4:
                            pe.wait_ge(placed[b], (i - 4) // NB + 1)
                        for part in range(3):
                            last = pe.matmul(place_bank(i), sel[:, h, part, :], parts_sb[part][:, (qt + 1) % 2, b * BLK:(b + 1) * BLK],
                                             start=part == 0, stop=part == 2)
                        last.then_inc(place_filled, 1)

            project_q(0)
            pe.wait_ge(sel_in, 16)
            for qt in range(4):
                if qt < 3:
                    project_q(qt + 1)
                place_q(qt)

            pe.wait_ge(mask_ready, 1)
            pe.wait_ge(kq_rest, NB + 4 * NB)
            nc.tensor.transpose(ps[0:1, 4, 0:P], maskf[:], identf[:]).then_inc(any_turned, 1)

            def m_scores(t, h, slot):
                pe.wait_ge(m_free, t * H0 + h + 1)
                width = (t + 1) * P
                for c0 in range(0, width, 512):
                    w = min(512, width - c0)
                    diag = c0 + w == width
                    pe.matmul(ps[:, 2 * slot + c0 // 512, 0:w], qstack[0:K_ROWS, h, t * P:(t + 1) * P],
                              kstack[0:K_ROWS, tri(t) + c0:tri(t) + c0 + w], start=True, stop=not diag)
                d = t * P
                last = pe.matmul(ps[:, 2 * slot + d // 512, d % 512:d % 512 + P], identb[:], masku[:], start=False, stop=True)
                last.then_inc(m_filled, 1)

            def m_turn(t):
                pe.wait_ge(m_free, H0 * (t + 1) + 2)
                if t:
                    pe.wait_ge(m_split, 3 * t)
                if t >= 2:
                    pe.wait_ge(head_done, HG0 * (t - 1))
                nc.tensor.transpose(ps[0:H0, TURNB, 0:P], negm[:, t % 2, :], identf[:]).then_inc(m_turned, 1)

            def t_scores(t, hg, kt, odd):
                n = unit(t, hg, kt)
                if not (isinstance(n, int) and n < 2):
                    pe.wait_ge(exp_done, n - 1)
                if t and isinstance(hg, int) and hg == 0 and kt == 0:
                    pe.wait_ge(m_rows, 48 * (t + 1))
                out = ps[:, TB[parity(t, hg, kt, odd)], :].rearrange("p (h q) -> p h q", h=4)
                q = qstack[0:T_ROWS, bass.ds(hg * 4, 4), t * P:(t + 1) * P]
                last = pe.matmul(out, kstack[0:T_ROWS, tri(t) + kt * P:tri(t) + (kt + 1) * P], q, start=True, stop=kt != t)
                if kt == t:
                    last = pe.matmul(out, masku[:],
                                     identb[:].unsqueeze(1).to_broadcast([P, 4, P]), start=False, stop=True)
                last.then_inc(t_filled, 1)

            def values(t, hg, kt, odd):
                if kt == 0 and not (t == 0 and isinstance(hg, int) and hg == 0):
                    pe.wait_ge(acc_copied, hg + HG0 * t)
                pe.wait_ge(exp_done, unit(t, hg, kt + 1))
                for j in range(4):
                    last = pe.matmul(ps[32 * j:32 * j + 32, ACCB, 0:P], vaug[:, kt, :],
                                     pt[:, parity(t, hg, kt, odd), j * P:(j + 1) * P], start=kt == 0, stop=kt == t)
                last.then_inc(av_done, 1)

            def unit_group(t, hg, odd, following):
                head = isinstance(hg, int) and hg == 0
                ahead = [lambda k=k: t_scores(t, hg, k, odd) for k in range(2, t + 1)]
                if following:
                    nt, nhg, nodd = following
                    ahead += [lambda k=k: t_scores(nt, nhg, k, nodd) for k in range(min(2, nt + 1))]
                main = []
                for k in range(t + 1):
                    if k == t and following:
                        main.append(ahead.pop(0))
                    main.append(lambda k=k: values(t, hg, k, odd))
                    if ahead and (k < t - 1 or k == t):
                        main.append(ahead.pop(0))
                side = [lambda j=j: m_scores(t + 2, hg * 4 + j, j % 2) for j in range(4)] if t + 2 < ST else []
                turned_here = head and 2 <= t + 1 < ST
                if turned_here:
                    side.insert(min(2, len(side)), lambda: m_turn(t + 1))
                steps, at = [], 0
                for i, s in enumerate(main):
                    while at < len(side) and at * len(main) // len(side) <= i:
                        steps.append(side[at])
                        at += 1
                    steps.append(s)
                if not (t == 0 and head):
                    after = steps.index(side[min(2, len(side) - 1)]) + 1 if turned_here else 3
                    steps.insert(min(after, len(steps) - 1), lambda: turn(t, hg))
                for step in steps:
                    step()

            def turn(t, hg):
                u = hg + (HG0 * t - 1)
                pe.wait_ge(acc_copied, u + 1)
                if not (isinstance(u, int) and u == 0):
                    pe.wait_ge(head_done, u + 1)
                pe.wait_ge(m_split, 3 * min(t + 2, ST))
                nc.tensor.transpose(ps[:, TURNB, 0:P], acc_sb[:], identf[:]).then_inc(acc_turned, 1)

            pe.wait_ge(aux_in, 32)
            pe.wait_ge(k_placed, K_PLACES)
            all_placed(pe)
            for t in range(2):
                with pe.Fori(0, HG0) as hg:
                    for j in range(4):
                        m_scores(t, hg * 4 + j, j % 2)
                m_turn(t)
            pe.wait_ge(v_ready, 1)
            pe.wait_ge(flag_ready, 1)
            pe.wait_ge(m_rows, 48)
            t_scores(0, 0, 0, 0)
            for t in range(ST):
                groups(pe, t, unit_group)
            turn(ST, 0)

            pe.wait_ge(wl_step, 1 + CODES_L * HG0)
            for ot in range(DT):
                for c in range(DT):
                    last = nc.tensor.transpose(ps[:, c, ot * P:(ot + 1) * P], wl[:, ot, c * P:(c + 1) * P], identf[:])
            last.then_inc(wl_turned, 1)

            pe.wait_ge(wo_low, DT)
            pe.wait_ge(wl_low, DT)

            def turn_att(t):
                pe.wait_ge(head_done, HG0 * ST + 1)
                if t >= 2:
                    pe.wait_ge(att_low, t - 1)
                for c in range(DT):
                    last = nc.tensor.transpose(ps[:, t % 2, c * P:(c + 1) * P], xn[:, t, c * P:(c + 1) * P], identf[:])
                last.then_inc(att_turned, 1)

            turn_att(0)
            for t in range(ST):
                if t >= 2:
                    pe.wait_ge(x1_ready, t - 1)
                for c in range(DT):
                    last = products(pe, ps[:, 2 + t % 2, :], (xth[:, c, t * P:(t + 1) * P], xtl[:, c, t * P:(t + 1) * P]),
                                    (wlh[:, c, :], wll[:, c, :]), c == 0, c == DT - 1)
                last.then_inc(y_ps, 1)
                if t + 1 < ST:
                    turn_att(t + 1)
                pe.wait_ge(att_low, t + 1)
                for c in range(DT):
                    last = products(pe, ps[:, 4 + t % 2, :], (atth[:, t % 2, c, :], attl[:, t % 2, c, :]),
                                    (woh[:, c, :], wol[:, c, :]), c == 0, c == DT - 1)
                last.then_inc(o_ps, 1)

            some = pe.value_load(flag[0:1, 0:1], min_val=0, max_val=1)
            with pe.If(some > 0):
                pe.wait_ge(rare_w, 1)
                for ot in range(DT):
                    for c in range(DT):
                        last = nc.tensor.transpose(ps[:, c, ot * P:(ot + 1) * P], wl[:, ot, c * P:(c + 1) * P], identf[:])
                last.then_inc(rare_turned, 1)
                pe.wait_ge(rare_split, 2 * DT)
                for t in range(ST):
                    if t >= 2:
                        pe.wait_ge(rare_used, 2 * t - 2)
                    for c in range(DT):
                        last = products(pe, ps[:, 6 + t % 2, :], (xth[:, c, t * P:(t + 1) * P], xtl[:, c, t * P:(t + 1) * P]),
                                        (wlh[:, c, :], wll[:, c, :]), c == 0, c == DT - 1)
                    last.then_inc(rare_y, 1)

        @block.scalar
        def _(act):
            norm.scalar_sqrt(nc, act)
            act.wait_ge(wkv_in, 16)
            nc.scalar.activation(wkh[:].rearrange("p c (r d) -> p c r d", r=8),
                                 wkv[:, :, 0:HD0].unsqueeze(2).to_broadcast([P, DT, 8, HD0]), ACT.Copy).then_inc(wk_high, 1)
            nc.scalar.activation(wvh[:], wkv[:, :, HD0:2 * HD0], ACT.Copy).then_inc(wk_high, 1)
            act.wait_ge(wq_in, 16)
            for c in range(DT):
                nc.scalar.activation(wqh[:, c, :], wl[:, c, :], ACT.Copy).then_inc(wq_high, 1)
            norm.scalar_high(nc, act)

            for st in range(ST):
                act.wait_ge(norm.xn_ready, st + 1)
                if st:
                    act.wait_ge(esq_ready, st)
                nc.scalar.activation(rest[:, 0, :], xn[:, st, :], ACT.Square, accum_out=esq[:, st:st + 1]).then_inc(esq_ready, 1)
            act.wait_ge(esq_ready, ST)
            nc.scalar.activation(enorm[:], esq[:], ACT.Sqrt).then_inc(esq_ready, 1)

            def two_parts(src, scale, n, out0, out1):
                nc.scalar.activation(out0, src, ACT.Copy, scale=scale).then_inc(kq_part[0], 1)
                act.wait_ge(kq_rest, n + 1)
                nc.scalar.activation(out1, rest[:, n % 2, :], ACT.Copy).then_inc(kq_part[1], 1)

            for b in range(NB):
                act.wait_ge(k_ps, b + 1)
                cols = slice(b * BLK, (b + 1) * BLK)
                two_parts(bank(b), 1.0, b, parts_sb[0][:, 0, cols], parts_sb[1][:, 0, cols])
            act.wait_ge(v_ps, 1)
            act.wait_ge(v_init, 2)
            nc.scalar.activation(vaug[:, :, 0:HD0], ps[:, 2, 0:ST * HD0].rearrange("p (t d) -> p t d", t=ST),
                                 ACT.Copy).then_inc(v_ready, 1)
            def q_parts(qt):
                for n in (NB * qt, NB * qt + 1):
                    act.wait_ge(q_ps, n + 1)
                    cols = slice(n % NB * BLK, (n % NB + 1) * BLK)
                    parts_free(act, n)
                    two_parts(q_bank(n), HD0 ** -0.5, NB + n, parts_sb[0][:, (qt + 1) % 2, cols], parts_sb[1][:, (qt + 1) % 2, cols])

            q_parts(0)
            for qt in range(4):
                if qt < 3:
                    q_parts(qt + 1)
                for h in range(8):
                    i = QT_PLACES * qt + NB * h
                    act.wait_ge(place_filled, i + 1)
                    nc.scalar.activation(qstack[0:AUX, 8 * qt + h, 0:BLK], place_bank(i), ACT.Copy).then_inc(placed[0], 1)

            def exponential(t, hg, kt, odd):
                n = unit(t, hg, kt)
                act.wait_ge(t_filled, n + 1)
                if not (isinstance(n, int) and n < 2):
                    act.wait_ge(av_done, n - 1)
                par = parity(t, hg, kt, odd)
                nc.scalar.activation(pt[:, par, :], ps[:, TB[par], :], ACT.Exp).then_inc(exp_done, 1)

            def unit_group(t, hg, odd, following):
                for k in range(2, t + 1):
                    exponential(t, hg, k, odd)
                if following:
                    nt, nhg, nodd = following
                    exponential(nt, nhg, 0, nodd)
                act.wait_ge(av_done, unit(t, hg, t + 1))
                if not (t == 0 and isinstance(hg, int) and hg == 0):
                    act.wait_ge(acc_turned, hg + HG0 * t)
                nc.scalar.activation(acc_sb[:], ps[:, ACCB, 0:P], ACT.Copy).then_inc(acc_copied, 1)
                if following and nt >= 1:
                    exponential(nt, nhg, 1, nodd)

            all_placed(act)
            exponential(0, 0, 0, 0)
            for t in range(ST):
                groups(act, t, unit_group)
                if t == 1:
                    act.wait_ge(wo_in, 16)
                    for c in range(DT):
                        nc.scalar.activation(woh[:, c, :], woraw[:, c, :], ACT.Copy).then_inc(wo_high, 1)
            act.wait_ge(wl_turned, 1)
            for c in range(DT):
                nc.scalar.activation(wlh[:, c, :], bank(c), ACT.Copy).then_inc(wl_high, 1)
            for t in range(ST):
                act.wait_ge(att_turned, t + 1)
                if t >= 2:
                    act.wait_ge(o_ps, t - 1)
                nc.scalar.activation(atth[:, t % 2, :, :], bank(t % 2).rearrange("p (c s) -> p c s", c=DT), ACT.Copy).then_inc(att_high, 1)

        @block.vector
        def _(dve):
            dve.sem_inc(head_done, 1)
            nc.vector.memset(vaug[:], 0.0).then_inc(v_init, 1)
            dve.wait_ge(v_init, 1)
            nc.vector.memset(vaug[:, :, HD0:HD0 + 1], 1.0).then_inc(v_init, 1)
            nc.vector.memset(credit[:, 0:1], 0.0).then_inc(m_free, 2)
            norm.vector(nc, dve, lambda e, st: e.wait_ge(x_in[st // 2], 16))
            dve.wait_ge(wk_high, 2)
            nc.vector.tensor_tensor(wkl[:].rearrange("p c (r d) -> p c r d", r=8),
                                    wkv[:, :, 0:HD0].unsqueeze(2).to_broadcast([P, DT, 8, HD0]),
                                    wkh[:].bitcast(F32).rearrange("p c (r d) -> p c r d", r=8), ALU.subtract).then_inc(wk_low, 1)
            nc.vector.tensor_tensor(wvl[:], wkv[:, :, HD0:2 * HD0], wvh[:].bitcast(F32), ALU.subtract).then_inc(wk_low, 1)

            def parts(src, scale, n, part0, part1, part2):
                dve.wait_ge(kq_part[0], n + 1)
                if n >= 2:
                    dve.wait_ge(kq_part[2], n - 1)
                nc.vector.scalar_tensor_tensor(out=rest[:, n % 2, :], in0=src, scalar=scale, in1=part0,
                                               op0=ALU.mult, op1=ALU.subtract).then_inc(kq_rest, 1)
                dve.wait_ge(kq_rest, n + 1)
                dve.wait_ge(kq_part[1], n + 1)
                nc.vector.tensor_tensor(part2, rest[:, n % 2, :], part1, ALU.subtract).then_inc(kq_part[2], 1)

            def take_bits(level, js):
                for j in js:
                    nc.vector.tensor_scalar(bits[:, j:DT * D:32], qw[:, level, :, :].rearrange("p c w -> p (c w)"),
                                            j, 1, ALU.logical_shift_right, ALU.bitwise_and).then_inc(bit_step, 1)

            def add_plane(level):
                dve.wait_ge(bit_step, 32 * (level + 1))
                if level == 0:
                    nc.vector.tensor_copy(idx[:], bits).then_inc(idx_step, 1)
                else:
                    nc.vector.scalar_tensor_tensor(out=idx[:], in0=bits, scalar=float(1 << level),
                                                   in1=idx[:], op0=ALU.mult, op1=ALU.add).then_inc(idx_step, 1)
                dve.wait_ge(idx_step, level + 1)

            dve.wait_ge(qw_in, 16)
            dve.wait_ge(norm.turned, ST)
            dve.wait_ge(esq_ready, ST)
            take_bits(0, range(32))
            add_plane(0)
            for b in range(NB):
                dve.wait_ge(k_ps, b + 1)
                cols = slice(b * BLK, (b + 1) * BLK)
                parts(bank(b), 1.0, b, *(part[:, 0, cols] for part in parts_sb))
            for i in range(3):
                dve.wait_ge(kq_part[i], NB)
            whole = tri(ST - 1)
            for part, lo, hi in ((0, 0, 32), (1, 32, 64), (2, 64, 96), (0, 96, 112)):
                nc.vector.tensor_copy(kstack[lo:hi, whole:whole + S], parts_sb[part][lo:hi, 0, :]).then_inc(k_placed, 1)
            dve.wait_ge(k_placed, 4)
            for t in range(ST - 1):
                nc.vector.tensor_copy(kstack[0:AUX, tri(t):tri(t + 1)], kstack[0:AUX, whole:whole + (t + 1) * P]).then_inc(k_placed, 1)

            def q_parts(qt):
                for n in (NB * qt, NB * qt + 1):
                    dve.wait_ge(q_ps, n + 1)
                    cols = slice(n % NB * BLK, (n % NB + 1) * BLK)
                    parts_free(dve, n)
                    parts(q_bank(n), HD0 ** -0.5, NB + n, *(part[:, (qt + 1) % 2, cols] for part in parts_sb))

            q_parts(0)
            for qt in range(4):
                if qt < 3:
                    q_parts(qt + 1)
                for h in range(8):
                    i = QT_PLACES * qt + NB * h + 1
                    dve.wait_ge(place_filled, i + 1)
                    nc.vector.tensor_copy(qstack[0:AUX, 8 * qt + h, BLK:S], place_bank(i)).then_inc(placed[1], 1)
                    if qt < 3:
                        take_bits(qt + 1, range(4 * h, 4 * h + 4))
                if qt < 3:
                    add_plane(qt + 1)
            dve.wait_ge(lut_in, 16)
            for half in range(2):
                nc.vector.tensor_copy(lut2[:].rearrange("p c (o i) -> p c o i", i=2)[:, :, :, half], lutl[:].rearrange("p o c -> p c o")).then_inc(lut2_made, 1)
            dve.wait_ge(lut2_made, 2)

            def codes(t, hg):
                n = CODES_AT[t]
                for i in range(n):
                    k = hg * n + (HG0 * sum(CODES_AT[:t]) + i)
                    if not (isinstance(k, int) and k == i):
                        dve.wait_ge(wl_step, k + (1 if i == 0 else 0))
                    c = sum(CODES_AT[:t]) + i
                    part = slice(hg * CUT, (hg + 1) * CUT) if isinstance(hg, int) else bass.ds(hg * CUT, CUT)
                    entry = slice(hg, hg + 1) if isinstance(hg, int) else bass.ds(hg, 1)
                    nc.vector.tensor_scalar(onehot[:, i % 2, :], idx[:, part], float(c), lut2[:, c, entry],
                                            ALU.is_equal, ALU.mult).then_inc(hot_made, 1)

            dve.wait_ge(esq_ready, ST + 1)
            astep = Count(any_step)
            astep.inc(nc.vector.tensor_scalar(masks[:], enorm[:], EST_T, None, ALU.is_gt))
            dve.wait_ge(any_step, 1)
            nc.vector.tensor_reduce(maskf[:], masks[:], AX.X, ALU.max).then_inc(mask_ready, 1)
            dve.wait_ge(any_turned, 1)
            nc.vector.tensor_reduce(flag[:], ps[0:1, 4, 0:P], AX.X, ALU.max).then_inc(flag_ready, 1)

            def head_max(t, h, slot):
                n = h + t * H0
                dve.wait_ge(m_filled, n + 1)
                width = (t + 1) * P
                nc.vector.tensor_reduce(negm[:, t % 2, bass.ds(h, 1)], ps[:, 2 * slot:2 * slot + 2, :].rearrange("p b c -> p (b c)")[:, 0:width],
                                        AX.X, ALU.max, negate=True).then_inc(m_free, 1)

            def maxima(t, hg, js=range(4)):
                for j in js:
                    head_max(t, hg * 4 + j, j % 2)

            def split_max(t):
                dve.wait_ge(m_turned, t + 1)
                if t:
                    dve.wait_ge(m_rows, 48 * t)
                src = ps[0:H0, TURNB, 0:P]
                nc.vector.tensor_copy(mrows[:, 0, :], src).then_inc(m_split, 1)
                dve.wait_ge(m_split, 3 * t + 1)
                nc.vector.tensor_tensor(mrest[:], src, mrows[:, 0, :], ALU.subtract).then_inc(any_step, 1)
                dve.wait_ge(any_step, 2 + t)
                nc.vector.tensor_copy(mrows[:, 1, :], mrest[:]).then_inc(m_split, 1)
                dve.wait_ge(m_split, 3 * t + 2)
                nc.vector.tensor_tensor(mrows[:, 2, :], mrest[:], mrows[:, 1, :], ALU.subtract).then_inc(m_split, 1)

            def normalise(t, hg):
                u = hg + (HG0 * t - 1)
                dve.wait_ge(acc_turned, u + 1)
                src = ps[:, TURNB, 0:P].rearrange("p (h d) -> p h d", h=4)
                nc.vector.reciprocal(rden[:], src[:, :, HD0]).then_inc(norm_step, 1)
                dve.wait_ge(norm_step, u + 1)
                if isinstance(hg, int) and hg == 0:
                    dst = xn[:, t - 1, (H0 - 4) * HD0:H0 * HD0]
                else:
                    dst = xn[:, t, bass.ds(hg * 64 - 64, 64)]
                nc.vector.tensor_tensor(dst.rearrange("p (h d) -> p h d", h=4), src[:, :, 0:HD0],
                                        rden[:].unsqueeze(2).to_broadcast([P, 4, HD0]), ALU.mult).then_inc(head_done, 1)

            for t in range(2):
                with dve.Fori(0, HG0) as hg:
                    maxima(t, hg)
                split_max(t)
            for t in range(ST):
                if t + 2 < ST:
                    maxima(t + 2, 0, (0, 1))
                if 2 <= t + 1 < ST:
                    split_max(t + 1)
                if t + 2 < ST:
                    maxima(t + 2, 0, (2, 3))
                if t:
                    normalise(t, 0)
                if t == DT:
                    dve.wait_ge(wo_low, DT)
                codes(t, 0)
                with dve.Fori(1, HG0) as hg:
                    if t + 2 < ST:
                        maxima(t + 2, hg)
                    normalise(t, hg)
                    codes(t, hg)
            normalise(ST, 0)

            dve.wait_ge(wl_turned, 1)
            for c in range(DT):
                dve.wait_ge(wl_high, c + 1)
                nc.vector.tensor_tensor(wll[:, c, :], bank(c), wlh[:, c, :].bitcast(F32), ALU.subtract).then_inc(wl_low, 1)

            dve.wait_ge(xb_ready, ST)
            for t in range(ST):
                dve.wait_ge(att_turned, t + 1)
                dve.wait_ge(att_high, t + 1)
                if t >= 2:
                    dve.wait_ge(o_ps, t - 1)
                nc.vector.tensor_tensor(attl[:, t % 2, :, :], bank(t % 2).rearrange("p (c s) -> p c s", c=DT),
                                        atth[:, t % 2, :, :].bitcast(F32), ALU.subtract).then_inc(att_low, 1)
                dve.wait_ge(o_ps, t + 1)
                nc.vector.tensor_tensor(xn[:, t, :], ps[:, 4 + t % 2, :], resid[:, t, :], ALU.add).then_inc(t_ready, 1)
                dve.wait_ge(t_ready, t + 1)
                dve.wait_ge(y_ps, t + 1)
                nc.vector.tensor_tensor(resid[:, t, :], ps[:, 2 + t % 2, :], xn[:, t, :], ALU.add).then_inc(x1_ready, 1)

            some = dve.value_load(flag[0:1, 0:1], min_val=0, max_val=1)
            with dve.If(some > 0):
                step = Count(rare_step)
                dve.wait_ge(luth_in, 16)
                dve.wait_ge(x1_ready, ST)

                def chained(ins):
                    dve.wait_ge(rare_step, step.inc(ins))

                for level in range(NPLANE):
                    for j in range(32):
                        n = step.inc(nc.vector.tensor_scalar(rbits[:, j:DT * D:32], qw[:, level, :, :].rearrange("p c w -> p (c w)"),
                                                             j, 1, ALU.logical_shift_right, ALU.bitwise_and))
                    dve.wait_ge(rare_step, n)
                    if level == 0:
                        chained(nc.vector.tensor_copy(ridx[:], rbits[:]))
                    else:
                        chained(nc.vector.scalar_tensor_tensor(out=ridx[:], in0=rbits[:], scalar=float(1 << level),
                                                               in1=ridx[:], op0=ALU.mult, op1=ALU.add))
                chained(nc.vector.memset(wl[:], 0.0))
                base, per = step.n, 2 * DT + 1
                with dve.Fori(0, CODES_H) as c:
                    for ot in range(DT):
                        nc.vector.tensor_scalar(rhot[:], ridx[:, ot * D:(ot + 1) * D], 0.0, luth[:, ot, bass.ds(c, 1)],
                                                ALU.is_equal, ALU.mult).then_inc(rare_step, 1)
                        dve.wait_ge(rare_step, c * per + (base + 2 * ot + 1))
                        nc.vector.tensor_tensor(wl[:, ot, :], wl[:, ot, :], rhot[:], ALU.add).then_inc(rare_step, 1)
                        dve.wait_ge(rare_step, c * per + (base + 2 * ot + 2))
                    nc.vector.tensor_scalar(ridx[:], ridx[:], -1.0, None, ALU.add).then_inc(rare_step, 1)
                    dve.wait_ge(rare_step, c * per + (base + per))
                nc.vector.memset(credit[:], 0.0).then_inc(rare_w, 1)
                dve.wait_ge(rare_turned, 1)
                for c in range(DT):
                    nc.vector.tensor_copy(wlh[:, c, :], bank(c)).then_inc(rare_split, 1)
                    dve.wait_ge(rare_split, 2 * c + 1)
                    nc.vector.tensor_tensor(wll[:, c, :], bank(c), wlh[:, c, :].bitcast(F32), ALU.subtract).then_inc(rare_split, 1)
                for t in range(ST):
                    dve.wait_ge(rare_y, t + 1)
                    if t:
                        dve.wait_ge(rare_used, 2 * t)
                    nc.vector.tensor_tensor(rsum[:], ps[:, 6 + t % 2, :], xn[:, t, :], ALU.add).then_inc(rare_used, 1)
                    dve.wait_ge(rare_used, 2 * t + 1)
                    dve.wait_ge(x1_ready, ST)
                    nc.vector.copy_predicated(resid[:, t, :], masks[:, t:t + 1].to_broadcast([P, D]), rsum[:]).then_inc(rare_used, 1)
                dve.wait_ge(rare_used, 2 * ST)

        @block.gpsimd
        def _(pool):
            for c in range(DT):
                pool.wait_ge(wq_high, c + 1)
                nc.gpsimd.tensor_tensor(wql[:, c, :], wl[:, c, :], wqh[:, c, :].bitcast(F32), ALU.subtract).then_inc(wq_low, 1)
            pool.wait_ge(wq_low, DT)
            nc.gpsimd.memset(wl[:], 0.0).then_inc(wl_step, 1)
            pool.wait_ge(bias_in, 16)
            for st in range(ST):
                pool.wait_ge(norm.xn_ready, st + 1)
                nc.gpsimd.tensor_tensor(resid[:, st, :], resid[:, st, :], biasb[:], ALU.add).then_inc(xb_ready, 1)

            def codes(t, hg):
                n = CODES_AT[t]
                for i in range(n):
                    k = hg * n + (HG0 * sum(CODES_AT[:t]) + i)
                    pool.wait_ge(hot_made, k + 1)
                    pool.wait_ge(wl_step, k + 1)
                    pool.sem_inc(waited, 1)
                    part = slice(hg * CUT, (hg + 1) * CUT) if isinstance(hg, int) else bass.ds(hg * CUT, CUT)
                    flat = wl[:].rearrange("p c n -> p (c n)")
                    nc.gpsimd.tensor_tensor(flat[:, part], flat[:, part], onehot[:, i % 2, :], ALU.add).then_inc(wl_step, 1)

            for t in range(ST):
                if CODES_AT[t]:
                    codes(t, 0)
                    with pool.Fori(1, HG0) as hg:
                        codes(t, hg)
                if t == 2:
                    for c in range(DT):
                        pool.wait_ge(wo_high, c + 1)
                        nc.gpsimd.tensor_tensor(wol[:, c, :], woraw[:, c, :], woh[:, c, :].bitcast(F32), ALU.subtract).then_inc(wo_low, 1)



QUADS = ((7, 0), (6, 1), (5, 2), (4, 3))
PAIRS = [(t, p) for a, b in QUADS for t, p in ((a, 0), (b, 0), (a, 1), (b, 1))]
UNITS = [(j, k) for j, (t, _) in enumerate(PAIRS) for k in range(0, t + 1, 2)]
PT_RING, W_RING, RAW_RING = 4, 3, 2
AHEAD = 3
NPAIR, NUNIT, NHEADS = len(PAIRS), len(UNITS), 2 * len(PAIRS)
NCHUNK, NFILL = 2 + G1, NB * (2 + G1)
ROT_STEPS = 5 + 2 * 9
NTOK = len(PAIRS) // 2


def group_steps(more):
    turns = [("turn", u) for u in range(NUNIT)]
    main = [[] for _ in PAIRS]
    for u, (j, k) in enumerate(UNITS):
        main[j].append(("av", u))
        if u + 2 < NUNIT:
            main[j].append(turns[u + 2])
    out = [("wo", i) for i in range(G1)] + turns[:2]
    for j in range(NPAIR):
        side = []
        if j + AHEAD < NPAIR:
            side += [("qk", 2 * (j + AHEAD)), ("qk", 2 * (j + AHEAD) + 1)]
        q, r = divmod(j, 4)
        if r == 0 and q:
            side.insert(0, ("out", 2 * q - 2))
            side.insert(2, ("out", 2 * q - 1))
        if more and 4 <= j < 4 + W_RING:
            side.append(("w", j - 4))
        if more and j >= NPAIR - 2:
            half = NFILL // 2
            for f in range((j - NPAIR + 2) * half, (j - NPAIR + 3) * half):
                side.append(("proj", f))
                if f % NB == NB - 1 and f // NB + W_RING < NCHUNK:
                    side.append(("w", f // NB + W_RING))
        out += interleave(main[j], side)
    out.append(("out", NTOK - 2))
    if more:
        out += [("vturn", 0), ("vturn", 1)] + [("qknext", n) for n in range(2 * AHEAD)]
    out.append(("out", NTOK - 1))
    return out


def first_steps():
    out = [("w", c) for c in range(W_RING)]
    for f in range(NFILL):
        out.append(("proj", f))
        if f % NB == NB - 1 and f // NB + W_RING < NCHUNK:
            out.append(("w", f // NB + W_RING))
    return out + [("vturn", 0), ("vturn", 1)] + [("qknext", n) for n in range(2 * AHEAD)]


BANK_KINDS = ("turn", "vturn", "out")
SPLIT_FIRST = 2
SPLIT_GROUP = NUNIT + 2


FIRST_TILE = [n for n in range(NHEADS) if PAIRS[n // 2][0] == 0]


class Place:

    def __init__(self, steps):
        self.fill, self.split = {}, {}
        fills = [s for s in steps if s[0] in BANK_KINDS]
        self.fills = fills
        n = 0
        for i, s in enumerate(fills):
            self.fill[s] = i
            if s[0] != "out":
                self.split[s] = n
                n += 1


def layer1(nc, a, keep):
    ctx = ExitStack()
    with ctx:
        def sb(name, shape, dt=F32):
            return ctx.enter_context(nc.sbuf_tensor(name, shape, dt))

        def sem(name):
            return ctx.enter_context(nc.semaphore(name))

        resid, xth, xtl = keep["resid"], keep["xth"], keep["xtl"]
        identf, identb, masku = keep["identf"], keep["identb"], keep["masku"]
        ps = ctx.enter_context(nc.psum_tensor("ps1", [P, 8, 512], F32))

        def bank(b):
            return ps[:, b % 8, :]

        qth, qtl = sb("qth", [P, G1, S], F32R), sb("qtl", [P, G1, S], F32R)
        kth, ktl = sb("kth", [P, S], F32R), sb("ktl", [P, S], F32R)
        k0h, k0l = sb("k0h", [P, 2 * P], F32R), sb("k0l", [P, 2 * P], F32R)
        vh, vl = sb("vh", [P, ST, P], F32R), sb("vl", [P, ST, P], F32R)
        wh, wl = sb("wh", [P, W_RING, BLK], F32R), sb("wl1", [P, W_RING, BLK], F32R)
        woh, wol = sb("woh1", [P, G1, D], F32R), sb("wol1", [P, G1, D], F32R)
        raw = sb("raw", [P, RAW_RING, BLK])
        cos, sin = sb("cos", [P, S]), sb("sin", [P, S])
        kscale, tscale = sb("kscale", [P, P]), sb("tscale", [P, P])
        negm, rowsum, rinv = sb("negm1", [P, NHEADS]), sb("rowsum", [P, NHEADS]), sb("rinv", [P, NHEADS])
        norm = Norm(nc, ctx, keep, "l1_", None, bank)
        with ExitStack() as early:
            norm.xn = early.enter_context(nc.sbuf_tensor("xn1", [P, ST, D], F32))
        with ExitStack() as late:
            def sbl(name, shape, dt=F32):
                return late.enter_context(nc.sbuf_tensor(name, shape, dt))
            plong, pshort = sbl("plong", [P, 2, 2, S]), sbl("pshort", [P, 2, 2, BLK])
            ptnh, ptnl = sbl("ptnh", [P, PT_RING, BLK], F32R), sbl("ptnl", [P, PT_RING, BLK], F32R)
            oth, otl = sbl("oth", [P, 2, G1, P], F32R), sbl("otl", [P, 2, G1, P], F32R)
            rota, rotb = sbl("rota", [P, 2, BLK]), sbl("rotb", [P, 2, BLK])
            vt = sbl("vt", [P, NB, BLK])

        const_in = sem("c1_in")
        raw_in = [sem(f"raw_in{i}") for i in range(RAW_RING)]
        w_split, w_high = sem("w_split"), sem("w_high")
        proj_filled, rope_read, vt_ready = sem("proj_filled"), sem("rope_read"), sem("vt_ready")
        rot_step, kq_ready = sem("rot_step"), sem("kq_ready")
        qk_filled, max_step, max_ready, exp_ready, rinv_ready, p_ready = (
            sem(n) for n in ("qk_filled", "max_step", "max_ready", "exp_ready", "rinv_ready", "p_ready"))
        bank_filled, high_ready, low_ready, av_unit = sem("bank_filled"), sem("bk_high"), sem("bk_low"), sem("av_unit")
        o_high, o_low, y_added = sem("o_high"), sem("o_low"), sem("y_added")
        k0_init, waited = sem("k0_init"), sem("waited")

        block = ctx.enter_context(nc.Block())

        first, more, final = first_steps(), group_steps(True), group_steps(False)
        place_first, place_more, place_final = Place(first), Place(more), Place(final)
        GFILL = len(place_more.fills)
        CHUNKS = NCHUNK + G1

        def length(j):
            return PAIRS[j][0] + 1

        def pbuf(n):
            j, i = divmod(n, 2)
            t = PAIRS[j][0]
            if t >= 4:
                return plong[:, j // 2 % 2, i, 0:(t + 1) * P]
            return pshort[:, j // 2 % 2, i, 0:(t + 1) * P]

        def qk_banks(n):
            return ps[:, 2 * (n % 2):2 * (n % 2) + 2, :].rearrange("p b c -> p (b c)")

        def place_of(g):
            return (place_first if g < 0 else place_final) if isinstance(g, int) else place_more

        def bank_of(s, g):
            return 4 + place_of(g).fill[s] % 2

        def walk(eng, step, lag=0, late_step=None):
            def go(steps, g):
                for i, s in enumerate(steps):
                    step(s, g)
                    if late_step and i >= lag:
                        late_step(steps[i - lag], g)
                if late_step:
                    for s in steps[max(0, len(steps) - lag):]:
                        late_step(s, g)
            go(first, -1)
            with eng.Fori(0, KV1 - 1) as g:
                go(more, g)
            go(final, KV1 - 1)

        def fill_count(s, g):
            if isinstance(g, int) and g < 0:
                return place_first.fill[s]
            return g * GFILL + (SPLIT_FIRST + place_of(g).fill[s])

        def split_count(s, g):
            if isinstance(g, int) and g < 0:
                return place_first.split[s]
            return g * SPLIT_GROUP + (SPLIT_FIRST + place_of(g).split[s])

        def free_probabilities(eng, n, g):
            j = n // 2
            if j >= 4:
                u = max(i for i, (jj, _) in enumerate(UNITS) if jj == j - 4)
                eng.wait_ge(bank_filled, fill_count(("turn", u), g) + 1)

        @block.sync
        def _(sp):
            sp.dma_start(cos[:], a["cos"]).then_inc(const_in, 16)
            sp.dma_start(sin[:], a["sin"]).then_inc(const_in, 16)
            sp.dma_start(kscale[:], a["kscale"]).then_inc(const_in, 16)
            sp.dma_start(tscale[:], a["tscale"]).then_inc(const_in, 16)

            def load(c, g, k):
                r = k % RAW_RING
                src = a["w1"][g, c] if c < NCHUNK else a["wo1"][g, c - NCHUNK]
                sp.dma_start(raw[:, r, :], src).then_inc(raw_in[r], 16)

            for c in range(NCHUNK):
                if c >= RAW_RING:
                    sp.wait_ge(w_split, c - RAW_RING + 1)
                load(c, 0, c)
            def group(g, chunks):
                for k in range(chunks):
                    sp.wait_ge(w_split, g * CHUNKS + (NCHUNK + k - RAW_RING + 1))
                    if k < G1:
                        load(NCHUNK + k, g, k)
                    else:
                        load(k - G1, g + 1, k)

            with sp.Fori(0, KV1 - 1) as g:
                group(g, CHUNKS)
            group(KV1 - 1, G1)

        @block.tensor
        def _(pe):
            norm.tensor(nc, pe)

            def proj(f, g):
                c, b = divmod(f, NB)
                if f < 4:
                    if isinstance(g, int) and g == 0:
                        if f == 0:
                            pe.wait_ge(norm.low_ready, ST)
                    else:
                        pe.wait_ge(exp_ready, g * NHEADS)
                elif f < 6:
                    pe.wait_ge(rope_read, g * 10 + (f - 3))
                elif f < 8:
                    pe.wait_ge(vt_ready, g * 2 + (f - 5))
                else:
                    pe.wait_ge(rope_read, g * 10 + (f - 5))
                if b == 0:
                    pe.wait_ge(w_split, g * CHUNKS + (c + 1))
                for d in range(DT):
                    w = (wh[:, c % W_RING, d * P:(d + 1) * P], wl[:, c % W_RING, d * P:(d + 1) * P])
                    last = products(pe, bank(f % 4), w, (xth[:, d, b * BLK:(b + 1) * BLK], xtl[:, d, b * BLK:(b + 1) * BLK]),
                                    d == 0, d == DT - 1)
                last.then_inc(proj_filled, 1)

            def qk(n, g):
                j, i = divmod(n, 2)
                t, p = PAIRS[j]
                h = 2 * p + i
                if n >= 2:
                    pe.wait_ge(exp_ready, g * NHEADS + (n - 1))
                else:
                    pe.wait_ge(rope_read, g * 10 + 10)
                    pe.wait_ge(vt_ready, g * 2 + 2)
                pe.wait_ge(kq_ready, g * 10 + (2 * h + 4))
                q = (qth[:, h, t * P:(t + 1) * P], qtl[:, h, t * P:(t + 1) * P])
                out = qk_banks(n)
                width = (t + 1) * P
                for c0 in range(0, width, BLK):
                    w = max(2 * P, min(BLK, width - c0))
                    k = (k0h[:, 0:w], k0l[:, 0:w]) if t == 0 else (kth[:, c0:c0 + w], ktl[:, c0:c0 + w])
                    products(pe, out[:, c0:c0 + w], q, k, True, c0 + BLK < width)
                pe.matmul(out[:, t * P:(t + 1) * P], identb[:], masku[:], start=False, stop=True).then_inc(qk_filled, 1)

            def bank_free(s, g):
                if isinstance(g, int) and g < 0:
                    return
                place = place_of(g)
                i = place.fill[s]
                past = place.fills[i - 2] if i >= 2 else place_more.fills[i - 2]
                if past[0] == "out":
                    pe.wait_ge(y_added, g * NTOK + (past[1] + 2 - (0 if i >= 2 else NTOK)))
                else:
                    pe.wait_ge(low_ready, g * SPLIT_GROUP + (SPLIT_FIRST + place_more.split[past] + 1 - (0 if i >= 2 else SPLIT_GROUP)))

            def turn(u, g):
                j, k = UNITS[u]
                t = PAIRS[j][0]
                bank_free(("turn", u), g)
                pe.wait_ge(p_ready, g * NPAIR + (j + 1))
                b = bank_of(("turn", u), g)
                for kk in range(k, min(k + 2, t + 1)):
                    for i in range(2):
                        last = nc.tensor.transpose(ps[:, b, (2 * (kk - k) + i) * P:(2 * (kk - k) + i + 1) * P],
                                                   pbuf(2 * j + i)[:, kk * P:(kk + 1) * P], identf[:])
                last.then_inc(bank_filled, 1)

            def av(u, g):
                j, k = UNITS[u]
                t = PAIRS[j][0]
                if k == 0:
                    pe.wait_ge(o_low, g * NPAIR + max(1, j))
                pe.wait_ge(low_ready, split_count(("turn", u), g) + 1)
                for kk in range(k, min(k + 2, t + 1)):
                    c = 2 * P * (kk - k)
                    last = products(pe, ps[:, 6 + j % 2, 0:2 * P], (vh[:, kk, :], vl[:, kk, :]),
                                    (ptnh[:, u % PT_RING, c:c + 2 * P], ptnl[:, u % PT_RING, c:c + 2 * P]), kk == 0, kk == t)
                last.then_inc(av_unit, 1)

            def out(o, g):
                q, ab = divmod(o, 2)
                bank_free(("out", o), g)
                pe.wait_ge(o_low, g * NPAIR + (4 * q + 4 + ab))
                pe.wait_ge(w_split, g * CHUNKS + CHUNKS)
                b = bank_of(("out", o), g)
                for h in range(G1):
                    last = products(pe, bank(b), (oth[:, ab, h, :], otl[:, ab, h, :]), (woh[:, h, :], wol[:, h, :]), h == 0, h == G1 - 1)
                last.then_inc(bank_filled, 1)

            def vturn(v, g):
                bank_free(("vturn", v), g)
                pe.wait_ge(vt_ready, (g + 1) * 2 + (v + 1))
                b = bank_of(("vturn", v), g)
                for i in range(4):
                    last = nc.tensor.transpose(ps[:, b, i * P:(i + 1) * P], vt[:, v, i * P:(i + 1) * P], identf[:])
                last.then_inc(bank_filled, 1)

            def step(s, g):
                kind, i = s
                if kind == "proj":
                    proj(i, g + 1)
                elif kind == "qk":
                    qk(i, g)
                elif kind == "qknext":
                    qk(i, g + 1)
                elif kind == "turn":
                    turn(i, g)
                elif kind == "av":
                    av(i, g)
                elif kind == "out":
                    out(i, g)
                elif kind == "vturn":
                    vturn(i, g)

            pe.wait_ge(k0_init, 2)
            walk(pe, step)

        @block.scalar
        def _(act):
            norm.scalar_sqrt(nc, act)
            norm.scalar_high(nc, act)

            def step(s, g):
                kind, i = s
                if kind == "proj" and i in (2, 3):
                    gg = g + 1
                    act.wait_ge(proj_filled, gg * NFILL + (i + 1))
                    nc.scalar.activation(vt[:, i - 2, :], bank(i), ACT.Copy).then_inc(vt_ready, 1)
                elif kind in ("turn", "vturn"):
                    act.wait_ge(bank_filled, fill_count(s, g) + 1)
                    if kind == "turn":
                        j, k = UNITS[i]
                        w = 2 * P * min(2, PAIRS[j][0] + 1 - k)
                        if i >= PT_RING:
                            act.wait_ge(av_unit, g * NUNIT + (i - PT_RING + 1))
                        b = bank_of(s, g)
                        nc.scalar.activation(ptnh[:, i % PT_RING, 0:w], ps[:, b, 0:w], ACT.Copy).then_inc(high_ready, 1)
                    else:
                        gg = g + 1
                        b = bank_of(s, g)
                        act.wait_ge(av_unit, gg * NUNIT)
                        nc.scalar.activation(vh[:, 4 * i:4 * i + 4, :], bank(b).rearrange("p (t d) -> p t d", t=4),
                                             ACT.Copy).then_inc(high_ready, 1)
                elif kind == "av":
                    j, k = UNITS[i]
                    t, p = PAIRS[j]
                    if k + 2 > t:
                        act.wait_ge(av_unit, g * NUNIT + (i + 1))
                        ab = j % 2
                        act.wait_ge(y_added, g * NTOK + max(1, 2 * (j // 4) + ab))
                        nc.scalar.activation(oth[:, ab, 2 * p:2 * p + 2, :], ps[:, 6 + j % 2, 0:2 * P].rearrange("p (h q) -> p h q", h=2),
                                             ACT.Copy).then_inc(o_high, 1)

            def late_step(s, g):
                kind, n = s
                if kind in ("qk", "qknext"):
                    gg = g + 1 if kind == "qknext" else g
                    j, i = divmod(n, 2)
                    t = PAIRS[j][0]
                    act.wait_ge(max_ready, gg * NHEADS + (n + 1))
                    src = qk_banks(n)[:, 0:(t + 1) * P] if t else pbuf(n)
                    if t:
                        free_probabilities(act, n, gg)
                    nc.scalar.activation(pbuf(n), src, ACT.Exp, bias=negm[:, n:n + 1], accum_out=rowsum[:, n:n + 1]).then_inc(exp_ready, 1)

            walk(act, step, 2, late_step)

        @block.vector
        def _(dve):
            dve.sem_inc(y_added, 1)
            dve.sem_inc(o_low, 1)
            nc.vector.memset(k0h[:].bitcast(F32), 0.0).then_inc(k0_init, 1)
            nc.vector.memset(k0l[:].bitcast(F32), 0.0).then_inc(k0_init, 1)
            norm.vector(nc, dve, lambda e, st: None)
            dve.wait_ge(norm.xn_ready, ST)
            dve.wait_ge(const_in, 64)

            def rope(f, g):
                gg = g + 1
                r = f if f < 2 else f - 2
                c = HD1 ** -0.5 if f >= 4 else 1.0
                dve.wait_ge(proj_filled, gg * NFILL + (f + 1))
                if r >= 2 or not isinstance(gg, int):
                    dve.wait_ge(kq_ready, gg * 10 + (r - 1))
                cols = slice(f % NB * BLK, (f % NB + 1) * BLK)
                src = bank(f % 4)
                nc.vector.scalar_tensor_tensor(out=rota[:, r % 2, :], in0=src, scalar=c, in1=cos[:, cols], op0=ALU.mult, op1=ALU.mult)
                nc.vector.scalar_tensor_tensor(out=rotb[0:64, r % 2, :], in0=src[64:128, :], scalar=c, in1=sin[64:128, cols],
                                               op0=ALU.mult, op1=ALU.mult)
                nc.vector.scalar_tensor_tensor(out=rotb[64:128, r % 2, :], in0=src[0:64, :], scalar=c, in1=sin[0:64, cols],
                                               op0=ALU.mult, op1=ALU.mult).then_inc(rope_read, 1)

            def step(s, g):
                kind, i = s
                if kind == "proj" and i not in (2, 3):
                    rope(i, g)
                elif kind in ("qk", "qknext"):
                    gg = g + 1 if kind == "qknext" else g
                    t = PAIRS[i // 2][0]
                    dve.wait_ge(qk_filled, gg * NHEADS + (i + 1))
                    if t:
                        nc.vector.tensor_reduce(negm[:, i:i + 1], qk_banks(i)[:, 0:(t + 1) * P], AX.X, ALU.max, negate=True).then_inc(max_ready, 1)
                    else:
                        free_probabilities(dve, i, gg)
                        nc.vector.tensor_tensor(pbuf(i), qk_banks(i)[:, 0:P], tscale[:], ALU.mult).then_inc(max_step, 1)
                        dve.wait_ge(max_step, gg * 4 + FIRST_TILE.index(i) + 1)
                        nc.vector.tensor_reduce(negm[:, i:i + 1], pbuf(i), AX.X, ALU.max, negate=True).then_inc(max_ready, 1)
                elif kind in ("turn", "vturn"):
                    dve.wait_ge(high_ready, split_count(s, g) + 1)
                    if kind == "turn":
                        j, k = UNITS[i]
                        w = 2 * P * min(2, PAIRS[j][0] + 1 - k)
                        b = bank_of(s, g)
                        nc.vector.tensor_tensor(ptnl[:, i % PT_RING, 0:w], ps[:, b, 0:w], ptnh[:, i % PT_RING, 0:w].bitcast(F32),
                                                ALU.subtract).then_inc(low_ready, 1)
                    else:
                        b = bank_of(s, g)
                        nc.vector.tensor_tensor(vl[:, 4 * i:4 * i + 4, :], bank(b).rearrange("p (t d) -> p t d", t=4),
                                                vh[:, 4 * i:4 * i + 4, :].bitcast(F32), ALU.subtract).then_inc(low_ready, 1)
                elif kind == "av":
                    j, k = UNITS[i]
                    t, p = PAIRS[j]
                    if k + 2 > t:
                        dve.wait_ge(o_high, g * NPAIR + (j + 1))
                        ab = j % 2
                        nc.vector.tensor_tensor(otl[:, ab, 2 * p:2 * p + 2, :], ps[:, 6 + j % 2, 0:2 * P].rearrange("p (h q) -> p h q", h=2),
                                                oth[:, ab, 2 * p:2 * p + 2, :].bitcast(F32), ALU.subtract).then_inc(o_low, 1)
                elif kind == "out":
                    t = QUADS[i // 2][i % 2]
                    dve.wait_ge(bank_filled, fill_count(s, g) + 1)
                    dve.wait_ge(y_added, g * NTOK + 1)
                    nc.vector.tensor_tensor(resid[:, t, :], ps[:, bank_of(s, g), :], resid[:, t, :], ALU.add).then_inc(y_added, 1)

            def late_step(s, g):
                kind, n = s
                if kind in ("qk", "qknext") and n % 2 == 1:
                    gg = g + 1 if kind == "qknext" else g
                    dve.wait_ge(exp_ready, gg * NHEADS + (n + 1))
                    nc.vector.reciprocal(rinv[:, n - 1:n + 1], rowsum[:, n - 1:n + 1]).then_inc(rinv_ready, 1)

            walk(dve, step, 2, late_step)

        @block.gpsimd
        def _(pool):
            def split(src, high, low, n):
                pool.sem_inc(waited, 1)
                nc.gpsimd.tensor_scalar(high, src, 1.0, 1.0, ALU.mult, ALU.mult).then_inc(w_high, 1)
                pool.wait_ge(w_high, n)
                nc.gpsimd.tensor_tensor(low, src, high.bitcast(F32), ALU.subtract).then_inc(w_split, 1)

            def rotated(f, gg):
                r = f if f < 2 else f - 2
                base = 0 if r == 0 else 5 + 2 * (r - 1)
                pool.wait_ge(rope_read, gg * 10 + (r + 1))
                pool.wait_ge(qk_filled, gg * NHEADS)
                sums, other = rota[:, r % 2, :], rotb[:, r % 2, :]

                def chained(ins, n):
                    ins.then_inc(rot_step, 1)
                    pool.wait_ge(rot_step, gg * ROT_STEPS + (base + n))

                chained(nc.gpsimd.tensor_tensor(sums, sums, other, ALU.add), 1)
                cols = slice(f % NB * BLK, (f % NB + 1) * BLK)
                if r == 0:
                    pool.sem_inc(waited, 1)
                    chained(nc.gpsimd.tensor_scalar(k0h[:, 0:P], sums[:, 0:P], 1.0, 1.0, ALU.mult, ALU.mult), 2)
                    chained(nc.gpsimd.tensor_tensor(k0l[:, 0:P], sums[:, 0:P], k0h[:, 0:P].bitcast(F32), ALU.subtract), 3)
                    chained(nc.gpsimd.tensor_tensor(sums[:, 0:P], sums[:, 0:P], kscale[:], ALU.mult), 4)
                high, low = (kth[:, cols], ktl[:, cols]) if r < 2 else (qth[:, (r - 2) // NB, cols], qtl[:, (r - 2) // NB, cols])
                pool.sem_inc(waited, 1)
                chained(nc.gpsimd.tensor_scalar(high, sums, 1.0, 1.0, ALU.mult, ALU.mult), 5 if r == 0 else 2)
                nc.gpsimd.tensor_tensor(low, sums, high.bitcast(F32), ALU.subtract).then_inc(kq_ready, 1)

            def step(s, g):
                kind, i = s
                gg = g + 1
                if kind == "w":
                    pool.wait_ge(raw_in[i % RAW_RING], gg * (8 * CHUNKS) + 16 * (i // RAW_RING + 1))
                    if i >= W_RING:
                        pool.wait_ge(proj_filled, gg * NFILL + NB * (i - W_RING + 1))
                    else:
                        pool.wait_ge(proj_filled, gg * NFILL)
                    split(raw[:, i % RAW_RING, :], wh[:, i % W_RING, :], wl[:, i % W_RING, :], gg * CHUNKS + (i + 1))
                elif kind == "wo":
                    k = NCHUNK + i
                    pool.wait_ge(raw_in[k % RAW_RING], g * (8 * CHUNKS) + 16 * (k // RAW_RING + 1))
                    pool.wait_ge(y_added, g * NTOK + 1)
                    split(raw[:, k % RAW_RING, :], woh[:, i, :], wol[:, i, :], g * CHUNKS + (k + 1))
                elif kind == "proj" and i not in (2, 3):
                    rotated(i, gg)

            def late_step(s, g):
                kind, n = s
                if kind in ("qk", "qknext") and n % 2 == 1:
                    gg = g + 1 if kind == "qknext" else g
                    pool.wait_ge(rinv_ready, gg * NPAIR + (n // 2 + 1))
                    pool.sem_inc(waited, 1)
                    nc.gpsimd.tensor_scalar(pbuf(n - 1), pbuf(n - 1), rinv[:, n - 1:n], 1.0, ALU.mult, ALU.mult)
                    nc.gpsimd.tensor_scalar(pbuf(n), pbuf(n), rinv[:, n:n + 1], 1.0, ALU.mult, ALU.mult).then_inc(p_ready, 1)

            pool.wait_ge(const_in, 64)
            pool.wait_ge(k0_init, 2)
            walk(pool, step, 2, late_step)



FT = -(-FH // P)
FLAST = FH - (FT - 1) * P
RS, RROWS = 32, 96


def gated(nc, a, keep):
    ctx = ExitStack()
    with ctx:
        def sb(name, shape, dt=F32):
            return ctx.enter_context(nc.sbuf_tensor(name, shape, dt))

        def sem(name):
            return ctx.enter_context(nc.semaphore(name))

        resid, xth, xtl = keep["resid"], keep["xth"], keep["xtl"]
        ps = ctx.enter_context(nc.psum_tensor("ps2", [P, 8, 512], F32))
        raw = sb("raw2", [P, 6, BLK])
        wh, wl = sb("wh2", [P, 6, BLK], F32R), sb("wl2", [P, 6, BLK], F32R)
        sg, hid = sb("sg", [P, NB, BLK]), sb("hid", [P, NB, BLK])
        hidh, hidl = sb("hidh", [P, 2, S], F32R), sb("hidl", [P, 2, S], F32R)
        araw = sb("araw", [P, 2 * DT + FT, RANK])
        asplit = sb("asplit", [P, 2, 2 * DT + FT, RROWS], F32R)
        ah, al = asplit[:, 0, :, :], asplit[:, 1, :, :]
        bnow, anow = sb("bnow", [RROWS, 2, 2, P], F32R), sb("anow", [P, 2, 2, RROWS], F32R)
        BW = 2 * FH + D
        braw, bs = sb("braw", [RROWS, BW]), sb("bs", [RROWS, BW], F32R)
        xa = sb("xa", [RROWS, 2, S], F32R)
        zero = sb("zero", [P, P], BF16)
        ha = sb("ha", [RROWS, S], F32R)

        raw_in = [sem(f"raw2_in{i}") for i in range(6)]
        zero_ready, now_ready, waited = sem("zero_ready"), sem("now_ready"), sem("waited2")
        a_in, b_in, b_zero, a_zero = sem("a_in"), sem("b_in"), sem("b_zero"), sem("a_zero")
        a_high, a_low, b_high, b_ready = sem("a_high"), sem("a_low"), sem("b_high"), sem("b_ready")
        xa_filled, xa_high, xa_ready = sem("xa_filled"), sem("xa_high"), sem("xa_ready")
        w_high, w_split = sem("w2_high"), sem("w2_split")
        gu_filled, silu_done, hid_made, hid_high, hid_low = (sem(n) for n in ("gu_filled", "silu_done", "hid_made", "hid_high", "hid_low"))
        ha_filled, ha_high, ha_ready = sem("ha_filled"), sem("ha_high"), sem("ha_ready")
        down_filled, added, out_done = sem("down_filled"), sem("added"), sem("out2_done")
        block = ctx.enter_context(nc.Block())

        def rows(j):
            return FLAST if isinstance(j, int) and j == FT - 1 else P

        def walk(eng, start, body):
            start()
            loops = (FT - 2) // 2
            with eng.Fori(0, loops) as jj:
                body(jj * 2, 0)
                body(jj * 2 + 1, 1)
            for j in range(2 * loops, FT):
                body(j, j % 2)

        @block.sync
        def _(sp):
            def load(j, par, which):
                if not (isinstance(j, int) and j < 2):
                    sp.wait_ge(w_split, 3 * j + (which - 5))
                k, n = 3 * par + which, rows(j)
                if which < 2:
                    name = "gate" if which == 0 else "up"
                    src = a[name + "_last"] if n < P else a[name + "_main"][j]
                    sp.dma_start(raw[:, k, 0:DT * n], src).then_inc(raw_in[k], 16)
                else:
                    src = a["down_main"][j] if n == P else a["down_last"]
                    sp.dma_start(raw[0:n, k, :], src).then_inc(raw_in[k], 16)

            sp.dma_start(araw[:, 0:DT, :], a["gate_a"].rearrange("(c p) r -> p c r", p=P)).then_inc(a_in, 16)
            sp.dma_start(araw[:, DT:2 * DT, :], a["up_a"].rearrange("(c p) r -> p c r", p=P)).then_inc(a_in, 16)
            for which in (0, 1):
                load(0, 0, which)
            sp.wait_ge(a_zero, 1)
            sp.dma_start(araw[:, 2 * DT:2 * DT + FT - 1, :], a["down_a"][0:(FT - 1) * P, :].rearrange("(c p) r -> p c r", p=P)).then_inc(a_in, 16)
            sp.dma_start(araw[0:FLAST, 2 * DT + FT - 1, :], a["down_a"][(FT - 1) * P:FH, :]).then_inc(a_in, 16)
            sp.wait_ge(b_zero, 1)
            for r in range(3):
                for name, c0, n in (("gate_b", 0, FH), ("up_b", FH, FH), ("down_b", 2 * FH, D)):
                    sp.dma_start(braw[RS * r:RS * r + RANK, c0:c0 + n], a[name]).then_inc(b_in, 16)
            load(0, 0, 2)
            for which in (0, 1, 2):
                load(1, 1, which)

            def body(j, par):
                if not (isinstance(j, int) and j + 2 >= FT):
                    for which in (0, 1, 2):
                        load(j + 2, par, which)
            walk(sp, lambda: None, body)
            for t in range(ST):
                sp.wait_ge(added, ST * (FT - 1) + t + 2)
                sp.dma_start(a["out"].rearrange("(t p) d -> p t d", p=P)[:, t, :], resid[:, t, :]).then_inc(out_done, 16)
            sp.wait_ge(out_done, 16 * ST)

        @block.tensor
        def _(pe):
            pe.sem_inc(down_filled, 1)
            pe.wait_ge(a_low, 1)
            for g in range(2):
                for b in range(NB):
                    for d in range(DT):
                        last = products(pe, ps[0:RROWS, 2 * g + b, :], (ah[:, g * DT + d, :], al[:, g * DT + d, :]),
                                        (xth[:, d, b * BLK:(b + 1) * BLK], xtl[:, d, b * BLK:(b + 1) * BLK]), d == 0, d == DT - 1)
                    last.then_inc(xa_filled, 1)

            def gate_up(j, par):
                n = rows(j)
                for b in range(NB):
                    if isinstance(j, int) and j == 0:
                        pe.wait_ge(xa_ready, 4)
                    else:
                        pe.wait_ge(hid_made, j * 2 + (b - 1))
                    for which in range(2):
                        if b == 0:
                            pe.wait_ge(w_split, 3 * j + which + 1)
                        k = 3 * par + which
                        w3h = wh[:, k, 0:DT * n].rearrange("p (d n) -> p d n", d=DT)
                        w3l = wl[:, k, 0:DT * n].rearrange("p (d n) -> p d n", d=DT)
                        out = ps[0:n, 2 * b + which, :]
                        for d in range(DT):
                            products(pe, out, (w3h[:, d, :], w3l[:, d, :]),
                                     (xth[:, d, b * BLK:(b + 1) * BLK], xtl[:, d, b * BLK:(b + 1) * BLK]), d == 0, False)
                        pe.wait_ge(now_ready, 2 * j + 2)
                        last = pe.matmul(out, bnow[:, par, which, 0:n], xa[:, which, b * BLK:(b + 1) * BLK], start=False, stop=True)
                    last.then_inc(gu_filled, 1)

            def hidden_a(j, par):
                n = rows(j)
                pe.wait_ge(hid_low, 2 * j + 2)
                for b in range(NB):
                    cols = slice(b * BLK, (b + 1) * BLK)
                    l = (anow[0:n, par, 0, :], anow[0:n, par, 1, :])
                    r = (hidh[0:n, par, cols], hidl[0:n, par, cols])
                    start = isinstance(j, int) and j == 0
                    lastj = isinstance(j, int) and j == FT - 1
                    last = products(pe, ps[0:RROWS, 6 + b, :], l, r, start, lastj)
                    if lastj:
                        last.then_inc(ha_filled, 1)

            def down(j, par):
                n = rows(j)
                pe.wait_ge(w_split, 3 * j + 3)
                lastj = isinstance(j, int) and j == FT - 1
                if lastj:
                    pe.wait_ge(ha_ready, NB)
                for t in range(ST):
                    if not (isinstance(j, int) and j == 0 and t < 2):
                        pe.wait_ge(added, ST * j + max(1, t))
                    out = ps[:, 4 + t % 2, :]
                    last = products(pe, out, (hidh[0:n, par, t * P:(t + 1) * P], hidl[0:n, par, t * P:(t + 1) * P]),
                                    (wh[0:n, 3 * par + 2, :], wl[0:n, 3 * par + 2, :]), True, not lastj)
                    if lastj:
                        last = pe.matmul(out, ha[:, t * P:(t + 1) * P], bs[:, 2 * FH:2 * FH + D], start=False, stop=True)
                    last.then_inc(down_filled, 1)

            def start():
                pe.wait_ge(b_ready, 1)
                gate_up(0, 0)
                pe.wait_ge(zero_ready, 1)
                for b in range(NB):
                    pe.matmul(ps[0:RROWS, 6 + b, :], zero[:, 0:RROWS], zero[:, 0:1].to_broadcast([P, BLK]), start=True, stop=False)

            def body(j, par):
                if not (isinstance(j, int) and j == FT - 1):
                    gate_up(j + 1, 1 - par)
                hidden_a(j, par)
                down(j, par)
            walk(pe, start, body)

        @block.scalar
        def _(act):
            for g in range(2):
                for b in range(NB):
                    act.wait_ge(xa_filled, 2 * g + b + 1)
                    nc.scalar.activation(xa[:, g, b * BLK:(b + 1) * BLK], ps[0:RROWS, 2 * g + b, :], ACT.Copy).then_inc(xa_high, 1)

            def low_rank(j, par):
                n = rows(j)
                if not (isinstance(j, int) and j < 2):
                    act.wait_ge(down_filled, ST * j - (ST - 1))
                cols = slice(j * P, j * P + n) if isinstance(j, int) else bass.ds(j * P, n)
                nc.scalar.activation(bnow[:, par, :, 0:n], bs[:, 0:2 * FH].bitcast(F32).rearrange("p (w n) -> p w n", w=2)[:, :, cols],
                                     ACT.Copy).then_inc(now_ready, 1)
                tile = slice(2 * DT + j, 2 * DT + j + 1) if isinstance(j, int) else bass.ds(2 * DT + j, 1)
                nc.scalar.activation(anow[:, par, :, :].unsqueeze(2), asplit[:, :, tile, :].bitcast(F32), ACT.Copy).then_inc(now_ready, 1)

            def hidden(j, par):
                n = rows(j)
                for b in range(NB):
                    act.wait_ge(gu_filled, 2 * j + (b + 1))
                    nc.scalar.activation(sg[0:n, b, :], ps[0:n, 2 * b, :], ACT.Silu).then_inc(silu_done, 1)
                for b in range(NB):
                    act.wait_ge(hid_made, 2 * j + (b + 1))
                    if not (isinstance(j, int) and j < 2):
                        act.wait_ge(down_filled, ST * j - (ST - 1))
                    nc.scalar.activation(hidh[0:n, par, b * BLK:(b + 1) * BLK], hid[0:n, b, :], ACT.Copy).then_inc(hid_high, 1)

            def body(j, par):
                if not (isinstance(j, int) and j == FT - 1):
                    low_rank(j + 1, 1 - par)
                    hidden(j + 1, 1 - par)

            def start():
                act.wait_ge(b_ready, 1)
                low_rank(0, 0)
                hidden(0, 0)
            walk(act, start, body)
            for b in range(NB):
                act.wait_ge(ha_filled, b + 1)
                nc.scalar.activation(ha[:, b * BLK:(b + 1) * BLK], ps[0:RROWS, 6 + b, :], ACT.Copy).then_inc(ha_high, 1)

        @block.vector
        def _(dve):
            dve.sem_inc(added, 1)
            nc.vector.memset(araw[:, 2 * DT + FT - 1, :], 0.0).then_inc(a_zero, 1)
            nc.vector.memset(braw[:], 0.0).then_inc(b_zero, 1)
            nc.vector.memset(zero[:], 0.0).then_inc(zero_ready, 1)
            dve.wait_ge(a_in, 64)
            rep = araw[:].unsqueeze(2).to_broadcast([P, 2 * DT + FT, RROWS // RANK, RANK])
            nc.vector.tensor_copy(ah.rearrange("p c (k r) -> p c k r", r=RANK), rep).then_inc(a_high, 1)
            dve.wait_ge(a_high, 1)
            nc.vector.tensor_tensor(al.rearrange("p c (k r) -> p c k r", r=RANK), rep,
                                    ah.bitcast(F32).rearrange("p c (k r) -> p c k r", r=RANK), ALU.subtract).then_inc(a_low, 1)
            dve.wait_ge(b_in, 16 * 9)
            nc.vector.tensor_copy(bs[:], braw[:]).then_inc(b_high, 1)
            dve.wait_ge(b_high, 1)
            nc.vector.tensor_tensor(bs[RS:2 * RS, :], braw[RS:2 * RS, :], bs[RS:2 * RS, :].bitcast(F32), ALU.subtract).then_inc(b_ready, 1)
            for g in range(2):
                for b in range(NB):
                    dve.wait_ge(xa_high, 2 * g + b + 1)
                    part = xa[2 * RS:RROWS, g, b * BLK:(b + 1) * BLK]
                    nc.vector.tensor_tensor(part, ps[2 * RS:RROWS, 2 * g + b, :], part.bitcast(F32), ALU.subtract).then_inc(xa_ready, 1)

            def hidden(j):
                n = rows(j)
                for b in range(NB):
                    dve.wait_ge(silu_done, 2 * j + (b + 1))
                    if not (isinstance(j, int) and j == 0):
                        dve.wait_ge(hid_low, 2 * j + (b - 1))
                    nc.vector.tensor_tensor(hid[0:n, b, :], ps[0:n, 2 * b + 1, :], sg[0:n, b, :], ALU.mult).then_inc(hid_made, 1)

            def body(j, par):
                if not (isinstance(j, int) and j == FT - 1):
                    hidden(j + 1)
                else:
                    for b in range(NB):
                        dve.wait_ge(ha_high, b + 1)
                        part = ha[2 * RS:RROWS, b * BLK:(b + 1) * BLK]
                        nc.vector.tensor_tensor(part, ps[2 * RS:RROWS, 6 + b, :], part.bitcast(F32), ALU.subtract).then_inc(ha_ready, 1)
                dve.wait_ge(added, ST * j + 1)
                for t in range(ST):
                    dve.wait_ge(down_filled, ST * j + (t + 2))
                    nc.vector.tensor_tensor(resid[:, t, :], ps[:, 4 + t % 2, :], resid[:, t, :], ALU.add).then_inc(added, 1)
            walk(dve, lambda: hidden(0), body)

        @block.gpsimd
        def _(pool):
            def split(j, par, which):
                k, n = 3 * par + which, rows(j)
                pool.wait_ge(raw_in[k], 8 * (j - par) + 16)
                if not (isinstance(j, int) and j < 2):
                    if which < 2:
                        pool.wait_ge(gu_filled, 2 * j - 2)
                    else:
                        pool.wait_ge(down_filled, ST * j - (ST - 1))
                if which < 2:
                    src, high, low = raw[:, k, 0:DT * n], wh[:, k, 0:DT * n], wl[:, k, 0:DT * n]
                else:
                    src, high, low = raw[0:n, k, :], wh[0:n, k, :], wl[0:n, k, :]
                pool.sem_inc(waited, 1)
                nc.gpsimd.tensor_scalar(high, src, 1.0, 1.0, ALU.mult, ALU.mult).then_inc(w_high, 1)
                pool.wait_ge(w_high, 3 * j + which + 1)
                nc.gpsimd.tensor_tensor(low, src, high.bitcast(F32), ALU.subtract).then_inc(w_split, 1)

            def hidden(j, par):
                n = rows(j)
                for b in range(NB):
                    pool.wait_ge(hid_high, 2 * j + (b + 1))
                    cols = slice(b * BLK, (b + 1) * BLK)
                    nc.gpsimd.tensor_tensor(hidl[0:n, par, cols], hid[0:n, b, :], hidh[0:n, par, cols].bitcast(F32), ALU.subtract).then_inc(hid_low, 1)

            def start():
                for which in range(3):
                    split(0, 0, which)
                for which in range(3):
                    split(1, 1, which)
                hidden(0, 0)

            def body(j, par):
                if not (isinstance(j, int) and j == FT - 1):
                    hidden(j + 1, 1 - par)
                if not (isinstance(j, int) and j + 2 >= FT):
                    for which in range(3):
                        split(j + 2, par, which)
            walk(pool, start, body)


def _constants():
    import numpy as np
    bf = mybir.dt.np(BF16)

    def parts(v):
        v = np.asarray(v, np.float32)
        p0 = v.astype(bf)
        p1 = (v - p0.astype(np.float32)).astype(bf)
        return [p0, p1, (v - p0.astype(np.float32) - p1.astype(np.float32)).astype(bf)]

    ident = np.eye(P, dtype=np.float32)
    masku = np.where(np.arange(P)[None, :] > np.arange(P)[:, None], -1e30, 0.0).astype(np.float32)
    start = 2.0 ** (-2.0 ** (-(np.log2(H0) - 3)))
    slopes = np.array([start ** (i + 1) for i in range(H0)], dtype=np.float32)
    inner = (np.arange(S) % P).astype(np.float32)
    qaux = np.zeros((K_ROWS - AUX, H0, S), bf)
    for i, p in enumerate(parts(slopes)):
        qaux[i] = p[:, None]
        qaux[3 + i] = p[:, None]
    for i, p in enumerate(parts(-slopes[:, None] * inner[None, :])):
        qaux[6 + i] = p
    kaux = np.zeros((T_ROWS - AUX, tri(ST)), bf)
    for t in range(ST):
        k = np.arange((t + 1) * P)
        kaux[0:3, tri(t):tri(t + 1)] = (P * (k // P - t)).astype(bf)
        kaux[3:6, tri(t):tri(t + 1)] = (k % P).astype(bf)
        kaux[6:, tri(t):tri(t + 1)] = 1.0
    sel = np.zeros((P, 8, 3, AUX), bf)
    for m in range(AUX):
        for h in range(8):
            sel[HD0 * h + m % HD0, h, QPARTS[m // HD0], m] = 1.0
    inv_freq = (1.0 / 10000.0 ** (np.arange(0, HD1, 2, dtype=np.float32) / np.float32(HD1))).astype(np.float32)
    angle = np.arange(S, dtype=np.float32)[None, :] * np.concatenate([inv_freq, inv_freq])[:, None]
    cos, sin = np.cos(angle).astype(np.float32), np.sin(angle).astype(np.float32)
    sin[HD1 // 2:] *= -1.0
    pos = np.arange(P)
    key_scale = np.where(pos < 35, 0.5, np.where(pos < 35 + 72, 1.5, 1.0)).astype(np.float32)
    kscale = np.tile(key_scale[None, :], (P, 1))
    tscale = np.where(pos[:, None] >= 35 + 72, key_scale[None, :], 1.0).astype(np.float32)
    return {"cos": cos, "sin": sin, "kscale": kscale, "tscale": tscale, "identf": ident, "identb": ident.astype(bf), "masku": masku.astype(bf), "sel": sel, "qaux": qaux, "kaux": kaux}


def kernel(**inputs):
    import numpy as np
    import concourse.bacc as _bacc
    from concourse.bass_utils import run_bass_kernel_spmd as _run

    nc = _bacc.Bacc("TRN2", target_bir_lowering=False, num_devices=1)
    host = {k: np.asarray(v) for k, v in inputs.items()}
    laid = {
        "x": host["L0_attn_hidden_states"].reshape(S, D),
        "wq0": host["L0_attn_Wq"], "wkv0": host["L0_attn_Wkv"], "wo0": host["L0_attn_Wo"],
        "qw": host["L0_ffn_qweight"], "lut4": host["L0_ffn_lut4"], "lut8": host["L0_ffn_lut8"], "bias": host["L0_ffn_bias"],
    }
    wq, wk, wv = (host[f"L1_attn_w{n}"] for n in "qkv")
    def chunks(w, heads):
        return w.reshape(KV1, heads, HD1, DT, P).transpose(0, 1, 4, 3, 2).reshape(KV1, heads, P, BLK)

    laid["w1"] = np.concatenate([chunks(wk, 1), chunks(wv, 1), chunks(wq, G1)], axis=1)
    laid["wo1"] = host["L1_attn_wo"].T.reshape(KV1, G1, HD1, D)
    cut = (FT - 1) * P
    for name in ("gate", "up"):
        w = host[f"L1_ffn_{name}_w"]
        laid[name + "_main"] = w[:cut].reshape(FT - 1, P, DT, P).transpose(0, 3, 2, 1).reshape(FT - 1, P, BLK)
        laid[name + "_last"] = w[cut:].reshape(FLAST, DT, P).transpose(2, 1, 0).reshape(P, DT * FLAST)
    down = host["L1_ffn_down_w"].T
    laid["down_main"], laid["down_last"] = down[:cut].reshape(FT - 1, P, D), down[cut:]
    for name in ("gate", "up", "down"):
        laid[name + "_a"], laid[name + "_b"] = host[f"L1_ffn_{name}_a"].T, host[f"L1_ffn_{name}_b"].T
    laid.update(_constants())
    arrays, aps = {}, {}
    for name, v in laid.items():
        v = np.ascontiguousarray(v)
        arrays[f"in_{name}"] = v
        aps[name] = nc.dram_tensor(f"in_{name}", v.shape, mybir.dt.from_np(v.dtype), kind="ExternalInput").ap()
    aps["out"] = nc.dram_tensor("out_0", (S, D), F32, kind="ExternalOutput").ap()
    build(nc, aps)
    r = _run(nc, [arrays], core_ids=[0])
    return r.results[0]["out_0"].reshape(1, S, D)
```

```python
from contextlib import ExitStack

import concourse.bass as bass
from concourse import mybir

ALU = mybir.AluOpType
ACT = mybir.ActivationFunctionType
AX = mybir.AxisListType
F32 = mybir.dt.float32
F32R = mybir.dt.float32r
BF16 = mybir.dt.bfloat16
I32 = mybir.dt.int32

P = 128
S, D = 1024, 512
ST, DT, BLK = S // P, D // P, 512
NB = S // BLK
EARLY = 6
EPS = 1e-5

H0, HD0 = 32, 16
HG0 = H0 // 4
AUX, K_ROWS, T_ROWS = 112, 121, 124
QPARTS = (0, 1, 0, 1, 0, 1, 2)
KPARTS = (0, 0, 1, 1, 2, 2, 0)
PT0 = 4
CODES_AT = (1, 1, 2, 2, 2, 2, 1, 5)
NPLANE, WORDS, CODES_L, CODES_H = 8, 16, 16, 256
CUT = D * (D // P) // HG0
EST_T = 64.0

H1, KV1, HD1 = 32, 8, 128
G1 = H1 // KV1
FH, RANK = 1376, 16
FT = -(-FH // P)
FLAST = FH - (FT - 1) * P
RS, RROWS = 32, 96


class Count:

    def __init__(self, sem):
        self.sem, self.n = sem, 0

    def inc(self, ins, by=1):
        ins.then_inc(self.sem, by)
        self.n += by
        return self.n


def products(pe, out, left, right, first, last):
    (lh, ll), (rh, rl) = left, right
    pe.matmul(out, lh, rh, start=first, stop=False)
    pe.matmul(out, lh, rl, start=False, stop=False)
    return pe.matmul(out, ll, rh, start=False, stop=last)


def build(nc, a):
    ctx = ExitStack()
    with ctx:
        def sb(name, shape, dt):
            return ctx.enter_context(nc.sbuf_tensor(name, shape, dt))

        keep = {
            "resid": sb("resid", [P, ST, D], F32),
            "xth": sb("xth", [P, DT, S], F32R),
            "xtl": sb("xtl", [P, DT, S], F32R),
            "identf": sb("identf", [P, P], F32),
            "identb": sb("identb", [P, P], BF16),
            "masku": sb("masku", [P, P], BF16),
            "stats": sb("stats", [P, ST, 6], F32),
        }
        layer0(nc, a, keep)
        keep["raw"] = sb("raw2", [P, 6, BLK], F32)
        keep["araw"] = sb("araw", [P, 2 * DT + FT, RANK], F32)
        layer1(nc, a, keep)
        gated(nc, a, keep)



class Norm:

    def __init__(self, nc, ctx, keep, name, xn, bank):
        def sb(n, shape, dt=F32):
            return ctx.enter_context(nc.sbuf_tensor(name + n, shape, dt))

        def sem(n):
            return ctx.enter_context(nc.semaphore(name + n))

        self.x, self.xn, self.bank = keep["resid"], xn, bank
        self.xth, self.xtl, self.identf = keep["xth"], keep["xtl"], keep["identf"]
        self.stats, self.mv = keep["stats"], sb("mv", [P, ST, 2])
        self.veps, self.sd, self.r = sb("veps", [P, ST]), sb("sd", [P, ST]), sb("r", [P, ST])
        self.t, self.rstd = sb("t", [P, ST]), self.r
        self.step = sem("norm_step")
        self.veps_ready, self.sd_ready = sem("veps_ready"), sem("sd_ready")
        self.xn_ready, self.turned = sem("xn_ready"), sem("turned")
        self.high_ready, self.low_ready = sem("high_ready"), sem("low_ready")

    def vector(self, nc, dve, arrived, meanwhile=lambda: None):
        step = Count(self.step)
        for st in range(ST):
            if arrived:
                arrived(dve, st)
                n = step.inc(nc.vector.bn_stats(self.stats[:, st, :], self.x[:, st, :]))
        for st in range(ST):
            if arrived:
                dve.wait_ge(self.step, st + 1)
            n = step.inc(nc.vector.bn_aggr(self.mv[:, st, :], self.stats[:, st, :]))
        dve.wait_ge(self.step, n)
        nc.vector.tensor_scalar(self.veps[:], self.mv[:, :, 1], EPS, None, ALU.add).then_inc(self.veps_ready, 1)
        meanwhile()
        dve.wait_ge(self.sd_ready, 1)
        n = step.inc(nc.vector.reciprocal(self.r[:], self.sd[:]))
        dve.wait_ge(self.step, n)
        n = step.inc(nc.vector.tensor_tensor(self.t[:], self.r[:], self.r[:], ALU.mult))
        dve.wait_ge(self.step, n)
        n = step.inc(nc.vector.tensor_tensor(self.t[:], self.t[:], self.veps[:], ALU.mult))
        dve.wait_ge(self.step, n)
        n = step.inc(nc.vector.tensor_scalar(self.t[:], self.t[:], -0.5, 1.5, ALU.mult, ALU.add))
        dve.wait_ge(self.step, n)
        n = step.inc(nc.vector.tensor_tensor(self.rstd[:], self.r[:], self.t[:], ALU.mult))
        dve.wait_ge(self.step, n)

        def low(st):
            dve.wait_ge(self.turned, st + 1)
            dve.wait_ge(self.high_ready, st + 1)
            nc.vector.tensor_tensor(self.xtl[:, :, st * P:(st + 1) * P], self.bank(st).rearrange("p (c s) -> p c s", c=DT),
                                    self.xth[:, :, st * P:(st + 1) * P].bitcast(F32), ALU.subtract).then_inc(self.low_ready, 1)

        for st in range(ST):
            nc.vector.tensor_scalar(self.xn[:, st, :], self.x[:, st, :], self.mv[:, st, 0:1], self.rstd[:, st:st + 1],
                                    ALU.subtract, ALU.mult).then_inc(self.xn_ready, 1)
            if st >= 2:
                low(st - 2)
        low(ST - 2)
        low(ST - 1)

    def tensor(self, nc, pe, tiles):
        for st in tiles:
            pe.wait_ge(self.xn_ready, st + 1)
            for c in range(DT):
                last = nc.tensor.transpose(self.bank(st)[:, c * P:(c + 1) * P], self.xn[:, st, c * P:(c + 1) * P], self.identf[:])
            last.then_inc(self.turned, 1)

    def scalar_sqrt(self, nc, act):
        act.wait_ge(self.veps_ready, 1)
        nc.scalar.activation(self.sd[:], self.veps[:], ACT.Sqrt).then_inc(self.sd_ready, 1)

    def scalar_high(self, nc, act):
        for st in range(ST):
            act.wait_ge(self.turned, st + 1)
            nc.scalar.activation(self.xth[:, :, st * P:(st + 1) * P], self.bank(st).rearrange("p (c s) -> p c s", c=DT),
                                 ACT.Copy).then_inc(self.high_ready, 1)



def tri(t):
    return P * t * (t + 1) // 2


def interleave(main, side):
    out, at = [], 0
    for i, step in enumerate(main):
        out.append(step)
        want = (i + 1) * len(side) // len(main)
        out += side[at:want]
        at = want
    return out


def layer0(nc, a, keep):
    ctx = ExitStack()
    with ctx:
        def sb(name, shape, dt=F32):
            return ctx.enter_context(nc.sbuf_tensor(name, shape, dt))

        def sem(name):
            return ctx.enter_context(nc.semaphore(name))

        resid, xth, xtl = keep["resid"], keep["xth"], keep["xtl"]
        identf, identb, masku = keep["identf"], keep["identb"], keep["masku"]
        ps = ctx.enter_context(nc.psum_tensor("ps0", [P, 8, 512], F32))

        def bank(b):
            return ps[:, b % 8, :]

        xn = sb("xn0", [P, ST, D])
        bits = xn[:, 0:DT, :].rearrange("p c n -> p (c n)").bitcast(I32)
        woraw = xn[:, DT:2 * DT, :]
        norm = Norm(nc, ctx, keep, "l0_", xn, bank)
        esq, enorm, maskf, masks = sb("esq", [P, ST]), sb("enorm", [P, ST]), sb("maskf", [P, 1]), sb("masks", [P, ST], I32)
        flag = sb("flag", [1, 1], I32)
        credit = sb("credit", [1, 1])
        qstack = sb("qstack", [P, H0, S], BF16)
        kstack = sb("kstack", [P, tri(ST)], BF16)
        wqh, wql = sb("wqh", [P, DT, D], F32R), sb("wql", [P, DT, D], F32R)
        wlh, wll = wqh, wql
        wl = sb("wl", [P, DT, D])
        vaug = sb("vaug", [P, ST, 32])
        negm = sb("negm", [P, 2, H0])
        mrows = sb("mrows", [H0, 3, P], BF16)
        acc_sb, rden = sb("acc_sb", [P, P]), sb("rden", [P, 4])
        biasb = sb("biasb", [P, D])
        mrest = biasb[0:H0, 0:P]
        qw = sb("qw", [P, NPLANE, DT, WORDS], I32)
        lutl = sb("lutl", [P, DT, CODES_L])
        idx = sb("idx", [P, DT * D], BF16)
        onehot = sb("onehot", [P, 2, CUT])
        lut2 = sb("lut2", [P, CODES_L, HG0])
        with ExitStack() as early:
            def sbe(name, shape, dt=F32):
                return early.enter_context(nc.sbuf_tensor(name, shape, dt))
            wkv = sbe("wkv", [P, DT, 2 * HD0])
            vrows = sbe("vrows", [P, S])
            wkh, wkl = sbe("wkh", [P, DT, P], F32R), sbe("wkl", [P, DT, P], F32R)
            rest = sbe("rest", [P, 2, BLK])
            parts_sb = [sbe(f"part{i}", [P, 2, S], BF16) for i in range(3)]
            sel = sbe("sel", [P, 8, 3, AUX], BF16)
        with ExitStack() as late:
            def sbl(name, shape, dt=F32):
                return late.enter_context(nc.sbuf_tensor(name, shape, dt))
            woh, wol = sbl("woh", [P, DT, D], F32R), sbl("wol", [P, DT, D], F32R)
            atth, attl = sbl("atth", [P, 2, DT, P], F32R), sbl("attl", [P, 2, DT, P], F32R)
            pt = sbl("pt0", [P, PT0, BLK])
        luth = qstack[:, 0:2, :].rearrange("p h s -> p (h s)").bitcast(F32).rearrange("p (c k) -> p c k", c=DT)
        with ExitStack() as rare:
            ridx = rare.enter_context(nc.sbuf_tensor("ridx", [P, DT * D], F32))
            rbits = rare.enter_context(nc.sbuf_tensor("rbits", [P, DT * D], I32))
            rhot = rare.enter_context(nc.sbuf_tensor("rhot", [P, D], F32))
            rsum = rare.enter_context(nc.sbuf_tensor("rsum", [P, D], F32))

        x_in = [sem(f"x_in{i}") for i in range(4)]
        const_in, wkv_in, wq_in, wo_in = sem("const_in"), sem("wkv_in"), sem("wq_in"), sem("wo_in")
        aux_in, qw_in, lut_in, bias_in = sem("aux_in"), sem("qw_in"), sem("lut_in"), sem("bias_in")
        esq_ready, mask_ready = sem("esq_ready"), sem("mask_ready")
        wk_high, wk_low, wq_high, wq_low, wo_high, wo_low = (sem(n) for n in ("wk_high", "wk_low", "wq_high", "wq_low", "wo_high", "wo_low"))
        k_ps, v_ps, q_ps = sem("k_ps"), sem("v_ps"), sem("q_ps")
        kq_part = [sem(f"kq_part{i}") for i in range(3)]
        kq_rest = sem("kq_rest")
        v_rows, v_ready, v_init = sem("v_rows"), sem("v_ready"), sem("v_init")
        sel_in, lut2_made, k_placed = sem("sel_in"), sem("lut2_made"), sem("k_placed")
        place_filled, placed = sem("place_filled"), [sem("placed_act"), sem("placed_dve")]
        m_filled, m_free = sem("m_filled"), sem("m_free")
        m_turned, m_split, m_rows = sem("m_turned"), sem("m_split"), sem("m_rows")
        t_filled, exp_done, av_done = sem("t_filled"), sem("exp_done"), sem("av_done")
        acc_copied, acc_turned, norm_step, head_done = (sem(n) for n in ("acc_copied", "acc_turned", "norm_step", "head_done"))
        bit_step, idx_step, hot_made, wl_step, waited = (sem(n) for n in ("bit_step", "idx_step", "hot_made", "wl_step", "waited0"))
        wl_turned, wl_high, wl_low = sem("wl_turned"), sem("wl_high"), sem("wl_low")
        att_turned, att_high, att_low = sem("att_turned"), sem("att_high"), sem("att_low")
        o_ps, y_ps, xb_ready, t_ready, x1_ready = (sem(n) for n in ("o_ps", "y_ps", "xb_ready", "t_ready", "x1_ready"))
        any_turned, any_step, flag_ready = sem("any_turned"), sem("any_step"), sem("flag_ready")
        rare_step, rare_w, rare_turned, rare_split, rare_y, rare_used = (
            sem(n) for n in ("rare_step", "rare_w", "rare_turned", "rare_split", "rare_y", "rare_used"))
        luth_in = sem("luth_in")

        block = ctx.enter_context(nc.Block())

        K_PLACES = 4 + ST - 1
        QT_PLACES = 8 * NB
        MCREDIT = 4

        def m_slots(t):
            return 4 if (t + 1) * P <= BLK else 2

        def m_bank(t, j):
            return j % m_slots(t) * (4 // m_slots(t))

        TB = (4, 5, 0, 1)
        ACCB, TURNB = 6, 7

        def parts_free(eng, n):
            if n // NB == 1:
                eng.wait_ge(k_placed, K_PLACES)
            elif n // NB >= 2:
                eng.wait_ge(place_filled, QT_PLACES * (n // NB - 1))

        def q_bank(n):
            return ps[:, 3 + n % 4, :]

        def place_bank(i):
            return ps[0:AUX, (7, 0, 1, 2)[i % 4], :]

        def all_placed(eng):
            for sem_placed in placed:
                eng.wait_ge(sem_placed, QT_PLACES * 4 // 2)

        def unit(t, hg, kt):
            return hg * (t + 1) + (HG0 * t * (t + 1) // 2 + kt)

        LATE = ST - 1

        def lead(t):
            return min(t + 1, 3 if t >= LATE else 2)

        def place(t, kt, odd):
            return kt % 4 if t >= LATE else (odd * (t + 1) + kt) % 2

        def distance(t, hg, kt):
            return 2 if t < LATE or (isinstance(hg, int) and hg == 0 and kt < 2) else 4

        def groups(eng, t, step):
            step(t, 0, 0, (t, 1, 1))
            with eng.Fori(0, 2) as pair:
                step(t, pair * 2 + 1, 1, (t, pair * 2 + 2, 0))
                step(t, pair * 2 + 2, 0, (t, pair * 2 + 3, 1))
            for hg in range(5, HG0 - 1):
                step(t, hg, hg % 2, (t, hg + 1, 1 - hg % 2))
            step(t, HG0 - 1, 1, (t + 1, 0, 0) if t + 1 < ST else None)

        MORE = 2

        def maxima_beside(t, hg):
            if isinstance(hg, int) and hg >= HG0 - MORE:
                return (t + 2, hg - (HG0 - MORE)) if t + 2 < ST else None
            return (t + 1, hg + MORE) if t + 1 < ST else None

        def turns_maxima(t, hg):
            return isinstance(hg, int) and hg == HG0 - MORE and t + 1 < ST


        @block.sync
        def _(sp):
            for i in range(4):
                sp.dma_start(resid[:, 2 * i:2 * i + 2, :], a["x"].rearrange("(t p) d -> p t d", p=P)[:, 2 * i:2 * i + 2, :]).then_inc(x_in[i], 16)
            sp.dma_start(identf[:], a["identf"]).then_inc(const_in, 16)
            sp.dma_start(identb[:], a["identb"]).then_inc(const_in, 16)
            sp.dma_start(masku[:], a["masku"]).then_inc(const_in, 16)
            sp.dma_start(wkv[:], a["wkv0"].rearrange("(c p) n -> p c n", p=P)).then_inc(wkv_in, 16)
            sp.dma_start(wl[:], a["wq0"].rearrange("(c p) n -> p c n", p=P)).then_inc(wq_in, 16)
            sp.dma_start(qw[:], a["qw"].rearrange("l (c p) w -> p l c w", p=P)).then_inc(qw_in, 16)
            sp.dma_start(lutl[:], a["lut4"].rearrange("(c p) k -> p c k", p=P)).then_inc(lut_in, 16)
            sp.dma_start(sel[:], a["sel"]).then_inc(sel_in, 16)
            sp.dma_start(qstack[AUX:K_ROWS, :, :], a["qaux"]).then_inc(aux_in, 16)
            sp.dma_start(kstack[AUX:T_ROWS, :], a["kaux"]).then_inc(aux_in, 16)
            sp.dma_start(biasb[:], a["bias"].partition_broadcast(P)).then_inc(bias_in, 16)
            sp.wait_ge(norm.turned, ST)
            sp.wait_ge(esq_ready, ST)
            sp.dma_start(woraw, a["wo0"].rearrange("(c p) n -> p c n", p=P)).then_inc(wo_in, 16)
            for t in range(ST):
                sp.wait_ge(m_split, 3 * t + 3)
                if t:
                    sp.wait_ge(m_rows, 48 * t)
                for i in range(3):
                    sp.dma_start(qstack[K_ROWS + i:K_ROWS + i + 1, :, t * P:(t + 1) * P], mrows[:, i, :]).then_inc(m_rows, 16)
            sp.wait_ge(head_done, HG0 * ST + 1)
            sp.dma_start(luth, a["lut8"].rearrange("(c p) k -> p c k", p=P)).then_inc(luth_in, 16)
            sp.wait_ge(luth_in, 16)

        @block.tensor
        def _(pe):
            pe.wait_ge(const_in, 48)
            norm.tensor(nc, pe, range(ST))

            pe.wait_ge(wk_low, 2)
            for b in range(NB):
                pe.wait_ge(norm.low_ready, ST // NB * (b + 1))
                for c in range(DT):
                    last = products(pe, bank(b), (wkh[:, c, :], wkl[:, c, :]),
                                    (xth[:, c, b * BLK:(b + 1) * BLK], xtl[:, c, b * BLK:(b + 1) * BLK]), c == 0, c == DT - 1)
                last.then_inc(k_ps, 1)
            pe.wait_ge(wq_low, DT)
            def project_q(qt):
                for n in (NB * qt, NB * qt + 1):
                    b = n % NB
                    if n >= 4:
                        pe.wait_ge(kq_rest, NB + n - 3)
                    for c in range(DT):
                        last = products(pe, q_bank(n), (wqh[:, c, qt * P:(qt + 1) * P], wql[:, c, qt * P:(qt + 1) * P]),
                                        (xth[:, c, b * BLK:(b + 1) * BLK], xtl[:, c, b * BLK:(b + 1) * BLK]), c == 0, c == DT - 1)
                    last.then_inc(q_ps, 1)

            def place_q(qt):
                for i in range(3):
                    pe.wait_ge(kq_part[i], NB + NB * (qt + 1))
                for h in range(8):
                    for b in range(NB):
                        i = QT_PLACES * qt + NB * h + b
                        if i == 1:
                            pe.wait_ge(kq_rest, NB)
                            pe.wait_ge(v_rows, NB)
                        if i == 3:
                            pe.wait_ge(v_ready, 1)
                        if i >= 4:
                            pe.wait_ge(placed[b], (i - 4) // NB + 1)
                        for part in range(3):
                            last = pe.matmul(place_bank(i), sel[:, h, part, :], parts_sb[part][:, (qt + 1) % 2, b * BLK:(b + 1) * BLK],
                                             start=part == 0, stop=part == 2)
                        last.then_inc(place_filled, 1)

            project_q(0)
            for st in range(ST):
                pe.wait_ge(v_rows, st // (ST // NB) + 1)
                last = nc.tensor.transpose(ps[:, 2, st * 32:(st + 1) * 32], vrows[96:128, st * P:(st + 1) * P], identf[96:128, 96:128])
            last.then_inc(v_ps, 1)
            pe.wait_ge(sel_in, 16)
            for qt in range(4):
                if qt < 3:
                    project_q(qt + 1)
                place_q(qt)

            pe.wait_ge(mask_ready, 1)
            pe.wait_ge(kq_rest, NB + 4 * NB)
            nc.tensor.transpose(ps[0:1, 4, 0:P], maskf[:], identf[:]).then_inc(any_turned, 1)

            def m_scores(t, h, j):
                pe.wait_ge(m_free, h + (t * H0 + MCREDIT + 1 - m_slots(t)))
                b0 = m_bank(t, j)
                width = (t + 1) * P
                for c0 in range(0, width, 512):
                    w = min(512, width - c0)
                    diag = c0 + w == width
                    pe.matmul(ps[:, b0 + c0 // 512, 0:w], qstack[0:K_ROWS, h, t * P:(t + 1) * P],
                              kstack[0:K_ROWS, tri(t) + c0:tri(t) + c0 + w], start=True, stop=not diag)
                d = t * P
                last = pe.matmul(ps[:, b0 + d // 512, d % 512:d % 512 + P], identb[:], masku[:], start=False, stop=True)
                last.then_inc(m_filled, 1)

            def m_turn(t):
                pe.wait_ge(m_free, H0 * (t + 1) + MCREDIT)
                if t:
                    pe.wait_ge(m_split, 3 * t)
                    pe.wait_ge(head_done, HG0 * t - MORE)
                nc.tensor.transpose(ps[0:H0, TURNB, 0:P], negm[:, t % 2, :], identf[:]).then_inc(m_turned, 1)

            def t_scores(t, hg, kt, odd):
                n = unit(t, hg, kt)
                if t == LATE and isinstance(hg, int) and hg == 0 and kt in (2, 3):
                    pe.wait_ge(m_free, H0 * ST + MCREDIT)
                elif not (isinstance(n, int) and n < 2):
                    pe.wait_ge(exp_done, n + 1 - distance(t, hg, kt))
                if t and isinstance(hg, int) and hg == 0 and kt == 0:
                    pe.wait_ge(m_rows, 48 * (t + 1))
                out = ps[:, TB[place(t, kt, odd)], :].rearrange("p (h q) -> p h q", h=4)
                q = qstack[0:T_ROWS, bass.ds(hg * 4, 4), t * P:(t + 1) * P]
                last = pe.matmul(out, kstack[0:T_ROWS, tri(t) + kt * P:tri(t) + (kt + 1) * P], q, start=True, stop=kt != t)
                if kt == t:
                    last = pe.matmul(out, masku[:],
                                     identb[:].unsqueeze(1).to_broadcast([P, 4, P]), start=False, stop=True)
                last.then_inc(t_filled, 1)

            def values(t, hg, kt, odd):
                if kt == 0 and not (t == 0 and isinstance(hg, int) and hg == 0):
                    pe.wait_ge(acc_copied, hg + HG0 * t)
                pe.wait_ge(exp_done, unit(t, hg, kt + 1))
                for j in range(4):
                    last = pe.matmul(ps[32 * j:32 * j + 32, ACCB, 0:P], vaug[:, kt, :],
                                     pt[:, place(t, kt, odd), j * P:(j + 1) * P], start=kt == 0, stop=kt == t)
                last.then_inc(av_done, 1)

            def unit_group(t, hg, odd, following):
                head = isinstance(hg, int) and hg == 0
                ahead = [lambda k=k: t_scores(t, hg, k, odd) for k in range(lead(t), t + 1)]
                if following:
                    nt, nhg, nodd = following
                    ahead += [lambda k=k: t_scores(nt, nhg, k, nodd) for k in range(lead(nt))]
                main = []
                for k in range(t + 1):
                    if k == t and following and t < LATE:
                        main.append(ahead.pop(0))
                    main.append(lambda k=k: values(t, hg, k, odd))
                    if ahead and (k < t - 1 or t >= LATE):
                        main.append(ahead.pop(0))
                main += ahead
                beside = maxima_beside(t, hg)
                side = [lambda j=j: m_scores(beside[0], beside[1] * 4 + j, j) for j in range(4)] if beside else []
                turned_here = turns_maxima(t, hg)
                if turned_here:
                    side.insert(min(1, len(side)), lambda: m_turn(t + 1))
                steps, at = [], 0
                for i, s in enumerate(main):
                    while at < len(side) and at * len(main) // len(side) <= i:
                        steps.append(side[at])
                        at += 1
                    steps.append(s)
                if not (t == 0 and head):
                    after = steps.index(side[min(1, len(side) - 1)]) + 1 if turned_here else 3
                    steps.insert(min(after, len(steps) - 1), lambda: turn(t, hg))
                for step in steps:
                    step()

            def turn(t, hg):
                u = hg + (HG0 * t - 1)
                pe.wait_ge(acc_copied, u + 1)
                if not (isinstance(u, int) and u == 0):
                    pe.wait_ge(head_done, u + 1)
                pe.wait_ge(m_split, 3 * min(t + (2 if isinstance(hg, int) and hg >= HG0 - MORE else 1), ST))
                nc.tensor.transpose(ps[:, TURNB, 0:P], acc_sb[:], identf[:]).then_inc(acc_turned, 1)

            pe.wait_ge(aux_in, 32)
            pe.wait_ge(k_placed, K_PLACES)
            all_placed(pe)
            with pe.Fori(0, HG0) as hg:
                for j in range(4):
                    m_scores(0, hg * 4 + j, j)
            m_turn(0)
            for h in range(4 * MORE):
                m_scores(1, h, h % 4)
            pe.wait_ge(v_ready, 1)
            pe.wait_ge(flag_ready, 1)
            pe.wait_ge(m_rows, 48)
            t_scores(0, 0, 0, 0)
            for t in range(ST):
                groups(pe, t, unit_group)
            turn(ST, 0)

            pe.wait_ge(wl_step, 1 + CODES_L * HG0)
            for ot in range(DT):
                for c in range(DT):
                    last = nc.tensor.transpose(ps[:, c, ot * P:(ot + 1) * P], wl[:, ot, c * P:(c + 1) * P], identf[:])
            last.then_inc(wl_turned, 1)

            def turn_att(t):
                pe.wait_ge(head_done, HG0 * ST + 1)
                if t >= 2:
                    pe.wait_ge(att_low, t - 1)
                for c in range(DT):
                    last = nc.tensor.transpose(ps[:, 6 + t % 2, c * P:(c + 1) * P], xn[:, t, c * P:(c + 1) * P], identf[:])
                last.then_inc(att_turned, 1)

            turn_att(0)
            for t in range(ST):
                if t >= 2:
                    pe.wait_ge(x1_ready, t - 1)
                for c in range(DT):
                    if t == 0:
                        pe.wait_ge(wl_low, c + 1)
                    last = products(pe, ps[:, 4 + t % 2, :], (xth[:, c, t * P:(t + 1) * P], xtl[:, c, t * P:(t + 1) * P]),
                                    (wlh[:, c, :], wll[:, c, :]), c == 0, c == DT - 1)
                last.then_inc(y_ps, 1)
                if t + 1 < ST:
                    turn_att(t + 1)
                pe.wait_ge(att_low, t + 1)
                pe.wait_ge(wo_low, DT)
                for c in range(DT):
                    last = products(pe, ps[:, 2 + t % 2, :], (atth[:, t % 2, c, :], attl[:, t % 2, c, :]),
                                    (woh[:, c, :], wol[:, c, :]), c == 0, c == DT - 1)
                last.then_inc(o_ps, 1)

            some = pe.value_load(flag[0:1, 0:1], min_val=0, max_val=1)
            with pe.If(some > 0):
                pe.wait_ge(rare_w, 1)
                for ot in range(DT):
                    for c in range(DT):
                        last = nc.tensor.transpose(ps[:, c, ot * P:(ot + 1) * P], wl[:, ot, c * P:(c + 1) * P], identf[:])
                last.then_inc(rare_turned, 1)
                pe.wait_ge(rare_split, 2 * DT)
                for t in range(ST):
                    if t >= 2:
                        pe.wait_ge(rare_used, 2 * t - 2)
                    for c in range(DT):
                        last = products(pe, ps[:, 6 + t % 2, :], (xth[:, c, t * P:(t + 1) * P], xtl[:, c, t * P:(t + 1) * P]),
                                        (wlh[:, c, :], wll[:, c, :]), c == 0, c == DT - 1)
                    last.then_inc(rare_y, 1)

        @block.scalar
        def _(act):
            act.wait_ge(wkv_in, 16)
            nc.scalar.activation(wkh[:, :, 0:AUX].rearrange("p c (r d) -> p c r d", r=7),
                                 wkv[:, :, 0:HD0].unsqueeze(2).to_broadcast([P, DT, 7, HD0]), ACT.Copy).then_inc(wk_high, 1)
            nc.scalar.activation(wkh[:, :, AUX:P], wkv[:, :, HD0:2 * HD0], ACT.Copy).then_inc(wk_high, 1)
            norm.scalar_sqrt(nc, act)
            act.wait_ge(wq_in, 16)
            for c in range(DT):
                nc.scalar.activation(wqh[:, c, :], wl[:, c, :], ACT.Copy).then_inc(wq_high, 1)
            norm.scalar_high(nc, act)

            for st in range(ST):
                act.wait_ge(norm.xn_ready, st + 1)
                if st:
                    act.wait_ge(esq_ready, st)
                nc.scalar.activation(rest[:, 0, :], xn[:, st, :], ACT.Square, accum_out=esq[:, st:st + 1]).then_inc(esq_ready, 1)
            act.wait_ge(esq_ready, ST)
            nc.scalar.activation(enorm[:], esq[:], ACT.Sqrt).then_inc(esq_ready, 1)

            def two_parts(src, scale, n, out0, out1):
                nc.scalar.activation(out0, src, ACT.Copy, scale=scale).then_inc(kq_part[0], 1)
                act.wait_ge(kq_rest, n + 1)
                nc.scalar.activation(out1, rest[:, n % 2, :], ACT.Copy).then_inc(kq_part[1], 1)

            for b in range(NB):
                act.wait_ge(k_ps, b + 1)
                cols = slice(b * BLK, (b + 1) * BLK)
                nc.scalar.activation(vrows[96:128, cols], ps[96:128, b, :], ACT.Copy).then_inc(v_rows, 1)
                two_parts(bank(b), 1.0, b, parts_sb[0][:, 0, cols], parts_sb[1][:, 0, cols])
            def q_parts(qt):
                for n in (NB * qt, NB * qt + 1):
                    act.wait_ge(q_ps, n + 1)
                    cols = slice(n % NB * BLK, (n % NB + 1) * BLK)
                    parts_free(act, n)
                    two_parts(q_bank(n), HD0 ** -0.5, NB + n, parts_sb[0][:, (qt + 1) % 2, cols], parts_sb[1][:, (qt + 1) % 2, cols])

            q_parts(0)
            act.wait_ge(v_ps, 1)
            act.wait_ge(v_init, 2)
            nc.scalar.activation(vaug[:, :, 0:HD0], ps[:, 2, 0:ST * 32].rearrange("p (t d) -> p t d", t=ST)[:, :, HD0:32],
                                 ACT.Copy).then_inc(v_ready, 1)
            for qt in range(4):
                if qt < 3:
                    q_parts(qt + 1)
                for h in range(8):
                    i = QT_PLACES * qt + NB * h
                    act.wait_ge(place_filled, i + 1)
                    nc.scalar.activation(qstack[0:AUX, 8 * qt + h, 0:BLK], place_bank(i), ACT.Copy).then_inc(placed[0], 1)

            def exponential(t, hg, kt, odd):
                n = unit(t, hg, kt)
                act.wait_ge(t_filled, n + 1)
                at = place(t, kt, odd)
                if not (isinstance(n, int) and n < 2):
                    act.wait_ge(av_done, n + 1 - distance(t, hg, kt))
                nc.scalar.activation(pt[:, at, :], ps[:, TB[at], :], ACT.Exp).then_inc(exp_done, 1)

            def unit_group(t, hg, odd, following):
                for k in range(lead(t), t + 1):
                    exponential(t, hg, k, odd)
                if following:
                    nt, nhg, nodd = following
                    before = max(1, lead(nt) - 1)
                    for k in range(before):
                        exponential(nt, nhg, k, nodd)
                act.wait_ge(av_done, unit(t, hg, t + 1))
                if not (t == 0 and isinstance(hg, int) and hg == 0):
                    act.wait_ge(acc_turned, hg + HG0 * t)
                nc.scalar.activation(acc_sb[:], ps[:, ACCB, 0:P], ACT.Copy).then_inc(acc_copied, 1)
                if following:
                    for k in range(before, lead(nt)):
                        exponential(nt, nhg, k, nodd)

            all_placed(act)
            exponential(0, 0, 0, 0)
            for t in range(ST):
                groups(act, t, unit_group)
                if t == 1:
                    act.wait_ge(wo_in, 16)
                    for c in range(DT):
                        nc.scalar.activation(woh[:, c, :], woraw[:, c, :], ACT.Copy).then_inc(wo_high, 1)
            act.wait_ge(wl_turned, 1)
            for c in range(DT):
                nc.scalar.activation(wlh[:, c, :], bank(c), ACT.Copy).then_inc(wl_high, 1)
            for t in range(ST):
                act.wait_ge(att_turned, t + 1)
                if t >= 2:
                    act.wait_ge(o_ps, t - 1)
                nc.scalar.activation(atth[:, t % 2, :, :], bank(6 + t % 2).rearrange("p (c s) -> p c s", c=DT), ACT.Copy).then_inc(att_high, 1)

        @block.vector
        def _(dve):
            dve.sem_inc(head_done, 1)
            nc.vector.memset(vaug[:], 0.0).then_inc(v_init, 1)
            dve.wait_ge(v_init, 1)
            nc.vector.memset(vaug[:, :, HD0:HD0 + 1], 1.0).then_inc(v_init, 1)
            nc.vector.memset(credit[:, 0:1], 0.0).then_inc(m_free, MCREDIT)
            def split_wkv():
                dve.wait_ge(wk_high, 2)
                nc.vector.tensor_tensor(wkl[:, :, 0:AUX].rearrange("p c (r d) -> p c r d", r=7),
                                        wkv[:, :, 0:HD0].unsqueeze(2).to_broadcast([P, DT, 7, HD0]),
                                        wkh[:, :, 0:AUX].bitcast(F32).rearrange("p c (r d) -> p c r d", r=7), ALU.subtract).then_inc(wk_low, 1)
                nc.vector.tensor_tensor(wkl[:, :, AUX:P], wkv[:, :, HD0:2 * HD0], wkh[:, :, AUX:P].bitcast(F32), ALU.subtract).then_inc(wk_low, 1)

            norm.vector(nc, dve, lambda e, st: e.wait_ge(x_in[st // 2], 16), split_wkv)

            def parts(src, scale, n, part0, part1, part2):
                dve.wait_ge(kq_part[0], n + 1)
                if n >= 2:
                    dve.wait_ge(kq_part[2], n - 1)
                nc.vector.scalar_tensor_tensor(out=rest[:, n % 2, :], in0=src, scalar=scale, in1=part0,
                                               op0=ALU.mult, op1=ALU.subtract).then_inc(kq_rest, 1)
                dve.wait_ge(kq_rest, n + 1)
                dve.wait_ge(kq_part[1], n + 1)
                nc.vector.tensor_tensor(part2, rest[:, n % 2, :], part1, ALU.subtract).then_inc(kq_part[2], 1)

            def take_bits(level, js):
                for j in js:
                    nc.vector.tensor_scalar(bits[:, j:DT * D:32], qw[:, level, :, :].rearrange("p c w -> p (c w)"),
                                            j, 1, ALU.logical_shift_right, ALU.bitwise_and).then_inc(bit_step, 1)

            def add_plane(level):
                dve.wait_ge(bit_step, 32 * (level + 1))
                if level == 0:
                    nc.vector.tensor_copy(idx[:], bits).then_inc(idx_step, 1)
                else:
                    nc.vector.scalar_tensor_tensor(out=idx[:], in0=bits, scalar=float(1 << level),
                                                   in1=idx[:], op0=ALU.mult, op1=ALU.add).then_inc(idx_step, 1)
                dve.wait_ge(idx_step, level + 1)

            dve.wait_ge(qw_in, 16)
            dve.wait_ge(norm.turned, ST)
            dve.wait_ge(esq_ready, ST)
            take_bits(0, range(32))
            add_plane(0)
            for b in range(NB):
                dve.wait_ge(k_ps, b + 1)
                cols = slice(b * BLK, (b + 1) * BLK)
                parts(bank(b), 1.0, b, *(part[:, 0, cols] for part in parts_sb))
            for i in range(3):
                dve.wait_ge(kq_part[i], NB)
            whole = tri(ST - 1)
            for lo, hi in ((0, 32), (32, 64), (64, 96), (96, AUX)):
                part = KPARTS[lo // HD0]
                nc.vector.tensor_copy(kstack[lo:hi, whole:whole + S], parts_sb[part][lo:hi, 0, :]).then_inc(k_placed, 1)
            dve.wait_ge(k_placed, 4)
            for t in range(ST - 1):
                nc.vector.tensor_copy(kstack[0:AUX, tri(t):tri(t + 1)], kstack[0:AUX, whole:whole + (t + 1) * P]).then_inc(k_placed, 1)

            def q_parts(qt):
                for n in (NB * qt, NB * qt + 1):
                    dve.wait_ge(q_ps, n + 1)
                    cols = slice(n % NB * BLK, (n % NB + 1) * BLK)
                    parts_free(dve, n)
                    parts(q_bank(n), HD0 ** -0.5, NB + n, *(part[:, (qt + 1) % 2, cols] for part in parts_sb))

            q_parts(0)
            for qt in range(4):
                if qt < 3:
                    q_parts(qt + 1)
                for h in range(8):
                    i = QT_PLACES * qt + NB * h + 1
                    dve.wait_ge(place_filled, i + 1)
                    nc.vector.tensor_copy(qstack[0:AUX, 8 * qt + h, BLK:S], place_bank(i)).then_inc(placed[1], 1)
                    if qt < 3:
                        take_bits(qt + 1, range(4 * h, 4 * h + 4))
                if qt < 3:
                    add_plane(qt + 1)
            dve.wait_ge(lut_in, 16)
            for half in range(2):
                nc.vector.tensor_copy(lut2[:].rearrange("p c (o i) -> p c o i", i=2)[:, :, :, half], lutl[:].rearrange("p o c -> p c o")).then_inc(lut2_made, 1)
            dve.wait_ge(lut2_made, 2)

            def codes(t, hg):
                n = CODES_AT[t]
                for i in range(n):
                    k = hg * n + (HG0 * sum(CODES_AT[:t]) + i)
                    if not (isinstance(k, int) and k == i):
                        dve.wait_ge(wl_step, k + (1 if i == 0 else 0))
                    c = sum(CODES_AT[:t]) + i
                    part = slice(hg * CUT, (hg + 1) * CUT) if isinstance(hg, int) else bass.ds(hg * CUT, CUT)
                    entry = slice(hg, hg + 1) if isinstance(hg, int) else bass.ds(hg, 1)
                    nc.vector.tensor_scalar(onehot[:, i % 2, :], idx[:, part], float(c), lut2[:, c, entry],
                                            ALU.is_equal, ALU.mult).then_inc(hot_made, 1)

            dve.wait_ge(esq_ready, ST + 1)
            astep = Count(any_step)
            astep.inc(nc.vector.tensor_scalar(masks[:], enorm[:], EST_T, None, ALU.is_gt))
            dve.wait_ge(any_step, 1)
            nc.vector.tensor_reduce(maskf[:], masks[:], AX.X, ALU.max).then_inc(mask_ready, 1)
            dve.wait_ge(any_turned, 1)
            nc.vector.tensor_reduce(flag[:], ps[0:1, 4, 0:P], AX.X, ALU.max).then_inc(flag_ready, 1)

            def head_max(t, h, j):
                n = h + t * H0
                dve.wait_ge(m_filled, n + 1)
                width = (t + 1) * P
                nc.vector.tensor_reduce(negm[:, t % 2, bass.ds(h, 1)], ps[:, m_bank(t, j):m_bank(t, j) + 4 // m_slots(t), :].rearrange("p b c -> p (b c)")[:, 0:width],
                                        AX.X, ALU.max, negate=True).then_inc(m_free, 1)

            def maxima(t, hg, js=range(4)):
                for j in js:
                    head_max(t, hg * 4 + j, j)

            def split_max(t):
                dve.wait_ge(m_turned, t + 1)
                if t:
                    dve.wait_ge(m_rows, 48 * t)
                src = ps[0:H0, TURNB, 0:P]
                nc.vector.tensor_copy(mrows[:, 0, :], src).then_inc(m_split, 1)
                dve.wait_ge(m_split, 3 * t + 1)
                nc.vector.tensor_tensor(mrest, src, mrows[:, 0, :], ALU.subtract).then_inc(any_step, 1)
                dve.wait_ge(any_step, 2 + t)
                nc.vector.tensor_copy(mrows[:, 1, :], mrest).then_inc(m_split, 1)
                dve.wait_ge(m_split, 3 * t + 2)
                nc.vector.tensor_tensor(mrows[:, 2, :], mrest, mrows[:, 1, :], ALU.subtract).then_inc(m_split, 1)

            def normalise(t, hg):
                u = hg + (HG0 * t - 1)
                dve.wait_ge(acc_turned, u + 1)
                src = ps[:, TURNB, 0:P].rearrange("p (h d) -> p h d", h=4)
                nc.vector.reciprocal(rden[:], src[:, :, HD0]).then_inc(norm_step, 1)
                dve.wait_ge(norm_step, u + 1)
                if isinstance(hg, int) and hg == 0:
                    dst = xn[:, t - 1, (H0 - 4) * HD0:H0 * HD0]
                else:
                    dst = xn[:, t, bass.ds(hg * 64 - 64, 64)]
                nc.vector.tensor_tensor(dst.rearrange("p (h d) -> p h d", h=4), src[:, :, 0:HD0],
                                        rden[:].unsqueeze(2).to_broadcast([P, 4, HD0]), ALU.mult).then_inc(head_done, 1)

            dve.wait_ge(xb_ready, ST)
            with dve.Fori(0, HG0) as hg:
                maxima(0, hg)
            split_max(0)
            for hg in range(MORE):
                maxima(1, hg)
            def group(t, hg):
                beside = maxima_beside(t, hg)
                if beside:
                    maxima(*beside, (0,))
                if turns_maxima(t, hg):
                    split_max(t + 1)
                if beside:
                    maxima(*beside, (1, 2, 3))
                if t or not (isinstance(hg, int) and hg == 0):
                    normalise(t, hg)
                codes(t, hg)

            for t in range(ST):
                if t == DT:
                    dve.wait_ge(wo_low, DT)
                group(t, 0)
                with dve.Fori(1, 5) as hg:
                    group(t, hg)
                for hg in range(5, HG0):
                    group(t, hg)
            normalise(ST, 0)

            dve.wait_ge(wl_turned, 1)
            for c in range(DT):
                dve.wait_ge(wl_high, c + 1)
                nc.vector.tensor_tensor(wll[:, c, :], bank(c), wlh[:, c, :].bitcast(F32), ALU.subtract).then_inc(wl_low, 1)

            def next_stats(t):
                dve.wait_ge(x1_ready, t + 1)
                nc.vector.bn_stats(keep["stats"][:, t, :], resid[:, t, :])

            for t in range(ST):
                dve.wait_ge(att_turned, t + 1)
                dve.wait_ge(att_high, t + 1)
                if t >= 2:
                    dve.wait_ge(o_ps, t - 1)
                nc.vector.tensor_tensor(attl[:, t % 2, :, :], bank(6 + t % 2).rearrange("p (c s) -> p c s", c=DT),
                                        atth[:, t % 2, :, :].bitcast(F32), ALU.subtract).then_inc(att_low, 1)
                dve.wait_ge(o_ps, t + 1)
                nc.vector.tensor_tensor(xn[:, t, :], ps[:, 2 + t % 2, :], resid[:, t, :], ALU.add).then_inc(t_ready, 1)
                dve.wait_ge(t_ready, t + 1)
                dve.wait_ge(y_ps, t + 1)
                nc.vector.tensor_tensor(resid[:, t, :], ps[:, 4 + t % 2, :], xn[:, t, :], ALU.add).then_inc(x1_ready, 1)
                if t:
                    next_stats(t - 1)
            next_stats(ST - 1)

            some = dve.value_load(flag[0:1, 0:1], min_val=0, max_val=1)
            with dve.If(some > 0):
                step = Count(rare_step)
                dve.wait_ge(luth_in, 16)
                dve.wait_ge(x1_ready, ST)

                def chained(ins):
                    dve.wait_ge(rare_step, step.inc(ins))

                for level in range(NPLANE):
                    for j in range(32):
                        n = step.inc(nc.vector.tensor_scalar(rbits[:, j:DT * D:32], qw[:, level, :, :].rearrange("p c w -> p (c w)"),
                                                             j, 1, ALU.logical_shift_right, ALU.bitwise_and))
                    dve.wait_ge(rare_step, n)
                    if level == 0:
                        chained(nc.vector.tensor_copy(ridx[:], rbits[:]))
                    else:
                        chained(nc.vector.scalar_tensor_tensor(out=ridx[:], in0=rbits[:], scalar=float(1 << level),
                                                               in1=ridx[:], op0=ALU.mult, op1=ALU.add))
                chained(nc.vector.memset(wl[:], 0.0))
                base, per = step.n, 2 * DT + 1
                with dve.Fori(0, CODES_H) as c:
                    for ot in range(DT):
                        nc.vector.tensor_scalar(rhot[:], ridx[:, ot * D:(ot + 1) * D], 0.0, luth[:, ot, bass.ds(c, 1)],
                                                ALU.is_equal, ALU.mult).then_inc(rare_step, 1)
                        dve.wait_ge(rare_step, c * per + (base + 2 * ot + 1))
                        nc.vector.tensor_tensor(wl[:, ot, :], wl[:, ot, :], rhot[:], ALU.add).then_inc(rare_step, 1)
                        dve.wait_ge(rare_step, c * per + (base + 2 * ot + 2))
                    nc.vector.tensor_scalar(ridx[:], ridx[:], -1.0, None, ALU.add).then_inc(rare_step, 1)
                    dve.wait_ge(rare_step, c * per + (base + per))
                nc.vector.memset(credit[:], 0.0).then_inc(rare_w, 1)
                dve.wait_ge(rare_turned, 1)
                for c in range(DT):
                    nc.vector.tensor_copy(wlh[:, c, :], bank(c)).then_inc(rare_split, 1)
                    dve.wait_ge(rare_split, 2 * c + 1)
                    nc.vector.tensor_tensor(wll[:, c, :], bank(c), wlh[:, c, :].bitcast(F32), ALU.subtract).then_inc(rare_split, 1)
                for t in range(ST):
                    dve.wait_ge(rare_y, t + 1)
                    if t:
                        dve.wait_ge(rare_used, 2 * t)
                    nc.vector.tensor_tensor(rsum[:], ps[:, 6 + t % 2, :], xn[:, t, :], ALU.add).then_inc(rare_used, 1)
                    dve.wait_ge(rare_used, 2 * t + 1)
                    dve.wait_ge(x1_ready, ST)
                    nc.vector.copy_predicated(resid[:, t, :], masks[:, t:t + 1].to_broadcast([P, D]), rsum[:]).then_inc(rare_used, 1)
                dve.wait_ge(rare_used, 2 * ST)
                for t in range(ST):
                    next_stats(t)

        @block.gpsimd
        def _(pool):
            for c in range(DT):
                pool.wait_ge(wq_high, c + 1)
                nc.gpsimd.tensor_tensor(wql[:, c, :], wl[:, c, :], wqh[:, c, :].bitcast(F32), ALU.subtract).then_inc(wq_low, 1)
            pool.wait_ge(wq_low, DT)
            nc.gpsimd.memset(wl[:], 0.0).then_inc(wl_step, 1)
            pool.wait_ge(bias_in, 16)
            for st in range(ST):
                pool.wait_ge(norm.xn_ready, st + 1)
                nc.gpsimd.tensor_tensor(resid[:, st, :], resid[:, st, :], biasb[:], ALU.add).then_inc(xb_ready, 1)

            def codes(t, hg):
                n = CODES_AT[t]
                for i in range(n):
                    k = hg * n + (HG0 * sum(CODES_AT[:t]) + i)
                    pool.wait_ge(hot_made, k + 1)
                    pool.wait_ge(wl_step, k + 1)
                    pool.sem_inc(waited, 1)
                    part = slice(hg * CUT, (hg + 1) * CUT) if isinstance(hg, int) else bass.ds(hg * CUT, CUT)
                    flat = wl[:].rearrange("p c n -> p (c n)")
                    nc.gpsimd.tensor_tensor(flat[:, part], flat[:, part], onehot[:, i % 2, :], ALU.add).then_inc(wl_step, 1)

            for t in range(ST):
                if CODES_AT[t]:
                    codes(t, 0)
                    with pool.Fori(1, HG0) as hg:
                        codes(t, hg)
                if t == 2:
                    for c in range(DT):
                        pool.wait_ge(wo_high, c + 1)
                        nc.gpsimd.tensor_tensor(wol[:, c, :], woraw[:, c, :], woh[:, c, :].bitcast(F32), ALU.subtract).then_inc(wo_low, 1)



QUADS = ((7, 0), (5, 2), (6, 1), (4, 3))
PAIRS = [(t, p) for a, b in QUADS for t, p in ((a, 0), (b, 0), (a, 1), (b, 1))]
UNITS = [(j, k) for j, (t, _) in enumerate(PAIRS) for k in range(0, t + 1, 2)]
PT_RING, W_RING, RAW_RING = 4, 3, 2
AHEAD = 3
NPAIR, NUNIT, NHEADS = len(PAIRS), len(UNITS), 2 * len(PAIRS)
NCHUNK, NFILL = 2 + G1, NB * (2 + G1)
ROT_STEPS = 4 + 9
NTOK = len(PAIRS) // 2


def group_steps(more):
    turns = [("turn", u) for u in range(NUNIT)]
    main = [[] for _ in PAIRS]
    for u, (j, k) in enumerate(UNITS):
        main[j].append(("av", u))
        if u + 2 < NUNIT:
            main[j].append(turns[u + 2])
    out = [("wo", i) for i in range(G1)] + turns[:2]
    for j in range(NPAIR):
        side = []
        if j + AHEAD < NPAIR:
            side += [("qk", 2 * (j + AHEAD)), ("qk", 2 * (j + AHEAD) + 1)]
        q, r = divmod(j, 4)
        if r == 0 and q:
            side.insert(0, ("out", 2 * q - 2))
            side.insert(2, ("out", 2 * q - 1))
        if more and 4 <= j < 4 + W_RING:
            side.append(("w", j - 4))
        if more and j >= NPAIR - 2:
            half = NFILL // 2
            for f in range((j - NPAIR + 2) * half, (j - NPAIR + 3) * half):
                side.append(("proj", f))
                if f % NB == NB - 1 and f // NB + W_RING < NCHUNK:
                    side.append(("w", f // NB + W_RING))
        out += interleave(main[j], side)
    out.append(("out", NTOK - 2))
    if more:
        out += [("vturn", 0), ("vturn", 1)] + [("qknext", n) for n in range(2 * AHEAD)]
    out.append(("out", NTOK - 1))
    return out


def first_steps():
    out = [("w", c) for c in range(W_RING)]
    for f in range(NFILL):
        out.append(("proj", f))
        if f % NB == NB - 1 and f // NB + W_RING < NCHUNK:
            out.append(("w", f // NB + W_RING))
    return out + [("vturn", 0), ("vturn", 1)] + [("qknext", n) for n in range(2 * AHEAD)]


BANK_KINDS = ("turn", "vturn", "out")
SPLIT_FIRST = 2
SPLIT_GROUP = NUNIT + 2


FIRST_TILE = [n for n in range(NHEADS) if PAIRS[n // 2][0] == 0]


class Place:

    def __init__(self, steps):
        self.fill, self.split = {}, {}
        fills = [s for s in steps if s[0] in BANK_KINDS]
        self.fills = fills
        n = 0
        for i, s in enumerate(fills):
            self.fill[s] = i
            if s[0] != "out":
                self.split[s] = n
                n += 1


def layer1(nc, a, keep):
    ctx = ExitStack()
    with ctx:
        def sb(name, shape, dt=F32):
            return ctx.enter_context(nc.sbuf_tensor(name, shape, dt))

        def sem(name):
            return ctx.enter_context(nc.semaphore(name))

        resid, xth, xtl = keep["resid"], keep["xth"], keep["xtl"]
        identf, identb, masku = keep["identf"], keep["identb"], keep["masku"]
        ps = ctx.enter_context(nc.psum_tensor("ps1", [P, 8, 512], F32))

        def bank(b):
            return ps[:, b % 8, :]

        qth, qtl = sb("qth", [P, G1, S], F32R), sb("qtl", [P, G1, S], F32R)
        kth, ktl = sb("kth", [P, S], F32R), sb("ktl", [P, S], F32R)
        k0h, k0l = sb("k0h", [P, 2 * P], F32R), sb("k0l", [P, 2 * P], F32R)
        vh, vl = sb("vh", [P, ST, P], F32R), sb("vl", [P, ST, P], F32R)
        wh, wl = sb("wh", [P, W_RING, BLK], F32R), sb("wl1", [P, W_RING, BLK], F32R)
        woh, wol = sb("woh1", [P, G1, D], F32R), sb("wol1", [P, G1, D], F32R)
        raw = sb("raw", [P, RAW_RING, BLK])
        cos, sin = (keep["raw"][:, 2 * i:2 * i + 2, :].rearrange("p b c -> p (b c)") for i in range(2))
        kscale, tscale = sb("kscale", [P, P]), sb("tscale", [P, P])
        negm, rowsum, rinv = sb("negm1", [P, NHEADS]), sb("rowsum", [P, NHEADS]), sb("rinv", [P, NHEADS])
        norm = Norm(nc, ctx, keep, "l1_", None, bank)
        with ExitStack() as early:
            norm.xn = early.enter_context(nc.sbuf_tensor("xn1", [P, ST, D], F32))
        with ExitStack() as late:
            def sbl(name, shape, dt=F32):
                return late.enter_context(nc.sbuf_tensor(name, shape, dt))
            plong, pshort = sbl("plong", [P, 2, 2, S]), sbl("pshort", [P, 2, 2, BLK])
            ptnh, ptnl = sbl("ptnh", [P, PT_RING, BLK], F32R), sbl("ptnl", [P, PT_RING, BLK], F32R)
            oth, otl = sbl("oth", [P, 2, G1, P], F32R), sbl("otl", [P, 2, G1, P], F32R)
            rota, rotb = sbl("rota", [P, 2, BLK]), sbl("rotb", [P, 2, BLK])
            vt = sbl("vt", [P, NB, BLK])

        const_in = sem("c1_in")
        raw_in = [sem(f"raw_in{i}") for i in range(RAW_RING)]
        w_split, w_high = sem("w_split"), sem("w_high")
        proj_filled, rope_read, vt_ready = sem("proj_filled"), sem("rope_read"), sem("vt_ready")
        rotated_ready, rot_step, kq_ready = sem("rotated_ready"), sem("rot_step"), sem("kq_ready")
        qk_filled, max_step, max_ready, exp_ready, rinv_ready, p_ready = (
            sem(n) for n in ("qk_filled", "max_step", "max_ready", "exp_ready", "rinv_ready", "p_ready"))
        bank_filled, high_ready, low_ready, av_unit = sem("bank_filled"), sem("bk_high"), sem("bk_low"), sem("av_unit")
        o_high, o_low, y_added = sem("o_high"), sem("o_low"), sem("y_added")
        next_in = [sem(f"next_in{i}") for i in range(3)]
        k0_init, waited = sem("k0_init"), sem("waited")

        block = ctx.enter_context(nc.Block())

        first, more, final = first_steps(), group_steps(True), group_steps(False)
        place_first, place_more, place_final = Place(first), Place(more), Place(final)
        GFILL = len(place_more.fills)
        CHUNKS = NCHUNK + G1

        def length(j):
            return PAIRS[j][0] + 1

        def pbuf(n):
            j, i = divmod(n, 2)
            t = PAIRS[j][0]
            if t >= 4:
                return plong[:, j // 2 % 2, i, 0:(t + 1) * P]
            return pshort[:, j // 2 % 2, i, 0:(t + 1) * P]

        def qk_banks(n):
            return ps[:, 2 * (n % 2):2 * (n % 2) + 2, :].rearrange("p b c -> p (b c)")

        def place_of(g):
            return (place_first if g < 0 else place_final) if isinstance(g, int) else place_more

        def bank_of(s, g):
            return 4 + place_of(g).fill[s] % 2

        def walk(eng, step, lag=0, late_step=None):
            def go(steps, g):
                for i, s in enumerate(steps):
                    step(s, g)
                    if late_step and i >= lag:
                        late_step(steps[i - lag], g)
                if late_step:
                    for s in steps[max(0, len(steps) - lag):]:
                        late_step(s, g)
            go(first, -1)
            with eng.Fori(0, KV1 - 1) as g:
                go(more, g)
            go(final, KV1 - 1)

        def fill_count(s, g):
            if isinstance(g, int) and g < 0:
                return place_first.fill[s]
            return g * GFILL + (SPLIT_FIRST + place_of(g).fill[s])

        def split_count(s, g):
            if isinstance(g, int) and g < 0:
                return place_first.split[s]
            return g * SPLIT_GROUP + (SPLIT_FIRST + place_of(g).split[s])

        def free_probabilities(eng, n, g):
            j = n // 2
            if j >= 4:
                u = max(i for i, (jj, _) in enumerate(UNITS) if jj == j - 4)
                eng.wait_ge(bank_filled, fill_count(("turn", u), g) + 1)

        @block.sync
        def _(sp):
            def load(c, g, k):
                r = k % RAW_RING
                src = a["w1"][g, c] if c < NCHUNK else a["wo1"][g, c - NCHUNK]
                sp.dma_start(raw[:, r, :], src).then_inc(raw_in[r], 16)

            for c in range(NCHUNK):
                if c == RAW_RING:
                    sp.dma_start(cos, a["cos"]).then_inc(const_in, 16)
                    sp.dma_start(sin, a["sin"]).then_inc(const_in, 16)
                    sp.dma_start(kscale[:], a["kscale"]).then_inc(const_in, 16)
                    sp.dma_start(tscale[:], a["tscale"]).then_inc(const_in, 16)
                if c >= RAW_RING:
                    sp.wait_ge(w_split, c - RAW_RING + 1)
                load(c, 0, c)
            def group(g, chunks):
                for k in range(chunks):
                    sp.wait_ge(w_split, g * CHUNKS + (NCHUNK + k - RAW_RING + 1))
                    if k < G1:
                        load(NCHUNK + k, g, k)
                    else:
                        load(k - G1, g + 1, k)

            with sp.Fori(0, KV1 - 1) as g:
                group(g, CHUNKS)
            group(KV1 - 1, G1)
            sp.wait_ge(rope_read, KV1 * 10)
            for j in range(2):
                for which in range(3):
                    load_chunk(sp, a, keep["raw"], j, j, which, P, next_in[j])
            araw = keep["araw"]
            sp.dma_start(araw[:, 0:DT, :], a["gate_a"].rearrange("(c p) r -> p c r", p=P)).then_inc(next_in[2], 16)
            sp.dma_start(araw[:, DT:2 * DT, :], a["up_a"].rearrange("(c p) r -> p c r", p=P)).then_inc(next_in[2], 16)
            sp.wait_ge(k0_init, 3)
            sp.dma_start(araw[:, 2 * DT:2 * DT + FT - 1, :], a["down_a"][0:(FT - 1) * P, :].rearrange("(c p) r -> p c r", p=P)).then_inc(next_in[2], 16)
            sp.dma_start(araw[0:FLAST, 2 * DT + FT - 1, :], a["down_a"][(FT - 1) * P:FH, :]).then_inc(next_in[2], 16)
            sp.wait_ge(next_in[0], 48)
            sp.wait_ge(next_in[1], 48)
            sp.wait_ge(next_in[2], 64)

        @block.tensor
        def _(pe):
            norm.tensor(nc, pe, range(EARLY))

            def proj(f, g):
                c, b = divmod(f, NB)
                if isinstance(g, int) and g == 0 and f == 1:
                    norm.tensor(nc, pe, range(EARLY, ST))
                    pe.wait_ge(norm.low_ready, ST)
                if f < 4:
                    if isinstance(g, int) and g == 0:
                        if f == 0:
                            pe.wait_ge(norm.low_ready, ST // NB)
                    else:
                        pe.wait_ge(exp_ready, g * NHEADS)
                elif f < 6:
                    pe.wait_ge(rope_read, g * 10 + (f - 3))
                elif f < 8:
                    pe.wait_ge(vt_ready, g * 2 + (f - 5))
                else:
                    pe.wait_ge(rope_read, g * 10 + (f - 5))
                if b == 0:
                    pe.wait_ge(w_split, g * CHUNKS + (c + 1))
                for d in range(DT):
                    w = (wh[:, c % W_RING, d * P:(d + 1) * P], wl[:, c % W_RING, d * P:(d + 1) * P])
                    last = products(pe, bank(f % 4), w, (xth[:, d, b * BLK:(b + 1) * BLK], xtl[:, d, b * BLK:(b + 1) * BLK]),
                                    d == 0, d == DT - 1)
                last.then_inc(proj_filled, 1)

            def qk(n, g):
                j, i = divmod(n, 2)
                t, p = PAIRS[j]
                h = 2 * p + i
                if n >= 2:
                    pe.wait_ge(exp_ready, g * NHEADS + (n - 1))
                else:
                    pe.wait_ge(rope_read, g * 10 + 10)
                    pe.wait_ge(vt_ready, g * 2 + 2)
                pe.wait_ge(kq_ready, g * 10 + (2 * h + 4))
                q = (qth[:, h, t * P:(t + 1) * P], qtl[:, h, t * P:(t + 1) * P])
                out = qk_banks(n)
                width = (t + 1) * P
                for c0 in range(0, width, BLK):
                    w = max(2 * P, min(BLK, width - c0))
                    k = (k0h[:, 0:w], k0l[:, 0:w]) if t == 0 else (kth[:, c0:c0 + w], ktl[:, c0:c0 + w])
                    products(pe, out[:, c0:c0 + w], q, k, True, c0 + BLK < width)
                pe.matmul(out[:, t * P:(t + 1) * P], identb[:], masku[:], start=False, stop=True).then_inc(qk_filled, 1)

            def bank_free(s, g):
                if isinstance(g, int) and g < 0:
                    return
                place = place_of(g)
                i = place.fill[s]
                past = place.fills[i - 2] if i >= 2 else place_more.fills[i - 2]
                if past[0] == "out":
                    pe.wait_ge(y_added, g * NTOK + (past[1] + 2 - (0 if i >= 2 else NTOK)))
                else:
                    pe.wait_ge(low_ready, g * SPLIT_GROUP + (SPLIT_FIRST + place_more.split[past] + 1 - (0 if i >= 2 else SPLIT_GROUP)))

            def turn(u, g):
                j, k = UNITS[u]
                t = PAIRS[j][0]
                bank_free(("turn", u), g)
                pe.wait_ge(p_ready, g * NPAIR + (j + 1))
                b = bank_of(("turn", u), g)
                for kk in range(k, min(k + 2, t + 1)):
                    for i in range(2):
                        last = nc.tensor.transpose(ps[:, b, (2 * (kk - k) + i) * P:(2 * (kk - k) + i + 1) * P],
                                                   pbuf(2 * j + i)[:, kk * P:(kk + 1) * P], identf[:])
                last.then_inc(bank_filled, 1)

            def av(u, g):
                j, k = UNITS[u]
                t = PAIRS[j][0]
                if k == 0:
                    pe.wait_ge(o_low, g * NPAIR + max(1, j))
                pe.wait_ge(low_ready, split_count(("turn", u), g) + 1)
                for kk in range(k, min(k + 2, t + 1)):
                    c = 2 * P * (kk - k)
                    last = products(pe, ps[:, 6 + j % 2, 0:2 * P], (vh[:, kk, :], vl[:, kk, :]),
                                    (ptnh[:, u % PT_RING, c:c + 2 * P], ptnl[:, u % PT_RING, c:c + 2 * P]), kk == 0, kk == t)
                last.then_inc(av_unit, 1)

            def out(o, g):
                q, ab = divmod(o, 2)
                bank_free(("out", o), g)
                pe.wait_ge(o_low, g * NPAIR + (4 * q + 4 + ab))
                pe.wait_ge(w_split, g * CHUNKS + CHUNKS)
                b = bank_of(("out", o), g)
                for h in range(G1):
                    last = products(pe, bank(b), (oth[:, ab, h, :], otl[:, ab, h, :]), (woh[:, h, :], wol[:, h, :]), h == 0, h == G1 - 1)
                last.then_inc(bank_filled, 1)

            def vturn(v, g):
                bank_free(("vturn", v), g)
                pe.wait_ge(vt_ready, (g + 1) * 2 + (v + 1))
                b = bank_of(("vturn", v), g)
                for i in range(4):
                    last = nc.tensor.transpose(ps[:, b, i * P:(i + 1) * P], vt[:, v, i * P:(i + 1) * P], identf[:])
                last.then_inc(bank_filled, 1)

            def step(s, g):
                kind, i = s
                if kind == "proj":
                    proj(i, g + 1)
                elif kind == "qk":
                    qk(i, g)
                elif kind == "qknext":
                    qk(i, g + 1)
                elif kind == "turn":
                    turn(i, g)
                elif kind == "av":
                    av(i, g)
                elif kind == "out":
                    out(i, g)
                elif kind == "vturn":
                    vturn(i, g)

            pe.wait_ge(k0_init, 2)
            walk(pe, step)

        @block.scalar
        def _(act):
            norm.scalar_sqrt(nc, act)
            norm.scalar_high(nc, act)

            def step(s, g):
                kind, i = s
                if kind == "proj" and i in (2, 3):
                    gg = g + 1
                    act.wait_ge(proj_filled, gg * NFILL + (i + 1))
                    nc.scalar.activation(vt[:, i - 2, :], bank(i), ACT.Copy).then_inc(vt_ready, 1)
                elif kind in ("turn", "vturn"):
                    act.wait_ge(bank_filled, fill_count(s, g) + 1)
                    if kind == "turn":
                        j, k = UNITS[i]
                        w = 2 * P * min(2, PAIRS[j][0] + 1 - k)
                        if i >= PT_RING:
                            act.wait_ge(av_unit, g * NUNIT + (i - PT_RING + 1))
                        b = bank_of(s, g)
                        nc.scalar.activation(ptnh[:, i % PT_RING, 0:w], ps[:, b, 0:w], ACT.Copy).then_inc(high_ready, 1)
                    else:
                        gg = g + 1
                        b = bank_of(s, g)
                        act.wait_ge(av_unit, gg * NUNIT)
                        nc.scalar.activation(vh[:, 4 * i:4 * i + 4, :], bank(b).rearrange("p (t d) -> p t d", t=4),
                                             ACT.Copy).then_inc(high_ready, 1)
                elif kind == "av":
                    j, k = UNITS[i]
                    t, p = PAIRS[j]
                    if k + 2 > t:
                        act.wait_ge(av_unit, g * NUNIT + (i + 1))
                        ab = j % 2
                        act.wait_ge(y_added, g * NTOK + max(1, 2 * (j // 4) + ab))
                        nc.scalar.activation(oth[:, ab, 2 * p:2 * p + 2, :], ps[:, 6 + j % 2, 0:2 * P].rearrange("p (h q) -> p h q", h=2),
                                             ACT.Copy).then_inc(o_high, 1)

            def late_step(s, g):
                kind, n = s
                if kind in ("qk", "qknext"):
                    gg = g + 1 if kind == "qknext" else g
                    j, i = divmod(n, 2)
                    t = PAIRS[j][0]
                    act.wait_ge(max_ready, gg * NHEADS + (n + 1))
                    src = qk_banks(n)[:, 0:(t + 1) * P] if t else pbuf(n)
                    if t:
                        free_probabilities(act, n, gg)
                    nc.scalar.activation(pbuf(n), src, ACT.Exp, bias=negm[:, n:n + 1], accum_out=rowsum[:, n:n + 1]).then_inc(exp_ready, 1)

            walk(act, step, 2, late_step)

        @block.vector
        def _(dve):
            dve.sem_inc(y_added, 1)
            dve.sem_inc(o_low, 1)
            nc.vector.memset(k0h[:].bitcast(F32), 0.0).then_inc(k0_init, 1)
            nc.vector.memset(k0l[:].bitcast(F32), 0.0).then_inc(k0_init, 1)
            nc.vector.memset(keep["araw"][:, 2 * DT + FT - 1, :], 0.0).then_inc(k0_init, 1)
            norm.vector(nc, dve, None)
            dve.wait_ge(norm.xn_ready, ST)
            dve.wait_ge(const_in, 64)

            def rope(f, g):
                gg = g + 1
                r = f if f < 2 else f - 2
                c = HD1 ** -0.5 if f >= 4 else 1.0
                dve.wait_ge(proj_filled, gg * NFILL + (f + 1))
                if r >= 2 or not isinstance(gg, int):
                    dve.wait_ge(kq_ready, gg * 10 + (r - 1))
                cols = slice(f % NB * BLK, (f % NB + 1) * BLK)
                src = bank(f % 4)
                nc.vector.scalar_tensor_tensor(out=rota[:, r % 2, :], in0=src, scalar=c, in1=cos[:, cols], op0=ALU.mult, op1=ALU.mult)
                nc.vector.scalar_tensor_tensor(out=rotb[0:64, r % 2, :], in0=src[64:128, :], scalar=c, in1=sin[64:128, cols],
                                               op0=ALU.mult, op1=ALU.mult)
                nc.vector.scalar_tensor_tensor(out=rotb[64:128, r % 2, :], in0=src[0:64, :], scalar=c, in1=sin[0:64, cols],
                                               op0=ALU.mult, op1=ALU.mult).then_inc(rope_read, 1)
                dve.wait_ge(rope_read, gg * 10 + (r + 1))
                nc.vector.tensor_tensor(rota[:, r % 2, :], rota[:, r % 2, :], rotb[:, r % 2, :], ALU.add).then_inc(rotated_ready, 1)

            def step(s, g):
                kind, i = s
                if kind == "proj" and i not in (2, 3):
                    rope(i, g)
                elif kind in ("qk", "qknext"):
                    gg = g + 1 if kind == "qknext" else g
                    t = PAIRS[i // 2][0]
                    dve.wait_ge(qk_filled, gg * NHEADS + (i + 1))
                    if t:
                        nc.vector.tensor_reduce(negm[:, i:i + 1], qk_banks(i)[:, 0:(t + 1) * P], AX.X, ALU.max, negate=True).then_inc(max_ready, 1)
                    else:
                        free_probabilities(dve, i, gg)
                        nc.vector.tensor_tensor(pbuf(i), qk_banks(i)[:, 0:P], tscale[:], ALU.mult).then_inc(max_step, 1)
                        dve.wait_ge(max_step, gg * 4 + FIRST_TILE.index(i) + 1)
                        nc.vector.tensor_reduce(negm[:, i:i + 1], pbuf(i), AX.X, ALU.max, negate=True).then_inc(max_ready, 1)
                elif kind in ("turn", "vturn"):
                    dve.wait_ge(high_ready, split_count(s, g) + 1)
                    if kind == "turn":
                        j, k = UNITS[i]
                        w = 2 * P * min(2, PAIRS[j][0] + 1 - k)
                        b = bank_of(s, g)
                        nc.vector.tensor_tensor(ptnl[:, i % PT_RING, 0:w], ps[:, b, 0:w], ptnh[:, i % PT_RING, 0:w].bitcast(F32),
                                                ALU.subtract).then_inc(low_ready, 1)
                    else:
                        b = bank_of(s, g)
                        nc.vector.tensor_tensor(vl[:, 4 * i:4 * i + 4, :], bank(b).rearrange("p (t d) -> p t d", t=4),
                                                vh[:, 4 * i:4 * i + 4, :].bitcast(F32), ALU.subtract).then_inc(low_ready, 1)
                elif kind == "av":
                    j, k = UNITS[i]
                    t, p = PAIRS[j]
                    if k + 2 > t:
                        dve.wait_ge(o_high, g * NPAIR + (j + 1))
                        ab = j % 2
                        nc.vector.tensor_tensor(otl[:, ab, 2 * p:2 * p + 2, :], ps[:, 6 + j % 2, 0:2 * P].rearrange("p (h q) -> p h q", h=2),
                                                oth[:, ab, 2 * p:2 * p + 2, :].bitcast(F32), ALU.subtract).then_inc(o_low, 1)
                elif kind == "out":
                    t = QUADS[i // 2][i % 2]
                    dve.wait_ge(bank_filled, fill_count(s, g) + 1)
                    dve.wait_ge(y_added, g * NTOK + 1)
                    nc.vector.tensor_tensor(resid[:, t, :], ps[:, bank_of(s, g), :], resid[:, t, :], ALU.add).then_inc(y_added, 1)

            def late_step(s, g):
                kind, n = s
                if kind in ("qk", "qknext") and n % 2 == 1:
                    gg = g + 1 if kind == "qknext" else g
                    dve.wait_ge(exp_ready, gg * NHEADS + (n + 1))
                    nc.vector.reciprocal(rinv[:, n - 1:n + 1], rowsum[:, n - 1:n + 1]).then_inc(rinv_ready, 1)

            walk(dve, step, 2, late_step)

        @block.gpsimd
        def _(pool):
            def split(src, high, low, n):
                pool.sem_inc(waited, 1)
                nc.gpsimd.tensor_scalar(high, src, 1.0, 1.0, ALU.mult, ALU.mult).then_inc(w_high, 1)
                pool.wait_ge(w_high, n)
                nc.gpsimd.tensor_tensor(low, src, high.bitcast(F32), ALU.subtract).then_inc(w_split, 1)

            def rotated(f, gg):
                r = f if f < 2 else f - 2
                base = 0 if r == 0 else 4 + (r - 1)
                if r == 0:
                    pool.wait_ge(const_in, 64)
                pool.wait_ge(rotated_ready, gg * 10 + (r + 1))
                pool.wait_ge(qk_filled, gg * NHEADS)
                sums = rota[:, r % 2, :]

                def chained(ins, n):
                    ins.then_inc(rot_step, 1)
                    pool.wait_ge(rot_step, gg * ROT_STEPS + (base + n))

                cols = slice(f % NB * BLK, (f % NB + 1) * BLK)
                if r == 0:
                    pool.sem_inc(waited, 1)
                    chained(nc.gpsimd.tensor_scalar(k0h[:, 0:P], sums[:, 0:P], 1.0, 1.0, ALU.mult, ALU.mult), 1)
                    chained(nc.gpsimd.tensor_tensor(k0l[:, 0:P], sums[:, 0:P], k0h[:, 0:P].bitcast(F32), ALU.subtract), 2)
                    chained(nc.gpsimd.tensor_tensor(sums[:, 0:P], sums[:, 0:P], kscale[:], ALU.mult), 3)
                high, low = (kth[:, cols], ktl[:, cols]) if r < 2 else (qth[:, (r - 2) // NB, cols], qtl[:, (r - 2) // NB, cols])
                pool.sem_inc(waited, 1)
                chained(nc.gpsimd.tensor_scalar(high, sums, 1.0, 1.0, ALU.mult, ALU.mult), 4 if r == 0 else 1)
                nc.gpsimd.tensor_tensor(low, sums, high.bitcast(F32), ALU.subtract).then_inc(kq_ready, 1)

            def step(s, g):
                kind, i = s
                gg = g + 1
                if kind == "w":
                    pool.wait_ge(raw_in[i % RAW_RING], gg * (8 * CHUNKS) + 16 * (i // RAW_RING + 1))
                    if i >= W_RING:
                        pool.wait_ge(proj_filled, gg * NFILL + NB * (i - W_RING + 1))
                    else:
                        pool.wait_ge(proj_filled, gg * NFILL)
                    split(raw[:, i % RAW_RING, :], wh[:, i % W_RING, :], wl[:, i % W_RING, :], gg * CHUNKS + (i + 1))
                elif kind == "wo":
                    k = NCHUNK + i
                    pool.wait_ge(raw_in[k % RAW_RING], g * (8 * CHUNKS) + 16 * (k // RAW_RING + 1))
                    pool.wait_ge(y_added, g * NTOK + 1)
                    split(raw[:, k % RAW_RING, :], woh[:, i, :], wol[:, i, :], g * CHUNKS + (k + 1))
                elif kind == "proj" and i not in (2, 3):
                    rotated(i, gg)

            def late_step(s, g):
                kind, n = s
                if kind in ("qk", "qknext") and n % 2 == 1:
                    gg = g + 1 if kind == "qknext" else g
                    pool.wait_ge(rinv_ready, gg * NPAIR + (n // 2 + 1))
                    pool.sem_inc(waited, 1)
                    nc.gpsimd.tensor_scalar(pbuf(n - 1), pbuf(n - 1), rinv[:, n - 1:n], 1.0, ALU.mult, ALU.mult)
                    nc.gpsimd.tensor_scalar(pbuf(n), pbuf(n), rinv[:, n:n + 1], 1.0, ALU.mult, ALU.mult).then_inc(p_ready, 1)

            pool.wait_ge(k0_init, 2)
            walk(pool, step, 2, late_step)





def load_chunk(sp, a, raw, j, par, which, n, arrived):
    k = 3 * par + which
    if which < 2:
        name = "gate" if which == 0 else "up"
        src = a[name + "_last"] if n < P else a[name + "_main"][j]
        sp.dma_start(raw[:, k, 0:DT * n], src).then_inc(arrived, 16)
    else:
        src = a["down_main"][j] if n == P else a["down_last"]
        sp.dma_start(raw[0:n, k, :], src).then_inc(arrived, 16)


def gated(nc, a, keep):
    ctx = ExitStack()
    with ctx:
        def sb(name, shape, dt=F32):
            return ctx.enter_context(nc.sbuf_tensor(name, shape, dt))

        def sem(name):
            return ctx.enter_context(nc.semaphore(name))

        resid, xth, xtl = keep["resid"], keep["xth"], keep["xtl"]
        ps = ctx.enter_context(nc.psum_tensor("ps2", [P, 8, 512], F32))
        raw, araw = keep["raw"], keep["araw"]
        wh, wl = sb("wh2", [P, 6, BLK], F32R), sb("wl2", [P, 6, BLK], F32R)
        sg, hid = sb("sg", [P, NB, BLK]), sb("hid", [P, NB, BLK])
        hidh, hidl = sb("hidh", [P, 2, S], F32R), sb("hidl", [P, 2, S], F32R)
        asplit = sb("asplit", [P, 2, 2 * DT + FT, RROWS], F32R)
        ah, al = asplit[:, 0, :, :], asplit[:, 1, :, :]
        bnow, anow = sb("bnow", [RROWS, 2, 2, P], F32R), sb("anow", [P, 2, 2, RROWS], F32R)
        BW = 2 * FH + D
        braw, bs = sb("braw", [RROWS, BW]), sb("bs", [RROWS, BW], F32R)
        xa = sb("xa", [RROWS, 2, S], F32R)
        zero = sb("zero", [P, P], BF16)
        ha = sb("ha", [RROWS, S], F32R)

        raw_in = [sem(f"raw2_in{i}") for i in range(6)]
        zero_ready, now_ready, waited = sem("zero_ready"), sem("now_ready"), sem("waited2")
        b_in, b_zero = sem("b_in"), sem("b_zero")
        a_high, a_low, b_high, b_ready = sem("a_high"), sem("a_low"), sem("b_high"), sem("b_ready")
        xa_filled, xa_high, xa_ready = sem("xa_filled"), sem("xa_high"), sem("xa_ready")
        w_high, w_split = sem("w2_high"), sem("w2_split")
        gu_filled, silu_done, hid_made, hid_high, hid_low = (sem(n) for n in ("gu_filled", "silu_done", "hid_made", "hid_high", "hid_low"))
        ha_filled, ha_high, ha_ready = sem("ha_filled"), sem("ha_high"), sem("ha_ready")
        down_filled, added, out_done = sem("down_filled"), sem("added"), sem("out2_done")
        block = ctx.enter_context(nc.Block())

        def rows(j):
            return FLAST if isinstance(j, int) and j == FT - 1 else P

        def walk(eng, start, body):
            start()
            loops = (FT - 2) // 2
            with eng.Fori(0, loops) as jj:
                body(jj * 2, 0)
                body(jj * 2 + 1, 1)
            for j in range(2 * loops, FT):
                body(j, j % 2)

        @block.sync
        def _(sp):
            def load(j, par, which):
                if not (isinstance(j, int) and j < 2):
                    sp.wait_ge(w_split, 3 * j + (which - 5))
                load_chunk(sp, a, raw, j, par, which, rows(j), raw_in[3 * par + which])

            sp.wait_ge(b_zero, 1)
            for r in range(3):
                for name, c0, n in (("gate_b", 0, FH), ("up_b", FH, FH), ("down_b", 2 * FH, D)):
                    sp.dma_start(braw[RS * r:RS * r + RANK, c0:c0 + n], a[name]).then_inc(b_in, 16)
            def body(j, par):
                if not (isinstance(j, int) and j + 2 >= FT):
                    for which in (0, 1, 2):
                        load(j + 2, par, which)
            walk(sp, lambda: None, body)
            for t in range(ST):
                sp.wait_ge(added, ST * (FT - 1) + t + 2)
                sp.dma_start(a["out"].rearrange("(t p) d -> p t d", p=P)[:, t, :], resid[:, t, :]).then_inc(out_done, 16)
            sp.wait_ge(out_done, 16 * ST)

        @block.tensor
        def _(pe):
            pe.sem_inc(down_filled, 1)
            pe.wait_ge(a_low, 1)
            for g in range(2):
                for b in range(NB):
                    for d in range(DT):
                        last = products(pe, ps[0:RROWS, 4 + 2 * g + b, :], (ah[:, g * DT + d, :], al[:, g * DT + d, :]),
                                        (xth[:, d, b * BLK:(b + 1) * BLK], xtl[:, d, b * BLK:(b + 1) * BLK]), d == 0, d == DT - 1)
                    last.then_inc(xa_filled, 1)

            def gate_up(j, par):
                n = rows(j)
                for b in range(NB):
                    if not (isinstance(j, int) and j == 0):
                        pe.wait_ge(hid_made, j * 2 + (b - 1))
                    for which in range(2):
                        if b == 0:
                            pe.wait_ge(w_split, 3 * j + which + 1)
                        k = 3 * par + which
                        w3h = wh[:, k, 0:DT * n].rearrange("p (d n) -> p d n", d=DT)
                        w3l = wl[:, k, 0:DT * n].rearrange("p (d n) -> p d n", d=DT)
                        out = ps[0:n, 2 * b + which, :]
                        for d in range(DT):
                            products(pe, out, (w3h[:, d, :], w3l[:, d, :]),
                                     (xth[:, d, b * BLK:(b + 1) * BLK], xtl[:, d, b * BLK:(b + 1) * BLK]), d == 0, False)
                        if isinstance(j, int) and j == 0:
                            pe.wait_ge(xa_ready, 4)
                        pe.wait_ge(now_ready, 2 * j + 2)
                        last = pe.matmul(out, bnow[:, par, which, 0:n], xa[:, which, b * BLK:(b + 1) * BLK], start=False, stop=True)
                    last.then_inc(gu_filled, 1)

            def hidden_a(j, par):
                n = rows(j)
                pe.wait_ge(hid_low, 2 * j + 2)
                for b in range(NB):
                    cols = slice(b * BLK, (b + 1) * BLK)
                    l = (anow[0:n, par, 0, :], anow[0:n, par, 1, :])
                    r = (hidh[0:n, par, cols], hidl[0:n, par, cols])
                    start = isinstance(j, int) and j == 0
                    lastj = isinstance(j, int) and j == FT - 1
                    last = products(pe, ps[0:RROWS, 6 + b, :], l, r, start, lastj)
                    if lastj:
                        last.then_inc(ha_filled, 1)

            def down(j, par):
                n = rows(j)
                pe.wait_ge(w_split, 3 * j + 3)
                lastj = isinstance(j, int) and j == FT - 1
                if lastj:
                    pe.wait_ge(ha_ready, NB)
                for t in range(ST):
                    if not (isinstance(j, int) and j == 0 and t < 2):
                        pe.wait_ge(added, ST * j + max(1, t))
                    out = ps[:, 4 + t % 2, :]
                    last = products(pe, out, (hidh[0:n, par, t * P:(t + 1) * P], hidl[0:n, par, t * P:(t + 1) * P]),
                                    (wh[0:n, 3 * par + 2, :], wl[0:n, 3 * par + 2, :]), True, not lastj)
                    if lastj:
                        last = pe.matmul(out, ha[:, t * P:(t + 1) * P], bs[:, 2 * FH:2 * FH + D], start=False, stop=True)
                    last.then_inc(down_filled, 1)

            def start():
                gate_up(0, 0)
                pe.wait_ge(zero_ready, 1)
                for b in range(NB):
                    pe.matmul(ps[0:RROWS, 6 + b, :], zero[:, 0:RROWS], zero[:, 0:1].to_broadcast([P, BLK]), start=True, stop=False)

            def body(j, par):
                if not (isinstance(j, int) and j == FT - 1):
                    gate_up(j + 1, 1 - par)
                hidden_a(j, par)
                down(j, par)
            walk(pe, start, body)

        @block.scalar
        def _(act):
            for g in range(2):
                for b in range(NB):
                    act.wait_ge(xa_filled, 2 * g + b + 1)
                    nc.scalar.activation(xa[:, g, b * BLK:(b + 1) * BLK], ps[0:RROWS, 4 + 2 * g + b, :], ACT.Copy).then_inc(xa_high, 1)

            def low_rank(j, par):
                n = rows(j)
                if not (isinstance(j, int) and j < 2):
                    act.wait_ge(down_filled, ST * j - (ST - 1))
                cols = slice(j * P, j * P + n) if isinstance(j, int) else bass.ds(j * P, n)
                nc.scalar.activation(bnow[:, par, :, 0:n], bs[:, 0:2 * FH].bitcast(F32).rearrange("p (w n) -> p w n", w=2)[:, :, cols],
                                     ACT.Copy).then_inc(now_ready, 1)
                tile = slice(2 * DT + j, 2 * DT + j + 1) if isinstance(j, int) else bass.ds(2 * DT + j, 1)
                nc.scalar.activation(anow[:, par, :, :].unsqueeze(2), asplit[:, :, tile, :].bitcast(F32), ACT.Copy).then_inc(now_ready, 1)

            def hidden(j, par):
                n = rows(j)
                for b in range(NB):
                    act.wait_ge(gu_filled, 2 * j + (b + 1))
                    nc.scalar.activation(sg[0:n, b, :], ps[0:n, 2 * b, :], ACT.Silu).then_inc(silu_done, 1)
                for b in range(NB):
                    act.wait_ge(hid_made, 2 * j + (b + 1))
                    if not (isinstance(j, int) and j < 2):
                        act.wait_ge(down_filled, ST * j - (ST - 1))
                    nc.scalar.activation(hidh[0:n, par, b * BLK:(b + 1) * BLK], hid[0:n, b, :], ACT.Copy).then_inc(hid_high, 1)

            def body(j, par):
                if not (isinstance(j, int) and j == FT - 1):
                    low_rank(j + 1, 1 - par)
                    hidden(j + 1, 1 - par)

            def start():
                act.wait_ge(b_ready, 1)
                low_rank(0, 0)
                hidden(0, 0)
            walk(act, start, body)
            for b in range(NB):
                act.wait_ge(ha_filled, b + 1)
                nc.scalar.activation(ha[:, b * BLK:(b + 1) * BLK], ps[0:RROWS, 6 + b, :], ACT.Copy).then_inc(ha_high, 1)

        @block.vector
        def _(dve):
            dve.sem_inc(added, 1)
            def split_a(c0, c1):
                rep = araw[:, c0:c1, :].unsqueeze(2).to_broadcast([P, c1 - c0, RROWS // RANK, RANK])
                high, low = (part[:, c0:c1, :].rearrange("p c (k r) -> p c k r", r=RANK) for part in (ah, al))
                nc.vector.tensor_copy(high, rep).then_inc(a_high, 1)
                dve.wait_ge(a_high, 1 if c0 == 0 else 2)
                nc.vector.tensor_tensor(low, rep, high.bitcast(F32), ALU.subtract).then_inc(a_low, 1)

            split_a(0, 2 * DT)
            nc.vector.memset(braw[:], 0.0).then_inc(b_zero, 1)
            nc.vector.memset(zero[:], 0.0).then_inc(zero_ready, 1)
            split_a(2 * DT, 2 * DT + FT)
            dve.wait_ge(b_in, 16 * 9)
            nc.vector.tensor_copy(bs[:], braw[:]).then_inc(b_high, 1)
            dve.wait_ge(b_high, 1)
            nc.vector.tensor_tensor(bs[RS:2 * RS, :], braw[RS:2 * RS, :], bs[RS:2 * RS, :].bitcast(F32), ALU.subtract).then_inc(b_ready, 1)
            for g in range(2):
                for b in range(NB):
                    dve.wait_ge(xa_high, 2 * g + b + 1)
                    part = xa[2 * RS:RROWS, g, b * BLK:(b + 1) * BLK]
                    nc.vector.tensor_tensor(part, ps[2 * RS:RROWS, 4 + 2 * g + b, :], part.bitcast(F32), ALU.subtract).then_inc(xa_ready, 1)

            def hidden(j):
                n = rows(j)
                for b in range(NB):
                    dve.wait_ge(silu_done, 2 * j + (b + 1))
                    if not (isinstance(j, int) and j == 0):
                        dve.wait_ge(hid_low, 2 * j + (b - 1))
                    nc.vector.tensor_tensor(hid[0:n, b, :], ps[0:n, 2 * b + 1, :], sg[0:n, b, :], ALU.mult).then_inc(hid_made, 1)

            def body(j, par):
                if not (isinstance(j, int) and j == FT - 1):
                    hidden(j + 1)
                else:
                    for b in range(NB):
                        dve.wait_ge(ha_high, b + 1)
                        part = ha[2 * RS:RROWS, b * BLK:(b + 1) * BLK]
                        nc.vector.tensor_tensor(part, ps[2 * RS:RROWS, 6 + b, :], part.bitcast(F32), ALU.subtract).then_inc(ha_ready, 1)
                dve.wait_ge(added, ST * j + 1)
                for t in range(ST):
                    dve.wait_ge(down_filled, ST * j + (t + 2))
                    nc.vector.tensor_tensor(resid[:, t, :], ps[:, 4 + t % 2, :], resid[:, t, :], ALU.add).then_inc(added, 1)
            walk(dve, lambda: hidden(0), body)

        @block.gpsimd
        def _(pool):
            def split(j, par, which):
                k, n = 3 * par + which, rows(j)
                if not (isinstance(j, int) and j < 2):
                    pool.wait_ge(raw_in[k], 8 * (j - par))
                if not (isinstance(j, int) and j < 2):
                    if which < 2:
                        pool.wait_ge(gu_filled, 2 * j - 2)
                    else:
                        pool.wait_ge(down_filled, ST * j - (ST - 1))
                if which < 2:
                    src, high, low = raw[:, k, 0:DT * n], wh[:, k, 0:DT * n], wl[:, k, 0:DT * n]
                else:
                    src, high, low = raw[0:n, k, :], wh[0:n, k, :], wl[0:n, k, :]
                pool.sem_inc(waited, 1)
                nc.gpsimd.tensor_scalar(high, src, 1.0, 1.0, ALU.mult, ALU.mult).then_inc(w_high, 1)
                pool.wait_ge(w_high, 3 * j + which + 1)
                nc.gpsimd.tensor_tensor(low, src, high.bitcast(F32), ALU.subtract).then_inc(w_split, 1)

            def hidden(j, par):
                n = rows(j)
                for b in range(NB):
                    pool.wait_ge(hid_high, 2 * j + (b + 1))
                    cols = slice(b * BLK, (b + 1) * BLK)
                    nc.gpsimd.tensor_tensor(hidl[0:n, par, cols], hid[0:n, b, :], hidh[0:n, par, cols].bitcast(F32), ALU.subtract).then_inc(hid_low, 1)

            def start():
                for which in range(3):
                    split(0, 0, which)
                for which in range(3):
                    split(1, 1, which)
                hidden(0, 0)

            def body(j, par):
                if not (isinstance(j, int) and j == FT - 1):
                    hidden(j + 1, 1 - par)
                if not (isinstance(j, int) and j + 2 >= FT):
                    for which in range(3):
                        split(j + 2, par, which)
            walk(pool, start, body)


def _constants():
    import numpy as np
    bf = mybir.dt.np(BF16)

    def parts(v):
        v = np.asarray(v, np.float32)
        p0 = v.astype(bf)
        p1 = (v - p0.astype(np.float32)).astype(bf)
        return [p0, p1, (v - p0.astype(np.float32) - p1.astype(np.float32)).astype(bf)]

    ident = np.eye(P, dtype=np.float32)
    masku = np.where(np.arange(P)[None, :] > np.arange(P)[:, None], -1e30, 0.0).astype(np.float32)
    start = 2.0 ** (-2.0 ** (-(np.log2(H0) - 3)))
    slopes = np.array([start ** (i + 1) for i in range(H0)], dtype=np.float32)
    inner = (np.arange(S) % P).astype(np.float32)
    qaux = np.zeros((K_ROWS - AUX, H0, S), bf)
    for i, p in enumerate(parts(slopes)):
        qaux[i] = p[:, None]
        qaux[3 + i] = p[:, None]
    for i, p in enumerate(parts(-slopes[:, None] * inner[None, :])):
        qaux[6 + i] = p
    kaux = np.zeros((T_ROWS - AUX, tri(ST)), bf)
    for t in range(ST):
        k = np.arange((t + 1) * P)
        kaux[0:3, tri(t):tri(t + 1)] = (P * (k // P - t)).astype(bf)
        kaux[3:6, tri(t):tri(t + 1)] = (k % P).astype(bf)
        kaux[6:, tri(t):tri(t + 1)] = 1.0
    sel = np.zeros((P, 8, 3, AUX), bf)
    for m in range(AUX):
        for h in range(8):
            sel[HD0 * h + m % HD0, h, QPARTS[m // HD0], m] = 1.0
    inv_freq = (1.0 / 10000.0 ** (np.arange(0, HD1, 2, dtype=np.float32) / np.float32(HD1))).astype(np.float32)
    angle = np.arange(S, dtype=np.float32)[None, :] * np.concatenate([inv_freq, inv_freq])[:, None]
    cos, sin = np.cos(angle).astype(np.float32), np.sin(angle).astype(np.float32)
    sin[HD1 // 2:] *= -1.0
    pos = np.arange(P)
    key_scale = np.where(pos < 35, 0.5, np.where(pos < 35 + 72, 1.5, 1.0)).astype(np.float32)
    kscale = np.tile(key_scale[None, :], (P, 1))
    tscale = np.where(pos[:, None] >= 35 + 72, key_scale[None, :], 1.0).astype(np.float32)
    return {"cos": cos, "sin": sin, "kscale": kscale, "tscale": tscale, "identf": ident, "identb": ident.astype(bf), "masku": masku.astype(bf), "sel": sel, "qaux": qaux, "kaux": kaux}


def kernel(**inputs):
    import numpy as np
    import concourse.bacc as _bacc
    from concourse.bass_utils import run_bass_kernel_spmd as _run

    nc = _bacc.Bacc("TRN2", target_bir_lowering=False, num_devices=1)
    host = {k: np.asarray(v) for k, v in inputs.items()}
    laid = {
        "x": host["L0_attn_hidden_states"].reshape(S, D),
        "wq0": host["L0_attn_Wq"], "wkv0": host["L0_attn_Wkv"], "wo0": host["L0_attn_Wo"],
        "qw": host["L0_ffn_qweight"], "lut4": host["L0_ffn_lut4"], "lut8": host["L0_ffn_lut8"], "bias": host["L0_ffn_bias"],
    }
    wq, wk, wv = (host[f"L1_attn_w{n}"] for n in "qkv")
    def chunks(w, heads):
        return w.reshape(KV1, heads, HD1, DT, P).transpose(0, 1, 4, 3, 2).reshape(KV1, heads, P, BLK)

    laid["w1"] = np.concatenate([chunks(wk, 1), chunks(wv, 1), chunks(wq, G1)], axis=1)
    laid["wo1"] = host["L1_attn_wo"].T.reshape(KV1, G1, HD1, D)
    cut = (FT - 1) * P
    for name in ("gate", "up"):
        w = host[f"L1_ffn_{name}_w"]
        laid[name + "_main"] = w[:cut].reshape(FT - 1, P, DT, P).transpose(0, 3, 2, 1).reshape(FT - 1, P, BLK)
        laid[name + "_last"] = w[cut:].reshape(FLAST, DT, P).transpose(2, 1, 0).reshape(P, DT * FLAST)
    down = host["L1_ffn_down_w"].T
    laid["down_main"], laid["down_last"] = down[:cut].reshape(FT - 1, P, D), down[cut:]
    for name in ("gate", "up", "down"):
        laid[name + "_a"], laid[name + "_b"] = host[f"L1_ffn_{name}_a"].T, host[f"L1_ffn_{name}_b"].T
    laid.update(_constants())
    arrays, aps = {}, {}
    for name, v in laid.items():
        v = np.ascontiguousarray(v)
        arrays[f"in_{name}"] = v
        aps[name] = nc.dram_tensor(f"in_{name}", v.shape, mybir.dt.from_np(v.dtype), kind="ExternalInput").ap()
    aps["out"] = nc.dram_tensor("out_0", (S, D), F32, kind="ExternalOutput").ap()
    build(nc, aps)
    r = _run(nc, [arrays], core_ids=[0])
    return r.results[0]["out_0"].reshape(1, S, D)
```
